# Optimizing a Trainium2 kernel written in Bass

```python
import numpy as np
import jax
import jax.numpy as jnp

def _softmax(x, axis=-1):
    return jax.nn.softmax(x, axis=axis)

def _gelu(x):
    return jax.nn.gelu(x, approximate=True)

def _silu(x):
    return jax.nn.silu(x)

def _sigmoid(x):
    return jax.nn.sigmoid(x)

def _layernorm(x, axis=-1, eps=1e-05):
    m = jnp.mean(x, axis=axis, keepdims=True)
    v = jnp.var(x, axis=axis, keepdims=True)
    return (x - m) / jnp.sqrt(v + eps)

def _scatter_add(tgt, idx, src, axis=0):
    return tgt.at[idx].add(src)

def _segment_sum(src, seg, n):
    return jax.ops.segment_sum(src, seg, n)
kernel_name = 'mk_adaln_attn_ffn_d2_seqx_r8_88fc5b'

def setup_inputs(seed: int=0):
    np.random.seed(seed)
    _w = jnp.asarray

    def _rec_inputs():
        import jax
        import jax.numpy as jnp
        _rk = jax.random.key(seed)
        x = -7.109e-05 + 0.9999 * jax.random.normal(jax.random.fold_in(_rk, 1), (32, 32, 128), jnp.float32)
        _lenS = 32 - jax.random.randint(jax.random.fold_in(_rk, 7), (32,), 0, max(1, 32 // 4) + 1, jnp.int32)
        _lenS2 = 32 - jax.random.randint(jax.random.fold_in(_rk, 8), (32,), 0, max(1, 32 // 4) + 1, jnp.int32)
        itok_B_0_8 = jax.random.randint(jax.random.fold_in(_rk, 11), (32,), 0, 9, jnp.int32)
        itok_B_2_61 = jax.random.randint(jax.random.fold_in(_rk, 12), (32,), 2, 62, jnp.int32)
        itok_B_0_2 = jax.random.randint(jax.random.fold_in(_rk, 13), (32,), 0, 3, jnp.int32)
        return (x, itok_B_0_8, itok_B_2_61, itok_B_0_2)
    x, itok_B_0_8, itok_B_2_61, itok_B_0_2 = _rec_inputs()

    def _L0_cond_setup():
        import jax, jax.numpy as jnp
        import numpy as np
        LN_EPS = 1e-05
        key = jax.random.key(seed)
        ks = jax.random.split(key, 8)
        B, S, H, A, L = (32, 256, 128, 32, 10)
        return {'hidden_states': jax.random.normal(ks[0], (B, S, H), dtype=jnp.float32), 'language_ids': jax.random.randint(ks[1], (B,), 0, L, dtype=jnp.int64), 'W1': jax.random.normal(ks[2], (L, H, A), dtype=jnp.float32) * (1.0 / np.sqrt(H)), 'b1': jnp.zeros((L, A), dtype=jnp.float32), 'W2': jax.random.normal(ks[3], (L, A, H), dtype=jnp.float32) * (1.0 / np.sqrt(A)), 'b2': jnp.zeros((L, H), dtype=jnp.float32), 'gamma': jnp.ones((L, H), dtype=jnp.float32), 'beta': jnp.zeros((L, H), dtype=jnp.float32)}
    _L0_cond_all = _L0_cond_setup()
    _L0_cond_in = {k: v for k, v in _L0_cond_all.items() if k in ('W1', 'b1', 'W2', 'b2', 'gamma', 'beta')}
    del _L0_cond_all

    def _L0_attn_setup():
        import jax, jax.numpy as jnp
        import numpy as np
        EMBED = 128
        HEADS = 16
        HEAD_DIM = EMBED // HEADS
        WIN = 32

        def _rope_headaxis(x):
            h, d = (x.shape[2], x.shape[3])
            inv = 1.0 / 10000.0 ** (jnp.arange(0, d, 2, dtype=jnp.float32) / d)
            freqs = jnp.arange(h, dtype=jnp.float32)[:, None] * inv[None, :]
            emb = jnp.concatenate([freqs, freqs], axis=-1)
            cos = jnp.cos(emb)[None, None]
            sin = jnp.sin(emb)[None, None]
            x2 = jnp.stack([-x[..., 1::2], x[..., 0::2]], axis=-1).reshape(x.shape)
            return x * cos + x2 * sin
        key = jax.random.key(seed)
        ks = jax.random.split(key, 10)
        b, s, e = (2, 512, EMBED)
        scale = 1.0 / np.sqrt(e)
        inp = {'x': jax.random.normal(ks[0], (b, s, e), jnp.float32)}
        for i, (wn, bn) in enumerate([('Wq', 'bq'), ('Wk', 'bk'), ('Wv', 'bv'), ('Wo', 'bo')]):
            inp[wn] = jax.random.normal(ks[1 + i], (e, e), jnp.float32) * scale
            inp[bn] = jax.random.normal(ks[5 + i], (e,), jnp.float32) * 0.01
        return inp
    _L0_attn_all = _L0_attn_setup()
    _L0_attn_in = {k: v for k, v in _L0_attn_all.items() if k in ('Wq', 'bq', 'Wk', 'bk', 'Wv', 'bv', 'Wo', 'bo')}
    del _L0_attn_all

    def _L0_cond2_setup():
        import jax, jax.numpy as jnp
        import numpy as np
        NUM_CATEGORIES = 64
        IN_DIM = 128
        OUT_DIM = 128
        BATCH = 32
        SEQ = 64
        key = jax.random.key(seed)
        k1, k2, k3 = jax.random.split(key, 3)
        x = jax.random.normal(k1, (BATCH, SEQ, IN_DIM), dtype=jnp.float32)
        category_ids = jax.random.randint(k2, (BATCH,), 0, NUM_CATEGORIES, dtype=jnp.int32)
        weight = jax.random.normal(k3, (NUM_CATEGORIES, IN_DIM, OUT_DIM), dtype=jnp.float32) * 0.02
        bias = jnp.zeros((NUM_CATEGORIES, OUT_DIM), dtype=jnp.float32)
        return {'x': x, 'category_ids': category_ids, 'weight': weight, 'bias': bias}
    _L0_cond2_all = _L0_cond2_setup()
    _L0_cond2_in = {k: v for k, v in _L0_cond2_all.items() if k in ('weight', 'bias')}
    del _L0_cond2_all

    def _L0_ffn_setup():
        import jax, jax.numpy as jnp
        import numpy as np
        B, S, D, H = (8, 128, 128, 512)
        E, R = (3, 8)
        SCALING = 1.0 / R

        def _mole(x, W, b, A, Bm, Rw):
            gates = jax.nn.softmax(jnp.einsum('bsd,de->bse', x, Rw), axis=-1)
            base = jnp.einsum('bsd,dh->bsh', x, W) + b
            z = jnp.einsum('bsd,edr->ebsr', x, A)
            zg = z * jnp.transpose(gates, (2, 0, 1))[..., None]
            lora = jnp.einsum('ebsr,erh->bsh', zg, Bm)
            return base + SCALING * lora
        key = jax.random.key(seed)
        ks = jax.random.split(key, 12)
        s = lambda k, shape, scale: jax.random.normal(k, shape, dtype=jnp.float32) * scale
        return {'x': s(ks[0], (B, S, D), 1.0), 'W1': s(ks[1], (D, H), D ** (-0.5)), 'b1': jnp.zeros((H,), jnp.float32), 'A1': s(ks[2], (E, D, R), D ** (-0.5)), 'B1': s(ks[3], (E, R, H), 0.0) + s(ks[4], (E, R, H), R ** (-0.5)), 'R1': s(ks[5], (D, E), D ** (-0.5)), 'W2': s(ks[6], (H, D), H ** (-0.5)), 'b2': jnp.zeros((D,), jnp.float32), 'A2': s(ks[7], (E, H, R), H ** (-0.5)), 'B2': s(ks[8], (E, R, D), R ** (-0.5)), 'R2': s(ks[9], (H, E), H ** (-0.5))}
    _L0_ffn_all = _L0_ffn_setup()
    _L0_ffn_in = {k: v for k, v in _L0_ffn_all.items() if k in ('W1', 'b1', 'A1', 'B1', 'R1', 'W2', 'b2', 'A2', 'B2', 'R2')}
    del _L0_ffn_all

    def _L1_cond_setup():
        import jax, jax.numpy as jnp
        import numpy as np
        B, S, D, F, E = (8, 128, 128, 512, 4)

        def _dense(x, wi, wo):
            return jax.nn.relu(x @ wi) @ wo
        key = jax.random.key(seed)
        ks = jax.random.split(key, 10)
        scale = 0.02
        return {'hidden_states': jax.random.normal(ks[0], (B, S, D), jnp.float32), 'type_idx': jax.random.randint(ks[1], (B,), 0, 3, jnp.int32), 'expert_wi': jax.random.normal(ks[2], (E, D, F), jnp.float32) * scale, 'expert_wo': jax.random.normal(ks[3], (E, F, D), jnp.float32) * scale, 'share_wi': jax.random.normal(ks[4], (3, D, F), jnp.float32) * scale, 'share_wo': jax.random.normal(ks[5], (3, F, D), jnp.float32) * scale, 'gate_vecs': jnp.array([[0.22, 0.22, 0.2, 0.2], [0.2, 0.22, 0.22, 0.2], [0.2, 0.2, 0.22, 0.22]], jnp.float32), 'gate_w1': jax.random.normal(ks[6], (4 * D, D), jnp.float32) * scale, 'gate_w2': jax.random.normal(ks[7], (D, 4), jnp.float32) * scale}
    _L1_cond_all = _L1_cond_setup()
    _L1_cond_in = {k: v for k, v in _L1_cond_all.items() if k in ('expert_wi', 'expert_wo', 'share_wi', 'share_wo', 'gate_vecs', 'gate_w1', 'gate_w2')}
    del _L1_cond_all

    def _L1_attn_setup():
        import jax, jax.numpy as jnp
        import numpy as np
        NUM_BLOCKS = 8
        D = 128
        FF = 512
        B, S = (4, 512)
        EPS_ATTN = 1e-06
        EPS_LN = 1e-06

        def _ln(x, scale, bias):
            m = jnp.mean(x, axis=-1, keepdims=True)
            v = jnp.var(x, axis=-1, keepdims=True)
            return (x - m) * jax.lax.rsqrt(v + EPS_LN) * scale + bias

        def _forward(x, Wq, bq, Wk, bk, Wv, bv, Wo, bo, ln1_s, ln1_b, W1, b1, W2, b2, ln2_s, ln2_b):
            gelu = lambda t: jax.nn.gelu(t, approximate=True)
            fmap = lambda t: jax.nn.elu(t) + 1.0
            for i in range(NUM_BLOCKS):
                residual = x
                Q = fmap(x @ Wq[i] + bq[i])
                K = fmap(x @ Wk[i] + bk[i])
                value = x @ Wv[i] + bv[i]
                KV = jnp.einsum('nsh,nsh->nh', K, value)
                Ksum = jnp.sum(K, axis=1)
                Z = 1.0 / (Q * Ksum[:, None, :] + EPS_ATTN)
                V = Q * KV[:, None, :] * Z
                attn_out = gelu(V @ Wo[i] + bo[i])
                x = _ln(attn_out + residual, ln1_s[i], ln1_b[i])
                residual = x
                h = gelu(x @ W1[i] + b1[i])
                ff_out = gelu(h @ W2[i] + b2[i])
                x = _ln(ff_out + residual, ln2_s[i], ln2_b[i])
            return x
        key = jax.random.key(seed)
        ks = jax.random.split(key, 16)
        g = lambda k, shape, fan: jax.random.normal(k, shape, jnp.float32) * (1.0 / np.sqrt(fan))
        inp = {'x': jax.random.normal(ks[0], (B, S, D), jnp.float32), 'Wq': g(ks[1], (NUM_BLOCKS, D, D), D), 'bq': jnp.zeros((NUM_BLOCKS, D), jnp.float32), 'Wk': g(ks[2], (NUM_BLOCKS, D, D), D), 'bk': jnp.zeros((NUM_BLOCKS, D), jnp.float32), 'Wv': g(ks[3], (NUM_BLOCKS, D, D), D), 'bv': jnp.zeros((NUM_BLOCKS, D), jnp.float32), 'Wo': g(ks[4], (NUM_BLOCKS, D, D), D), 'bo': jnp.zeros((NUM_BLOCKS, D), jnp.float32), 'ln1_s': jnp.ones((NUM_BLOCKS, D), jnp.float32), 'ln1_b': jnp.zeros((NUM_BLOCKS, D), jnp.float32), 'W1': g(ks[5], (NUM_BLOCKS, D, FF), D), 'b1': jnp.zeros((NUM_BLOCKS, FF), jnp.float32), 'W2': g(ks[6], (NUM_BLOCKS, FF, D), FF), 'b2': jnp.zeros((NUM_BLOCKS, D), jnp.float32), 'ln2_s': jnp.ones((NUM_BLOCKS, D), jnp.float32), 'ln2_b': jnp.zeros((NUM_BLOCKS, D), jnp.float32)}
        return inp
    _L1_attn_all = _L1_attn_setup()
    _L1_attn_in = {k: v for k, v in _L1_attn_all.items() if k in ('Wq', 'bq', 'Wk', 'bk', 'Wv', 'bv', 'Wo', 'bo', 'ln1_s', 'ln1_b', 'W1', 'b1', 'W2', 'b2', 'ln2_s', 'ln2_b')}
    del _L1_attn_all

    def _L1_cond2_setup():
        import jax, jax.numpy as jnp
        import numpy as np
        B, S, D, F, E = (8, 256, 128, 512, 5)

        def _dense(x, wi_, wo_):
            return jax.nn.relu(x @ wi_) @ wo_
        key = jax.random.key(seed)
        ks = jax.random.split(key, 9)
        sc = 0.02
        return {'hidden_states': jax.random.normal(ks[0], (B, S, D), jnp.float32), 'type_label': jax.random.randint(ks[1], (B,), 0, E, jnp.int32), 'wi': jax.random.normal(ks[2], (E, D, F), jnp.float32) * sc, 'wo': jax.random.normal(ks[3], (E, F, D), jnp.float32) * sc, 'swi': jax.random.normal(ks[4], (2, D, F), jnp.float32) * sc, 'swo': jax.random.normal(ks[5], (2, F, D), jnp.float32) * sc, 'g1': jax.random.normal(ks[6], (3 * D, D), jnp.float32) * sc, 'g2': jax.random.normal(ks[7], (D, 3), jnp.float32) * sc}
    _L1_cond2_all = _L1_cond2_setup()
    _L1_cond2_in = {k: v for k, v in _L1_cond2_all.items() if k in ('wi', 'wo', 'swi', 'swo', 'g1', 'g2')}
    del _L1_cond2_all

    def _L1_ffn_setup():
        import jax, jax.numpy as jnp
        import numpy as np
        LATENT = 128
        LEAF_W = 64
        DEPTH = 4
        N_LEAVES = 2 ** DEPTH
        N_NODES = 2 ** DEPTH - 1
        B, S = (4, 256)

        def _fff_params(key, prefix):
            ks = jax.random.split(key, 4)
            d, h, l, n = (LATENT, LEAF_W, N_LEAVES, N_NODES)
            s_in = 1.0 / np.sqrt(d).astype(np.float32)
            s_h = 1.0 / np.sqrt(h).astype(np.float32)
            return {f'{prefix}_node_w': jax.random.normal(ks[0], (n, d), jnp.float32) * s_in, f'{prefix}_node_b': jax.random.normal(ks[1], (n,), jnp.float32) * s_in, f'{prefix}_w1': jax.random.normal(ks[2], (l, d, h), jnp.float32) * s_in, f'{prefix}_b1': jnp.zeros((l, h), jnp.float32), f'{prefix}_w2': jax.random.normal(ks[3], (l, h, d), jnp.float32) * s_h, f'{prefix}_b2': jnp.zeros((l, d), jnp.float32)}

        def _fff(x, node_w, node_b, w1, b1, w2, b2):
            Bx, Sx, D = x.shape
            xf = x.reshape(-1, D)
            N = xf.shape[0]
            cur = jnp.zeros((N,), jnp.int32)
            for _ in range(DEPTH):
                pw = node_w[cur]
                score = jnp.einsum('nd,nd->n', xf, pw) + node_b[cur]
                cur = 2 * cur + 1 + (score >= 0).astype(jnp.int32)
            leaf = cur - N_NODES
            sel = jax.nn.one_hot(leaf, N_LEAVES, dtype=xf.dtype)
            hidden_all = jax.nn.relu(jnp.einsum('nd,ldh->lnh', xf, w1) + b1[:, None, :])
            hidden = hidden_all * sel.T[:, :, None]
            out = jnp.einsum('lnh,lho->no', hidden, w2) + sel @ b2
            return out.reshape(Bx, Sx, D)
        key = jax.random.key(seed)
        kx, kq, kk, kv = jax.random.split(key, 4)
        inp = {'x': jax.random.normal(kx, (B, S, LATENT), jnp.float32)}
        inp.update(_fff_params(kq, 'q'))
        inp.update(_fff_params(kk, 'k'))
        inp.update(_fff_params(kv, 'v'))
        return inp
    _L1_ffn_all = _L1_ffn_setup()
    _L1_ffn_in = {k: v for k, v in _L1_ffn_all.items() if k in ('q_node_w', 'q_node_b', 'q_w1', 'q_b1', 'q_w2', 'q_b2', 'k_node_w', 'k_node_b', 'k_w1', 'k_b1', 'k_w2', 'k_b2', 'v_node_w', 'v_node_b', 'v_w1', 'v_b1', 'v_w2', 'v_b2')}
    del _L1_ffn_all
    return {'x': x, 'itok_B_0_8': itok_B_0_8, 'itok_B_2_61': itok_B_2_61, 'itok_B_0_2': itok_B_0_2, 'L0_cond_W1': _L0_cond_in['W1'], 'L0_cond_b1': _L0_cond_in['b1'], 'L0_cond_W2': _L0_cond_in['W2'], 'L0_cond_b2': _L0_cond_in['b2'], 'L0_cond_gamma': _L0_cond_in['gamma'], 'L0_cond_beta': _L0_cond_in['beta'], 'L0_attn_Wq': _L0_attn_in['Wq'], 'L0_attn_bq': _L0_attn_in['bq'], 'L0_attn_Wk': _L0_attn_in['Wk'], 'L0_attn_bk': _L0_attn_in['bk'], 'L0_attn_Wv': _L0_attn_in['Wv'], 'L0_attn_bv': _L0_attn_in['bv'], 'L0_attn_Wo': _L0_attn_in['Wo'], 'L0_attn_bo': _L0_attn_in['bo'], 'L0_cond2_weight': _L0_cond2_in['weight'], 'L0_cond2_bias': _L0_cond2_in['bias'], 'L0_ffn_W1': _L0_ffn_in['W1'], 'L0_ffn_b1': _L0_ffn_in['b1'], 'L0_ffn_A1': _L0_ffn_in['A1'], 'L0_ffn_B1': _L0_ffn_in['B1'], 'L0_ffn_R1': _L0_ffn_in['R1'], 'L0_ffn_W2': _L0_ffn_in['W2'], 'L0_ffn_b2': _L0_ffn_in['b2'], 'L0_ffn_A2': _L0_ffn_in['A2'], 'L0_ffn_B2': _L0_ffn_in['B2'], 'L0_ffn_R2': _L0_ffn_in['R2'], 'L1_cond_expert_wi': _L1_cond_in['expert_wi'], 'L1_cond_expert_wo': _L1_cond_in['expert_wo'], 'L1_cond_share_wi': _L1_cond_in['share_wi'], 'L1_cond_share_wo': _L1_cond_in['share_wo'], 'L1_cond_gate_vecs': _L1_cond_in['gate_vecs'], 'L1_cond_gate_w1': _L1_cond_in['gate_w1'], 'L1_cond_gate_w2': _L1_cond_in['gate_w2'], 'L1_attn_Wq': _L1_attn_in['Wq'], 'L1_attn_bq': _L1_attn_in['bq'], 'L1_attn_Wk': _L1_attn_in['Wk'], 'L1_attn_bk': _L1_attn_in['bk'], 'L1_attn_Wv': _L1_attn_in['Wv'], 'L1_attn_bv': _L1_attn_in['bv'], 'L1_attn_Wo': _L1_attn_in['Wo'], 'L1_attn_bo': _L1_attn_in['bo'], 'L1_attn_ln1_s': _L1_attn_in['ln1_s'], 'L1_attn_ln1_b': _L1_attn_in['ln1_b'], 'L1_attn_W1': _L1_attn_in['W1'], 'L1_attn_b1': _L1_attn_in['b1'], 'L1_attn_W2': _L1_attn_in['W2'], 'L1_attn_b2': _L1_attn_in['b2'], 'L1_attn_ln2_s': _L1_attn_in['ln2_s'], 'L1_attn_ln2_b': _L1_attn_in['ln2_b'], 'L1_cond2_wi': _L1_cond2_in['wi'], 'L1_cond2_wo': _L1_cond2_in['wo'], 'L1_cond2_swi': _L1_cond2_in['swi'], 'L1_cond2_swo': _L1_cond2_in['swo'], 'L1_cond2_g1': _L1_cond2_in['g1'], 'L1_cond2_g2': _L1_cond2_in['g2'], 'L1_ffn_q_node_w': _L1_ffn_in['q_node_w'], 'L1_ffn_q_node_b': _L1_ffn_in['q_node_b'], 'L1_ffn_q_w1': _L1_ffn_in['q_w1'], 'L1_ffn_q_b1': _L1_ffn_in['q_b1'], 'L1_ffn_q_w2': _L1_ffn_in['q_w2'], 'L1_ffn_q_b2': _L1_ffn_in['q_b2'], 'L1_ffn_k_node_w': _L1_ffn_in['k_node_w'], 'L1_ffn_k_node_b': _L1_ffn_in['k_node_b'], 'L1_ffn_k_w1': _L1_ffn_in['k_w1'], 'L1_ffn_k_b1': _L1_ffn_in['k_b1'], 'L1_ffn_k_w2': _L1_ffn_in['k_w2'], 'L1_ffn_k_b2': _L1_ffn_in['k_b2'], 'L1_ffn_v_node_w': _L1_ffn_in['v_node_w'], 'L1_ffn_v_node_b': _L1_ffn_in['v_node_b'], 'L1_ffn_v_w1': _L1_ffn_in['v_w1'], 'L1_ffn_v_b1': _L1_ffn_in['v_b1'], 'L1_ffn_v_w2': _L1_ffn_in['v_w2'], 'L1_ffn_v_b2': _L1_ffn_in['v_b2']}

def reference(x, itok_B_0_8, itok_B_2_61, itok_B_0_2, L0_cond_W1, L0_cond_b1, L0_cond_W2, L0_cond_b2, L0_cond_gamma, L0_cond_beta, L0_attn_Wq, L0_attn_bq, L0_attn_Wk, L0_attn_bk, L0_attn_Wv, L0_attn_bv, L0_attn_Wo, L0_attn_bo, L0_cond2_weight, L0_cond2_bias, L0_ffn_W1, L0_ffn_b1, L0_ffn_A1, L0_ffn_B1, L0_ffn_R1, L0_ffn_W2, L0_ffn_b2, L0_ffn_A2, L0_ffn_B2, L0_ffn_R2, L1_cond_expert_wi, L1_cond_expert_wo, L1_cond_share_wi, L1_cond_share_wo, L1_cond_gate_vecs, L1_cond_gate_w1, L1_cond_gate_w2, L1_attn_Wq, L1_attn_bq, L1_attn_Wk, L1_attn_bk, L1_attn_Wv, L1_attn_bv, L1_attn_Wo, L1_attn_bo, L1_attn_ln1_s, L1_attn_ln1_b, L1_attn_W1, L1_attn_b1, L1_attn_W2, L1_attn_b2, L1_attn_ln2_s, L1_attn_ln2_b, L1_cond2_wi, L1_cond2_wo, L1_cond2_swi, L1_cond2_swo, L1_cond2_g1, L1_cond2_g2, L1_ffn_q_node_w, L1_ffn_q_node_b, L1_ffn_q_w1, L1_ffn_q_b1, L1_ffn_q_w2, L1_ffn_q_b2, L1_ffn_k_node_w, L1_ffn_k_node_b, L1_ffn_k_w1, L1_ffn_k_b1, L1_ffn_k_w2, L1_ffn_k_b2, L1_ffn_v_node_w, L1_ffn_v_node_b, L1_ffn_v_w1, L1_ffn_v_b1, L1_ffn_v_w2, L1_ffn_v_b2):
    import jax
    import jax.numpy as jnp

    def _L0_cond_ref(hidden_states, language_ids, W1, b1, W2, b2, gamma, beta):
        import jax, jax.numpy as jnp
        import numpy as np
        LN_EPS = 1e-05
        w1 = W1[language_ids]
        w2 = W2[language_ids]
        h = jnp.einsum('bsh,bha->bsa', hidden_states, w1) + b1[language_ids][:, None, :]
        h = jax.nn.relu(h)
        adapted = jnp.einsum('bsa,bah->bsh', h, w2) + b2[language_ids][:, None, :]
        x = hidden_states + adapted
        mean = jnp.mean(x, axis=-1, keepdims=True)
        var = jnp.mean(jnp.square(x - mean), axis=-1, keepdims=True)
        normed = (x - mean) * jax.lax.rsqrt(var + LN_EPS)
        return normed * gamma[language_ids][:, None, :] + beta[language_ids][:, None, :]

    def _L0_attn_ref(x, Wq, bq, Wk, bk, Wv, bv, Wo, bo):
        import jax, jax.numpy as jnp
        import numpy as np
        EMBED = 128
        HEADS = 16
        HEAD_DIM = EMBED // HEADS
        WIN = 32

        def _rope_headaxis(x):
            h, d = (x.shape[2], x.shape[3])
            inv = 1.0 / 10000.0 ** (jnp.arange(0, d, 2, dtype=jnp.float32) / d)
            freqs = jnp.arange(h, dtype=jnp.float32)[:, None] * inv[None, :]
            emb = jnp.concatenate([freqs, freqs], axis=-1)
            cos = jnp.cos(emb)[None, None]
            sin = jnp.sin(emb)[None, None]
            x2 = jnp.stack([-x[..., 1::2], x[..., 0::2]], axis=-1).reshape(x.shape)
            return x * cos + x2 * sin
        b, s, e = x.shape
        h, d, w = (HEADS, HEAD_DIM, WIN)
        q = (x @ Wq.T + bq).reshape(b, s, h, d)
        k = (x @ Wk.T + bk).reshape(b, s, h, d)
        v = (x @ Wv.T + bv).reshape(b, s, h, d)
        q = _rope_headaxis(q) / jnp.sqrt(jnp.float32(d))
        k = _rope_headaxis(k)
        nc = s // w
        qc = q.reshape(b, nc, w, h, d)
        pad = [(0, 0), (w, w), (0, 0), (0, 0)]
        kp = jnp.pad(k, pad)
        vp = jnp.pad(v, pad)
        idx = jnp.arange(nc)[:, None] * w + jnp.arange(3 * w)[None, :]
        k3 = kp[:, idx]
        v3 = vp[:, idx]
        scores = jnp.einsum('bcxhd,bcyhd->bhcxy', qc, k3)
        c = jnp.arange(nc)[:, None, None]
        xq = jnp.arange(w)[None, :, None]
        y = jnp.arange(3 * w)[None, None, :]
        kpos = c * w + y - w
        valid = (y >= xq) & (y <= xq + 2 * w) & (kpos >= 0) & (kpos < s)
        scores = jnp.where(valid[None, None], scores, -jnp.inf)
        probs = jax.nn.softmax(scores, axis=-1)
        ctx = jnp.einsum('bhcxy,bcyhd->bcxhd', probs, v3).reshape(b, s, e)
        return ctx @ Wo.T + bo

    def _L0_cond2_ref(x, category_ids, weight, bias):
        import jax, jax.numpy as jnp
        import numpy as np
        NUM_CATEGORIES = 64
        IN_DIM = 128
        OUT_DIM = 128
        BATCH = 32
        SEQ = 64
        W = weight[category_ids]
        b = bias[category_ids]
        return jnp.einsum('bli,bio->blo', x, W) + b[:, None, :]

    def _L0_ffn_ref(x, W1, b1, A1, B1, R1, W2, b2, A2, B2, R2):
        import jax, jax.numpy as jnp
        import numpy as np
        B, S, D, H = (8, 128, 128, 512)
        E, R = (3, 8)
        SCALING = 1.0 / R

        def _mole(x, W, b, A, Bm, Rw):
            gates = jax.nn.softmax(jnp.einsum('bsd,de->bse', x, Rw), axis=-1)
            base = jnp.einsum('bsd,dh->bsh', x, W) + b
            z = jnp.einsum('bsd,edr->ebsr', x, A)
            zg = z * jnp.transpose(gates, (2, 0, 1))[..., None]
            lora = jnp.einsum('ebsr,erh->bsh', zg, Bm)
            return base + SCALING * lora
        h = _mole(x, W1, b1, A1, B1, R1)
        h = jax.nn.relu(h)
        return _mole(h, W2, b2, A2, B2, R2)

    def _L1_cond_ref(hidden_states, type_idx, expert_wi, expert_wo, share_wi, share_wo, gate_vecs, gate_w1, gate_w2):
        import jax, jax.numpy as jnp
        import numpy as np
        B, S, D, F, E = (8, 128, 128, 512, 4)

        def _dense(x, wi, wo):
            return jax.nn.relu(x @ wi) @ wo
        s0 = _dense(hidden_states, share_wi[0], share_wo[0])
        s1 = _dense(hidden_states, share_wi[1], share_wo[1])
        s2 = _dense(hidden_states, share_wi[2], share_wo[2])
        idx_a = type_idx
        idx_b = type_idx + 1
        out_a = jnp.einsum('bsf,bfd->bsd', jax.nn.relu(jnp.einsum('bsd,bdf->bsf', hidden_states, expert_wi[idx_a])), expert_wo[idx_a])
        out_b = jnp.einsum('bsf,bfd->bsd', jax.nn.relu(jnp.einsum('bsd,bdf->bsf', hidden_states, expert_wi[idx_b])), expert_wo[idx_b])
        p = jax.nn.softmax(gate_vecs / 0.1, axis=-1)
        wa = p[type_idx, idx_a][:, None, None]
        wb = p[type_idx, idx_b][:, None, None]
        expert_out = out_a * wa + out_b * wb
        gi = jnp.concatenate([expert_out[:, 0], s0[:, 0], s1[:, 0], s2[:, 0]], axis=-1)
        g = jax.nn.softmax(jax.nn.relu(gi @ gate_w1) @ gate_w2, axis=-1)
        out = expert_out * g[:, 0, None, None] + s0 * g[:, 1, None, None] + s1 * g[:, 2, None, None] + s2 * g[:, 3, None, None]
        return out

    def _L1_attn_ref(x, Wq, bq, Wk, bk, Wv, bv, Wo, bo, ln1_s, ln1_b, W1, b1, W2, b2, ln2_s, ln2_b):
        import jax, jax.numpy as jnp
        import numpy as np
        NUM_BLOCKS = 8
        D = 128
        FF = 512
        B, S = (4, 512)
        EPS_ATTN = 1e-06
        EPS_LN = 1e-06

        def _ln(x, scale, bias):
            m = jnp.mean(x, axis=-1, keepdims=True)
            v = jnp.var(x, axis=-1, keepdims=True)
            return (x - m) * jax.lax.rsqrt(v + EPS_LN) * scale + bias

        def _forward(x, Wq, bq, Wk, bk, Wv, bv, Wo, bo, ln1_s, ln1_b, W1, b1, W2, b2, ln2_s, ln2_b):
            gelu = lambda t: jax.nn.gelu(t, approximate=True)
            fmap = lambda t: jax.nn.elu(t) + 1.0
            for i in range(NUM_BLOCKS):
                residual = x
                Q = fmap(x @ Wq[i] + bq[i])
                K = fmap(x @ Wk[i] + bk[i])
                value = x @ Wv[i] + bv[i]
                KV = jnp.einsum('nsh,nsh->nh', K, value)
                Ksum = jnp.sum(K, axis=1)
                Z = 1.0 / (Q * Ksum[:, None, :] + EPS_ATTN)
                V = Q * KV[:, None, :] * Z
                attn_out = gelu(V @ Wo[i] + bo[i])
                x = _ln(attn_out + residual, ln1_s[i], ln1_b[i])
                residual = x
                h = gelu(x @ W1[i] + b1[i])
                ff_out = gelu(h @ W2[i] + b2[i])
                x = _ln(ff_out + residual, ln2_s[i], ln2_b[i])
            return x
        return _forward(x, Wq, bq, Wk, bk, Wv, bv, Wo, bo, ln1_s, ln1_b, W1, b1, W2, b2, ln2_s, ln2_b)

    def _L1_cond2_ref(hidden_states, type_label, wi, wo, swi, swo, g1, g2):
        import jax, jax.numpy as jnp
        import numpy as np
        B, S, D, F, E = (8, 256, 128, 512, 5)

        def _dense(x, wi_, wo_):
            return jax.nn.relu(x @ wi_) @ wo_
        x = hidden_states
        s0 = _dense(x, swi[0], swo[0])
        s1 = _dense(x, swi[1], swo[1])
        wi_sel = wi[type_label]
        wo_sel = wo[type_label]
        h = jax.nn.relu(jnp.einsum('bsd,bdf->bsf', x, wi_sel))
        eo = jnp.einsum('bsf,bfd->bsd', h, wo_sel)
        gate_in = jnp.concatenate([eo[:, 0], s0[:, 0], s1[:, 0]], axis=-1)
        w = jax.nn.softmax(jax.nn.relu(gate_in @ g1) @ g2, axis=-1)
        w = w[:, :, None, None]
        return eo * w[:, 0] + s0 * w[:, 1] + s1 * w[:, 2]

    def _L1_ffn_ref(x, q_node_w, q_node_b, q_w1, q_b1, q_w2, q_b2, k_node_w, k_node_b, k_w1, k_b1, k_w2, k_b2, v_node_w, v_node_b, v_w1, v_b1, v_w2, v_b2):
        import jax, jax.numpy as jnp
        import numpy as np
        LATENT = 128
        LEAF_W = 64
        DEPTH = 4
        N_LEAVES = 2 ** DEPTH
        N_NODES = 2 ** DEPTH - 1
        B, S = (4, 256)

        def _fff_params(key, prefix):
            ks = jax.random.split(key, 4)
            d, h, l, n = (LATENT, LEAF_W, N_LEAVES, N_NODES)
            s_in = 1.0 / np.sqrt(d).astype(np.float32)
            s_h = 1.0 / np.sqrt(h).astype(np.float32)
            return {f'{prefix}_node_w': jax.random.normal(ks[0], (n, d), jnp.float32) * s_in, f'{prefix}_node_b': jax.random.normal(ks[1], (n,), jnp.float32) * s_in, f'{prefix}_w1': jax.random.normal(ks[2], (l, d, h), jnp.float32) * s_in, f'{prefix}_b1': jnp.zeros((l, h), jnp.float32), f'{prefix}_w2': jax.random.normal(ks[3], (l, h, d), jnp.float32) * s_h, f'{prefix}_b2': jnp.zeros((l, d), jnp.float32)}

        def _fff(x, node_w, node_b, w1, b1, w2, b2):
            Bx, Sx, D = x.shape
            xf = x.reshape(-1, D)
            N = xf.shape[0]
            cur = jnp.zeros((N,), jnp.int32)
            for _ in range(DEPTH):
                pw = node_w[cur]
                score = jnp.einsum('nd,nd->n', xf, pw) + node_b[cur]
                cur = 2 * cur + 1 + (score >= 0).astype(jnp.int32)
            leaf = cur - N_NODES
            sel = jax.nn.one_hot(leaf, N_LEAVES, dtype=xf.dtype)
            hidden_all = jax.nn.relu(jnp.einsum('nd,ldh->lnh', xf, w1) + b1[:, None, :])
            hidden = hidden_all * sel.T[:, :, None]
            out = jnp.einsum('lnh,lho->no', hidden, w2) + sel @ b2
            return out.reshape(Bx, Sx, D)
        q = _fff(x, q_node_w, q_node_b, q_w1, q_b1, q_w2, q_b2)
        k = _fff(x, k_node_w, k_node_b, k_w1, k_b1, k_w2, k_b2)
        v = _fff(x, v_node_w, v_node_b, v_w1, v_b1, v_w2, v_b2)
        scale = 1.0 / np.sqrt(LATENT).astype(np.float32)
        attn = jax.nn.softmax(jnp.einsum('bqd,bkd->bqk', q, k) * scale, axis=-1)
        return jnp.einsum('bqk,bkd->bqd', attn, v)
    x = x + _L0_attn_ref(_L0_cond_ref(x, itok_B_0_8, L0_cond_W1, L0_cond_b1, L0_cond_W2, L0_cond_b2, L0_cond_gamma, L0_cond_beta), L0_attn_Wq, L0_attn_bq, L0_attn_Wk, L0_attn_bk, L0_attn_Wv, L0_attn_bv, L0_attn_Wo, L0_attn_bo)
    x = x + _L0_ffn_ref(_L0_cond2_ref(x, itok_B_2_61, L0_cond2_weight, L0_cond2_bias), L0_ffn_W1, L0_ffn_b1, L0_ffn_A1, L0_ffn_B1, L0_ffn_R1, L0_ffn_W2, L0_ffn_b2, L0_ffn_A2, L0_ffn_B2, L0_ffn_R2)
    x = x + _L1_attn_ref(_L1_cond_ref(x, itok_B_0_2, L1_cond_expert_wi, L1_cond_expert_wo, L1_cond_share_wi, L1_cond_share_wo, L1_cond_gate_vecs, L1_cond_gate_w1, L1_cond_gate_w2), L1_attn_Wq, L1_attn_bq, L1_attn_Wk, L1_attn_bk, L1_attn_Wv, L1_attn_bv, L1_attn_Wo, L1_attn_bo, L1_attn_ln1_s, L1_attn_ln1_b, L1_attn_W1, L1_attn_b1, L1_attn_W2, L1_attn_b2, L1_attn_ln2_s, L1_attn_ln2_b)
    x = x + _L1_ffn_ref(_L1_cond2_ref(x, itok_B_0_2, L1_cond2_wi, L1_cond2_wo, L1_cond2_swi, L1_cond2_swo, L1_cond2_g1, L1_cond2_g2), L1_ffn_q_node_w, L1_ffn_q_node_b, L1_ffn_q_w1, L1_ffn_q_b1, L1_ffn_q_w2, L1_ffn_q_b2, L1_ffn_k_node_w, L1_ffn_k_node_b, L1_ffn_k_w1, L1_ffn_k_b1, L1_ffn_k_w2, L1_ffn_k_b2, L1_ffn_v_node_w, L1_ffn_v_node_b, L1_ffn_v_w1, L1_ffn_v_b1, L1_ffn_v_w2, L1_ffn_v_b2)
    return x

_drawn_inputs = setup_inputs


def setup_inputs(seed=0):
    import zlib

    import numpy as np

    out = dict(_drawn_inputs(seed))
    spreads = {'L0_cond_b1': (0.0, 0.1),
     'L0_cond_b2': (0.0, 0.1),
     'L0_cond_gamma': (1.0, 0.2),
     'L0_cond_beta': (0.0, 0.1),
     'L0_cond2_bias': (0.0, 0.1),
     'L0_ffn_b1': (0.0, 0.1),
     'L0_ffn_b2': (0.0, 0.1),
     'L1_attn_bq': (0.0, 0.8),
     'L1_attn_bk': (0.0, 0.8),
     'L1_attn_bv': (0.0, 0.1),
     'L1_attn_bo': (0.0, 0.1),
     'L1_attn_ln1_s': (1.0, 0.2),
     'L1_attn_ln1_b': (0.0, 0.1),
     'L1_attn_b1': (0.0, 0.1),
     'L1_attn_b2': (0.0, 0.1),
     'L1_attn_ln2_s': (1.0, 0.2),
     'L1_attn_ln2_b': (0.0, 0.1),
     'L1_ffn_q_b1': (0.0, 0.8),
     'L1_ffn_q_b2': (0.0, 0.8),
     'L1_ffn_k_b1': (0.0, 0.8),
     'L1_ffn_k_b2': (0.0, 0.8),
     'L1_ffn_v_b1': (0.0, 0.358),
     'L1_ffn_v_b2': (0.0, 0.1)}
    factors = {'L0_attn_bq': 8.0,
     'L0_attn_bk': 64.0,
     'L0_attn_bv': 7.522,
     'L0_attn_bo': 7.498,
     'L0_ffn_A1': 5.638,
     'L0_ffn_B1': 5.651,
     'L0_ffn_R1': 8.0,
     'L0_ffn_A2': 4.95,
     'L0_ffn_B2': 5.479,
     'L0_ffn_R2': 8.0,
     'L1_cond_gate_vecs': 8.0,
     'L1_cond_gate_w1': 8.0,
     'L1_cond_gate_w2': 8.0,
     'L1_attn_Wq': 8.0,
     'L1_cond2_swi': 3.684,
     'L1_cond2_g1': 8.0,
     'L1_cond2_g2': 8.0,
     'L1_ffn_q_node_w': 8.0,
     'L1_ffn_q_node_b': 8.0,
     'L1_ffn_q_w1': 8.0,
     'L1_ffn_q_w2': 8.0,
     'L1_ffn_k_node_w': 8.0,
     'L1_ffn_k_node_b': 8.0,
     'L1_ffn_k_w1': 8.0,
     'L1_ffn_k_w2': 8.0,
     'L1_ffn_v_w1': 3.47}
    for name, (base, spread) in spreads.items():
        noise = np.random.default_rng([zlib.crc32(name.encode()), seed]).standard_normal(out[name].shape)
        drawn = base * np.exp(spread * noise) if base else spread * noise
        out[name] = jnp.asarray(drawn.astype(out[name].dtype))
    for name, factor in factors.items():
        out[name] = (out[name] * factor).astype(out[name].dtype)
    return out
```

```python
from contextlib import ExitStack

import numpy as np

import concourse.bass as bass
from concourse import mybir

F32 = mybir.dt.float32
BF16 = mybir.dt.bfloat16
I32 = mybir.dt.int32
ALU = mybir.AluOpType
ACT = mybir.ActivationFunctionType
AX_X = mybir.AxisListType.X

P = 128
B, S, D = 32, 32, 128
HALVES = (0, 1)
HB = B // 2
HT = HB * S
TILES = HT // P
BANKS = 4

LANGS, ADIM = 10, 32
LCH = -(-LANGS * ADIM // P)
HEADS, HD = 16, 8
QUAD = 32
HPQ = QUAD // HD
HG = HEADS // HPQ
GB = 4
NG = HB // GB
CATS = 64
FF = 512
FC = FF // P
ME, MR = 3, 8
MER = ME * MR
L1E, L1S = 4, 3
TYPES = 3
L2S = 2
LAYERS = 8
TREES, LEAVES, LEAFW = 3, 16, 64
NODES = LEAVES - 1
LFC = LEAVES * LEAFW // P

EPS_COND = 1e-5
EPS_ATTN = 1e-6
EPS_LN = 1e-6

LV = 7 + FC
V_BQ, V_BK, V_BV, V_S1, V_B1, V_S2, V_B2, V_FF = range(8)
R_LEAF = LV * LAYERS
R_ADAPT = R_LEAF + LFC * TREES
R_L0Q, R_L0K, R_L0V = R_ADAPT + LCH, R_ADAPT + LCH + 1, R_ADAPT + LCH + 2
R_END = R_L0V + 1

K_IOTA, K_LANG, K_HEAD, K_LEAF, K_SLOT, K_BAND = 0, 1, 4, 8, 16, 18
K_IDENT, K_ROPEQ, K_ROPEK, K_VMASK = 32, 32 + P, 32 + 2 * P, 32 + 3 * P
K_END = 32 + 4 * P


def shape_constants():
    k = np.zeros((P, K_END), np.float32)
    p = np.arange(P)
    k[:, K_IOTA] = p
    for c in range(LCH):
        k[:, K_LANG + c] = c * (P // ADIM) + p // ADIM
    for j in range(HPQ):
        k[:, K_HEAD + j] = (p % QUAD) // HD == j
    for c in range(LFC):
        k[:, K_LEAF + c] = c * (P // LEAFW) + p // LEAFW
    k[:, K_SLOT] = p % QUAD
    for t in range(TYPES):
        k[t, K_BAND + t:K_BAND + t + 2] = 1.0
    k[:, K_IDENT:K_IDENT + P] = np.eye(P)
    inv = 1.0 / 10000.0 ** (np.arange(0, HD, 2, dtype=np.float64) / HD)
    rot = np.zeros((P, P))
    for h in range(HEADS):
        ang = np.concatenate([h * inv, h * inv])
        for d in range(HD):
            row = h * HD + d
            rot[row, row] = np.cos(ang[d])
            rot[row, row + 1 if d % 2 == 0 else row - 1] = -np.sin(ang[d]) if d % 2 == 0 else np.sin(ang[d])
    k[:, K_ROPEQ:K_ROPEQ + P] = rot.T / np.sqrt(HD)
    k[:, K_ROPEK:K_ROPEK + P] = rot.T
    for f in range(P):
        k[:, K_VMASK + f] = p // QUAD == (f % QUAD) // HD
    return k


class Chain:

    def __init__(self, eng, sem):
        self.eng, self.sem, self.n, self.base = eng, sem, 0, None

    def step(self, ins):
        ins.then_inc(self.sem, 1)
        self.n += 1

    def sync(self):
        self.eng.wait_ge(self.sem, self.n if self.base is None else self.base + self.n)

    def link(self, ins):
        self.step(ins)
        self.sync()


def expert_items(shares, experts):
    items = [(j, None, c, c == 0, c == FC - 1) for j in range(shares) for c in range(FC)]
    items += [(shares, e, c, e == 0 and c == 0, e == experts - 1 and c == FC - 1)
              for e in range(experts) for c in range(FC)]
    return items


def counts_of(items):
    seen = [0, 0]
    out = []
    for it in items:
        kind = int(it[1] is not None)
        out.append((kind, seen[kind]))
        seen[kind] += 1
    return out


def network(nc, I, konst, out):
    ctx = ExitStack()
    with ctx:
        def sb(name, shape, dt=F32):
            return ctx.enter_context(nc.sbuf_tensor(name, shape, dt))

        kc = sb("kc", [P, K_END])
        ident, rope_q, rope_k = (kc[:, k:k + P] for k in (K_IDENT, K_ROPEQ, K_ROPEK))
        vmask = kc[:, K_VMASK:K_VMASK + P]
        rows = sb("rows", [P, P])
        cols = sb("cols", [P, P])
        ids = sb("ids", [P, 3, B], I32)
        idf = sb("idf", [P, 3, B])
        ones = sb("ones", [1, P])
        minus_half = sb("minus_half", [P, TILES])
        eps_cond = sb("eps_cond", [P, TILES])
        eps_ln = sb("eps_ln", [P, TILES])
        lang_hot = sb("lang_hot", [P, B])
        cat_hot = sb("cat_hot", [P, B])
        type_hot = sb("type_hot", [P, B])
        lang_mask = sb("lang_mask", [P, LCH, B])
        type_mask = sb("type_mask", [P, TYPES, B])
        batch_cols = sb("batch_cols", [P, 3, B])
        gamma_b, beta_b, cbias_b = (batch_cols[:, n, :] for n in range(3))
        w1a = sb("w1a", [P, LANGS * ADIM])
        w2a = sb("w2a", [P, LCH, D])
        lang_rows = sb("lang_rows", [LANGS, 3, D])
        w_nat = sb("w_nat", [P, 4, D])
        w_att = sb("w_att", [P, 4, D])
        rope_bias = sb("rope_bias", [P, 2])
        key_bias = sb("key_bias", [P, HG])
        token_bias = sb("token_bias", [1, D])
        cat_bias = sb("cat_bias", [CATS, D])
        big = sb("big", [P, B * D])
        w_cat = big[:, :].rearrange("p (b n) -> p b n", b=B)
        ar1 = sb("ar1", [P, MER + ME])
        ar2 = sb("ar2", [P, FC, MER + ME])
        b1aug = sb("b1aug", [MER + 1, FF])
        b2aug = sb("b2aug", [MER + 1, D])
        w1f = sb("w1f", [P, FF])
        w2f = sb("w2f", [P, FC, D])
        NE1 = L1S + L1E
        arena = sb("arena", [P, NE1, 2, FF])
        gate1 = sb("gate1", [P, L1S + 1, D])
        gate2 = sb("gate2", [P, L1S + 1])
        gate1b = sb("gate1b", [P, L2S + 1, D])
        gate2b = sb("gate2b", [P, L2S + 1])
        gvec = sb("gvec", [TYPES, 3, L1E])
        gred = sb("gred", [TYPES, 4])
        gwide = sb("gwide", [TYPES, L1E, P])
        type_coef = sb("type_coef", [P, L1E, B])
        wl = [sb(f"wl{s}", [P, 4 * D + 2 * FF]) for s in range(2)]
        vl = [sb(f"vl{s}", [P, LV]) for s in range(2)]
        bl = [sb(f"bl{s}", [1, 2, D]) for s in range(2)]
        tree_v = sb("tree_v", [P, 2 * LFC * P])
        node_rows = sb("node_rows", [TREES * LEAVES, D])
        node_t = sb("node_t", [P, TREES * LEAVES])
        node_bias = sb("node_bias", [1, TREES * LEAVES])
        leaf_b2 = sb("leaf_b2", [TREES * QUAD, D])
        leaf_val = sb("leaf_val", [P, P], BF16)

        xt = [sb(f"xt{n}", [P, 2, TILES, D]) for n in range(2)]
        xf = sb("xf", [P, 2, HT])
        cf = sb("cf", [P, 2, HT])
        yt = sb("yt", [P, 2, TILES, D])
        xn = sb("xn", [P, 2, TILES, D])
        stat = sb("stat", [P, 2, TILES, 6])
        after_stats = sb("after_stats", [P, 1])
        mv = sb("mv", [P, 2, TILES, 2])
        rv = sb("rv", [P, 2, TILES])
        rstd = sb("rstd", [P, 2, TILES])
        small = sb("small", [P, 2, 64])
        small2 = sb("small2", [P, 2, 64])
        logit = sb("logit", [P, 2, TILES, ME])
        zg = sb("zg", [P, 2, TILES, QUAD])
        zgt = sb("zgt", [QUAD, 2, HT])
        gsm = sb("gsm", [HB, 2, 16])
        gwb = sb("gwb", [HB, 2, 4, P])
        gcol = sb("gcol", [P, 2, 4, HB])
        grel = sb("grel", [P, 2, HB])
        dec = sb("dec", [P, 2, TILES * TREES, LEAVES])
        reach = sb("reach", [P, 2, TILES * TREES, 16])
        sel = sb("sel", [P, 2, TILES, TREES, QUAD])
        selt = sb("selt", [TREES * QUAD, 2, HT])
        selb = sb("selb", [TREES * QUAD, 2, HT], BF16)
        Z = [sb(f"z{h}", [P, 16, HT]) for h in HALVES]
        lang_tok = Z[0][0:16, 14:16, :].rearrange("p a (b s) -> p (a b) s", s=S)

        ps = [ctx.enter_context(nc.psum_tensor(f"ps{h}", [P, BANKS, HT], F32)) for h in HALVES]

        class Sems(dict):
            def __missing__(self, name):
                self[name] = ctx.enter_context(nc.semaphore(name))
                return self[name]

        S_ = Sems()
        names = """ld_const ld_ids ld_x ld_rows ld_rowsb ld_a ld_b ld_cat ld_c ld_d ld_e ld_f0 ld_f1 ld_g ld_h st_out
            dve pool act_own k_mem p_cols p_colsc p_watt p_wattc p_rope p_ropec p_keyb p_node p_nodec p_hot p_bat p_batc
            p_gw p_coef p_coefc
            x_tr x_f a_hid a_relu a_mask a_out a_tr a_cond var rstd xn
            b_qk b_k b_rep b_qe b_vr b_vx b_sc b_sub b_exp b_pt b_ctx b_ctxc b_out b_res b_tr b_xf
            c_mm c_out d_r1 d_z d_e d_zt d_ztc d_hid d_relu d_r2 d_out d_res d_tr d_xf
            e_hid e_ra e_rd e_acc e_accc e_g1 e_g1c e_g2 e_ge e_gw e_gb e_gbc e_out e_tr0
            f_qkv f_exp f_rel f_k f_den f_lnexp f_v f_o f_og f_tr f_x f_ft f_w1 f_h f_w2 f_w2g
            g_res g_tr g_xf
            g_hid g_ra g_rd g_acc g_accc g_g1 g_g1c g_g2 g_ge g_gw g_gb g_gbc g_out
            h_sc h_sel h_st h_stc h_stb h_lb h_lbc h_hid h_relu h_mask h_acc h_accc h_s h_sub h_exp h_pt h_o h_fin"""
        for n in names.split():
            S_[n]
        block = ctx.enter_context(nc.Block())

        def w_tree(t):
            w = tree_v[:, :] if t == 2 else big[:, t * 2 * LFC * P:(t + 1) * 2 * LFC * P]
            return w.rearrange("p (a c n) -> p a c n", a=2, c=LFC)

        def tok(h, i):
            return slice(i * P, (i + 1) * P)

        def z(h, n, k=1):
            return Z[h][:, n, :] if k == 1 else Z[h][:, n:n + k, :]

        def by_batch(ap):
            return ap.rearrange("p (b s) -> p b s", s=S)

        def spread(ap, n):
            return ap.unsqueeze(len(ap.shape)).to_broadcast([*ap.shape, n])

        def keys_by_quadrant(h):
            return z(h, 4, 4).rearrange("p g (b q s) -> p (g b) q s", b=GB, q=HG)

        def tr_count(l, h, n):
            if n == 0 and h == 0:
                return l * 4 + 1
            return l * 4 + (2 if h == 0 else 3 + n)

        def ft_count(l, h, n):
            if n == 0:
                return 1 if h == 0 and isinstance(l, int) and l == 0 else l * 4 + 2 * h
            return l * 4 + (3 + 2 * h)

        E_ITEMS, G_ITEMS = expert_items(L1S, L1E), expert_items(L2S, TYPES)

        @block.sync
        def _(sp):
            def load(dst, src, sem):
                sp.dma_start(dst, src).then_inc(S_[sem], 16)

            def row(name):
                return I[name].rearrange("(a n) -> a n", a=1)

            load(kc[:, :], konst, "ld_const")
            load(xt[0][:, :, :, :].rearrange("p h i d -> p (h i) d"),
                 I["x"].rearrange("b s d -> (b s) d").rearrange("(n p) d -> p n d", p=P), "ld_x")
            for n, name in enumerate(("itok_B_0_8", "itok_B_2_61", "itok_B_0_2")):
                load(ids[:, n, :], row(name).to_broadcast([P, B]), "ld_ids")
            sp.wait_ge(S_["k_mem"], 1)
            full = LANGS * ADIM // P
            b1a = I["L0_cond_b1"].rearrange("l a -> (l a)")
            load(rows[R_ADAPT:R_ADAPT + full, :], b1a[0:full * P].rearrange("(n p) -> n p", p=P), "ld_rows")
            load(rows[R_ADAPT + full:R_ADAPT + full + 1, 0:LANGS * ADIM - full * P],
                 b1a[full * P:LANGS * ADIM].rearrange("(a n) -> a n", a=1), "ld_rows")
            for r, name in ((R_L0Q, "bq"), (R_L0K, "bk"), (R_L0V, "bv")):
                load(rows[r:r + 1, :], row("L0_attn_" + name), "ld_rows")
            for r, name in ((V_BQ, "bq"), (V_BK, "bk"), (V_BV, "bv"), (V_S1, "ln1_s"), (V_B1, "ln1_b"),
                            (V_S2, "ln2_s"), (V_B2, "ln2_b")):
                load(rows[r:r + LV * (LAYERS - 1) + 1:LV, :], I["L1_attn_" + name], "ld_rows")
            for c in range(FC):
                load(rows[V_FF + c:V_FF + c + LV * (LAYERS - 1) + 1:LV, :], I["L1_attn_b1"][:, c * P:(c + 1) * P], "ld_rows")
            for t, q in enumerate("qkv"):
                load(rows[R_LEAF + t * LFC:R_LEAF + (t + 1) * LFC, :],
                     I[f"L1_ffn_{q}_b1"].rearrange("(c a) n -> c (a n)", a=P // LEAFW), "ld_rows")
            load(w1a[:, :].rearrange("p (l a) -> p l a", l=LANGS), I["L0_cond_W1"].rearrange("l d a -> d l a"), "ld_a")
            w2 = I["L0_cond_W2"].rearrange("l a d -> (l a) d")
            load(w2a[:, 0:full, :], w2[0:full * P, :].rearrange("(c p) d -> p c d", p=P), "ld_a")
            load(w2a[0:LANGS * ADIM - full * P, full, :], w2[full * P:LANGS * ADIM, :], "ld_a")
            for n, name in enumerate(("b2", "gamma", "beta")):
                load(lang_rows[:, n, :], I["L0_cond_" + name], "ld_a")
            for n, q in enumerate("qkvo"):
                load(w_nat[:, n, :], I["L0_attn_W" + q], "ld_b")
            load(token_bias[:, :], row("L0_attn_bo"), "ld_b")
            load(cat_bias[:, :], I["L0_cond2_bias"], "ld_c")
            sp.wait_ge(S_["ld_ids"], 48)
            with sp.Fori(0, B) as b:
                cat = sp.value_load(ids[0:1, 1, bass.ds(b, 1)], min_val=0, max_val=CATS - 1)
                sp.dma_start(w_cat[:, bass.ds(b, 1), :],
                             I["L0_cond2_weight"][bass.ds(cat, 1), :, :].rearrange("a p n -> p a n")
                             ).then_inc(S_["ld_cat"], 16)
            for e in range(ME):
                load(ar1[:, e * MR:(e + 1) * MR], I["L0_ffn_A1"][e], "ld_d")
                load(ar2[:, :, e * MR:(e + 1) * MR], I["L0_ffn_A2"][e].rearrange("(c p) r -> p c r", p=P), "ld_d")
            load(ar1[:, MER:MER + ME], I["L0_ffn_R1"], "ld_d")
            load(ar2[:, :, MER:MER + ME], I["L0_ffn_R2"].rearrange("(c p) e -> p c e", p=P), "ld_d")
            load(b1aug[0:MER, :], I["L0_ffn_B1"].rearrange("e r n -> (e r) n"), "ld_d")
            load(b1aug[MER:MER + 1, :], row("L0_ffn_b1"), "ld_d")
            load(b2aug[0:MER, :], I["L0_ffn_B2"].rearrange("e r n -> (e r) n"), "ld_d")
            load(b2aug[MER:MER + 1, :], row("L0_ffn_b2"), "ld_d")
            load(w1f[:, :], I["L0_ffn_W1"], "ld_d")
            load(w2f[:, :, :], I["L0_ffn_W2"].rearrange("(c p) n -> p c n", p=P), "ld_d")

            def load_ffns(wi, wo, n, at, sem):
                load(arena[:, at:at + n, 0, :], I[wi][0:n].rearrange("e d f -> d e f"), sem)
                for e in range(n):
                    load(arena[:, at + e, 1, :].rearrange("p (c n) -> p c n", c=FC),
                         I[wo][e].rearrange("(c p) n -> p c n", p=P), sem)

            load(gvec[:, 0, :], I["L1_cond_gate_vecs"], "ld_e")
            load_ffns("L1_cond_share_wi", "L1_cond_share_wo", L1S, 0, "ld_e")
            load_ffns("L1_cond_expert_wi", "L1_cond_expert_wo", L1E, L1S, "ld_e")
            load(gate1[:, :, :], I["L1_cond_gate_w1"].rearrange("(c p) n -> p c n", p=P), "ld_e")
            load(gate2[:, :], I["L1_cond_gate_w2"], "ld_e")

            def load_layer(l, s):
                one = bass.ds(l, 1)
                for n, q in enumerate("qkvo"):
                    load(wl[s][:, n * D:(n + 1) * D].rearrange("p (a n) -> p a n", a=1),
                         I["L1_attn_W" + q][one].rearrange("a p n -> p a n"), f"ld_f{s}")
                load(wl[s][:, 4 * D:4 * D + FF].rearrange("p (a n) -> p a n", a=1),
                     I["L1_attn_W1"][one].rearrange("a p n -> p a n"), f"ld_f{s}")
                load(wl[s][:, 4 * D + FF:].rearrange("p (c n) -> p c n", c=FC),
                     I["L1_attn_W2"][one].rearrange("a (c p) n -> p (a c) n", p=P), f"ld_f{s}")
                load(vl[s][:, :].rearrange("p (a n) -> p a n", a=1),
                     cols[:, 0:LV * LAYERS].rearrange("p (l n) -> p l n", l=LAYERS)[:, one, :], f"ld_f{s}")
                load(bl[s][:, 0:1, :], I["L1_attn_bo"][one].rearrange("(o a) n -> o a n", o=1), f"ld_f{s}")
                load(bl[s][:, 1:2, :], I["L1_attn_b2"][one].rearrange("(o a) n -> o a n", o=1), f"ld_f{s}")

            sp.wait_ge(S_["p_colsc"], 1)
            for s in range(2):
                load_layer(s, s)
            load(gate1b[:, :, :], I["L1_cond2_g1"].rearrange("(c p) n -> p c n", p=P), "ld_g")
            load(gate2b[:, :], I["L1_cond2_g2"], "ld_g")
            sp.wait_ge(S_["dve"], 2)
            for t, q in enumerate("qkv"):
                load(node_rows[t * LEAVES:t * LEAVES + NODES, :], I[f"L1_ffn_{q}_node_w"], "ld_h")
                load(node_bias[0:1, t * LEAVES:t * LEAVES + NODES], row(f"L1_ffn_{q}_node_b"), "ld_h")
                load(leaf_b2[t * QUAD:t * QUAD + LEAVES, :], I[f"L1_ffn_{q}_b2"], "ld_h")
            sp.wait_ge(S_["c_mm"], 2)
            for t, q in enumerate("qkv"):
                load(w_tree(t)[:, 0].rearrange("p c (a n) -> p (c a) n", a=P // LEAFW),
                     I[f"L1_ffn_{q}_w1"].rearrange("l d n -> d l n"), "ld_h")
                load(w_tree(t)[:, 1], I[f"L1_ffn_{q}_w2"].rearrange("(c a) n d -> (a n) c d", a=P // LEAFW), "ld_h")
            sp.wait_ge(S_["e_acc"], 2 * (L1S + 1))
            load_ffns("L1_cond2_swi", "L1_cond2_swo", L2S, 0, "ld_g")
            load_ffns("L1_cond2_wi", "L1_cond2_wo", TYPES, L2S, "ld_g")
            with sp.Fori(1, LAYERS // 2) as it:
                for s in range(2):
                    sp.wait_ge(S_["f_x"], it * 8 + (4 * s - 4))
                    load_layer(it * 2 + s, s)
            for h in HALVES:
                sp.wait_ge(S_["h_fin"], h + 1)
                sp.dma_start(out.rearrange("b s d -> (b s) d").rearrange("(n p) d -> p n d", p=P)
                             [:, h * TILES:(h + 1) * TILES, :], yt[:, h]).then_inc(S_["st_out"], 16)
            sp.wait_ge(S_["st_out"], 32)

        @block.gpsimd
        def _(pool):
            own = Chain(pool, S_["pool"])
            nc.gpsimd.memset(rows[:, :], 0.0).then_inc(S_["k_mem"], 1)
            nc.gpsimd.memset(ones[:, :], 1.0).then_inc(S_["k_mem"], 1)
            nc.gpsimd.memset(minus_half[:, :], -0.5).then_inc(S_["k_mem"], 1)
            nc.gpsimd.memset(zg[:, :, :, :], 0.0).then_inc(S_["k_mem"], 1)
            nc.gpsimd.memset(eps_cond[:, :], EPS_COND).then_inc(S_["k_mem"], 1)
            nc.gpsimd.memset(eps_ln[:, :], EPS_LN).then_inc(S_["k_mem"], 1)
            pool.wait_ge(S_["k_mem"], 6)
            nc.gpsimd.memset(zg[:, :, :, MER:MER + 1], 1.0).then_inc(S_["k_mem"], 1)

            def root(n, eps, half):
                pool.wait_ge(S_["var"], n)
                own.link(nc.gpsimd.tensor_tensor(rv[:, half, :], mv[:, half, :, 1], eps, ALU.add))
                nc.gpsimd.tensor_tensor(rstd[:, half, :], rv[:, half, :], minus_half[:, :], ALU.pow
                                        ).then_inc(S_["rstd"], 1)

            for h in HALVES:
                root(h + 1, eps_cond[:, :], h)

            for n in range(2 * NG):
                h, g = n % 2, n // 2
                if g == 0:
                    pool.wait_ge(S_["a_cond"], h + 1)
                if g >= 3:
                    pool.wait_ge(S_["b_vr"], n - 5)
                src = cf[:, h][:, g * GB * S:(g + 1) * GB * S].rearrange("p (b s) -> p b s", s=S)
                nc.gpsimd.tensor_copy(z(h, g % 3).rearrange("p (b j s) -> p b j s", b=GB, j=HPQ),
                                      src.unsqueeze(2).to_broadcast([P, GB, HPQ, S])).then_inc(S_["b_rep"], 1)

            root(3, eps_ln[:, :], 0)
            own_base = own.n

            with pool.Fori(0, LAYERS - 1) as l:
                own.base, own.n = l * 4 + own_base, 0
                for n, h in enumerate((0, 1, 1, 0)):
                    root(l * 4 + (4 + n), eps_ln[:, :], h)
                assert own.n == 4
            own.base, own.n = None, own_base + 4 * (LAYERS - 1)
            last = 4 * (LAYERS - 1)
            for n, h in enumerate((0, 1, 1)):
                root(last + 4 + n, eps_ln[:, :], h)

        @block.scalar
        def _(act):
            def copy(dst, src, sem):
                nc.scalar.activation(dst, src, ACT.Copy).then_inc(S_[sem], 1)

            def linear(dst, src, bias, scale=1.0):
                return nc.scalar.activation(dst, src, ACT.Identity, bias=bias, scale=scale)

            for h in HALVES:
                act.wait_ge(S_["x_tr"], h + 1)
                copy(xf[:, h], ps[h][:, 3, :], "x_f")
            act.wait_ge(S_["p_cols"], 1)
            copy(cols[:, :], ps[0][:, 0, 0:P], "p_colsc")
            act.wait_ge(S_["p_watt"], 1)
            copy(w_att[:, :, :].rearrange("p a n -> p (a n)"), ps[1][:, 0, :], "p_wattc")
            act.wait_ge(S_["p_rope"], 1)
            copy(rope_bias[:, :], ps[0][:, 1, 0:2], "p_ropec")
            act.wait_ge(S_["p_bat"], 1)
            copy(batch_cols[:, :, :].rearrange("p a b -> p (a b)"), ps[0][:, 2, 0:3 * B], "p_batc")

            for c in range(LCH):
                m = min(P, LANGS * ADIM - c * P)
                for h in HALVES:
                    act.wait_ge(S_["a_hid"], 2 * c + h + 1)
                    nc.scalar.activation(z(h, c)[0:m, :], ps[h][0:m, c, :], ACT.Relu,
                                         bias=cols[0:m, R_ADAPT + c:R_ADAPT + c + 1]).then_inc(S_["a_relu"], 1)

            act.wait_ge(S_["p_keyb"], 1)
            for h in HALVES:
                act.wait_ge(S_["b_qk"], h + 1)
                for q in range(HG):
                    ins = linear(keys_by_quadrant(h)[:, :, q, :], by_batch(ps[h][:, 1, :]), key_bias[:, q:q + 1],
                                 vmask[:, q * HD:q * HD + 1])
                ins.then_inc(S_["b_k"], 1)
            for n in range(2 * NG):
                h, g = n % 2, n // 2
                act.wait_ge(S_["b_sub"], n + 1)
                nc.scalar.activation(z(h, 4 + g), z(h, 4 + g), ACT.Exp).then_inc(S_["b_exp"], 1)
            for h in HALVES:
                act.wait_ge(S_["b_ctx"], h + 1)
                linear(z(h, 0), ps[h][:, 1, :], cols[:, R_L0V:R_L0V + 1]).then_inc(S_["b_ctxc"], 1)
            for h in HALVES:
                act.wait_ge(S_["b_tr"], h + 1)
                copy(xf[:, h], ps[h][:, 3, :], "b_xf")

            def mixture(r):
                for h in HALVES:
                    act.wait_ge(S_["d_z"], 2 * (2 * r + h) + 1)
                    nc.scalar.activation(logit[:, h], logit[:, h], ACT.Exp).then_inc(S_["d_e"], 1)
                for h in HALVES:
                    act.wait_ge(S_["d_zt"], 2 * r + h + 1)
                    copy(zgt[:, h], ps[h][0:QUAD, 3, :], "d_ztc")

            mixture(0)
            for c in range(FC):
                for h in HALVES:
                    act.wait_ge(S_["d_hid"], 2 * c + h + 1)
                    nc.scalar.activation(z(h, c), ps[h][:, c % 3, :], ACT.Relu).then_inc(S_["d_relu"], 1)
            mixture(1)
            for h in HALVES:
                act.wait_ge(S_["d_tr"], h + 1)
                copy(xf[:, h], ps[h][:, 3, :], "d_xf")

            def experts(k, items, shares):
                for n, (j, e, c, first, last) in enumerate(items):
                    for h in HALVES:
                        if e is None:
                            act.wait_ge(S_[k + "_hid"], 2 * n + h + 1)
                            nc.scalar.activation(z(h, 4 + n % 4), ps[h][:, n % 2, :], ACT.Relu
                                                 ).then_inc(S_[k + "_ra"], 1)
                    if (n + 1 < len(items) and c == 0 and first and j > 0) or n + 1 == len(items):
                        g = j if n + 1 == len(items) else j - 1
                        for h in HALVES:
                            act.wait_ge(S_[k + "_acc"], 2 * g + h + 1)
                            copy(z(h, g), ps[h][:, 2 + g % 2, :], k + "_accc")
                for h in HALVES:
                    act.wait_ge(S_[k + "_g1"], h + 1)
                    nc.scalar.activation(grel[:, h], ps[h][:, 0, 0:HB], ACT.Relu).then_inc(S_[k + "_g1c"], 1)
                for h in HALVES:
                    act.wait_ge(S_[k + "_g2"], 2 * h + 2)
                    nc.scalar.activation(gsm[:, h, 4:5 + shares], ps[h][0:HB, 1, 0:shares + 1], ACT.Exp,
                                         bias=gsm[:, h, 8:9], accum_out=gsm[:, h, 9:10]).then_inc(S_[k + "_ge"], 1)
                for h in HALVES:
                    act.wait_ge(S_[k + "_gb"], h + 1)
                    copy(gcol[:, h, 0:shares + 1, :].rearrange("p a b -> p (a b)"),
                         ps[h][:, 2, 0:(shares + 1) * HB], k + "_gbc")

            act.wait_ge(S_["p_gw"], 1)
            nc.scalar.activation(gvec[:, 1, :], gvec[:, 1, :], ACT.Exp, scale=10.0,
                                 accum_out=gred[:, 1:2]).then_inc(S_["p_gw"], 1)
            act.wait_ge(S_["p_coef"], 1)
            copy(type_coef[:, :, :].rearrange("p e b -> p (e b)"), ps[0][:, 3, 0:L1E * B], "p_coefc")
            experts("e", E_ITEMS, L1S)

            def col(r, s):
                return vl[s][:, r:r + 1]

            def qkv(l, h, s):
                nc.scalar.preload_act_table_set("natural_log_exp_and_others")
                act.wait_ge(S_["f_qkv"], l * 2 + (h + 1))
                nc.scalar.activation(z(h, 6), ps[h][:, 1, :], ACT.Exp, bias=col(V_BK, s)).then_inc(S_["f_exp"], 1)
                nc.scalar.activation(z(h, 7), ps[h][:, 1, :], ACT.Relu, bias=col(V_BK, s)).then_inc(S_["f_exp"], 1)
                nc.scalar.activation(z(h, 4), ps[h][:, 0, :], ACT.Exp, bias=col(V_BQ, s)).then_inc(S_["f_exp"], 1)
                nc.scalar.activation(z(h, 5), ps[h][:, 0, :], ACT.Relu, bias=col(V_BQ, s)).then_inc(S_["f_exp"], 1)

            def den(l, h):
                act.wait_ge(S_["f_den"], l * 2 + (h + 1))
                nc.scalar.activation(z(h, 10), z(h, 10), ACT.Ln, scale=1.0 / EPS_ATTN, bias=1.0
                                     ).then_inc(S_["f_rel"], 1)
                act.wait_ge(S_["f_rel"], l * 2 + (h + 1))
                nc.scalar.activation(z(h, 10), z(h, 10), ACT.Exp, scale=-1.0).then_inc(S_["f_lnexp"], 1)

            def gelu_o(l, h):
                act.wait_ge(S_["f_o"], l * 2 + (h + 1))
                nc.scalar.activation(z(h, 4), ps[h][:, 0, :], ACT.Gelu_apprx_tanh).then_inc(S_["f_og"], 1)

            def affine(l, h, s, n):
                act.wait_ge(S_["f_tr"], tr_count(l, h, n))
                linear(cf[:, h], ps[h][:, 1 + n, :], col((V_B1, V_B2)[n], s), col((V_S1, V_S2)[n], s)
                       ).then_inc(S_["f_x"], 1)

            def gelu_h(l, h, s):
                for c in range(FC):
                    act.wait_ge(S_["f_w1"], l * (2 * FC) + (h * FC + c + 1))
                    nc.scalar.activation(z(h, c), ps[h][:, c % 3, :], ACT.Gelu_apprx_tanh,
                                         bias=col(V_FF + c, s)).then_inc(S_["f_h"], 1)

            def gelu_f(l, h):
                act.wait_ge(S_["f_w2"], l * 2 + (h + 1))
                nc.scalar.activation(z(h, 4), ps[h][:, 1, :], ACT.Gelu_apprx_tanh).then_inc(S_["f_w2g"], 1)

            qkv(0, 0, 0)
            den(0, 0)
            gelu_o(0, 0)

            def segment(l, a, sa, m, b, sb_):
                affine(m, b, sb_, 0)
                qkv(l, a, sa)
                den(l, a)
                gelu_h(m, b, sb_)
                gelu_o(l, a)
                gelu_f(m, b)
                affine(m, b, sb_, 1)

            def layer(l, s):
                segment(l, 1, s, l, 0, s)
                segment(l + 1, 0, 1 - s, l, 1, s)

            with act.Fori(0, LAYERS // 2 - 1) as it:
                layer(it * 2, 0)
                layer(it * 2 + 1, 1)
            layer(LAYERS - 2, 0)
            last = LAYERS - 1
            segment(last, 1, 1, last, 0, 1)
            affine(last, 1, 1, 0)
            gelu_h(last, 1, 1)
            gelu_f(last, 1)
            affine(last, 1, 1, 1)

            for h in HALVES:
                act.wait_ge(S_["g_tr"], h + 1)
                copy(xf[:, h], ps[h][:, 2, :], "g_xf")
            experts("g", G_ITEMS, L2S)

            act.wait_ge(S_["p_node"], 1)
            copy(node_t[:, :], ps[1][:, 1, 0:TREES * LEAVES], "p_nodec")
            for h in HALVES:
                act.wait_ge(S_["h_st"], h + 1)
                copy(selt[:, h], ps[h][0:TREES * QUAD, 3, :], "h_stc")
            for t in range(TREES):
                for h in HALVES:
                    act.wait_ge(S_["h_lb"], 2 * t + h + 1)
                    copy(z(h, 12 + t), ps[h][:, t, :], "h_lbc")
            for n in range(TREES * LFC):
                t, c = divmod(n, LFC)
                for h in HALVES:
                    act.wait_ge(S_["h_hid"], 2 * n + h + 1)
                    if n >= 3:
                        act.wait_ge(S_["h_mask"], 2 * (n - 3) + h + 1)
                    nc.scalar.activation(z(h, 4 + n % 3), ps[h][:, n % 2, :], ACT.Relu,
                                         bias=cols[:, R_LEAF + n:R_LEAF + n + 1]).then_inc(S_["h_relu"], 1)
                if n % LFC == 1 and t > 0 or n == TREES * LFC - 1:
                    g = t if n == TREES * LFC - 1 else t - 1
                    for h in HALVES:
                        act.wait_ge(S_["h_acc"], 2 * g + h + 1)
                        copy(z(h, g), ps[h][:, 2 + g % 2, :], "h_accc")
            for h in HALVES:
                act.wait_ge(S_["h_sub"], h + 1)
                nc.scalar.activation(z(h, 3)[:, 0:HT // 4], z(h, 3)[:, 0:HT // 4], ACT.Exp,
                                     scale=float(1.0 / np.sqrt(D))).then_inc(S_["h_exp"], 1)

        @block.vector
        def _(dve):
            own = Chain(dve, S_["dve"])
            V = nc.vector

            dve.wait_ge(S_["ld_ids"], 48)
            dve.wait_ge(S_["ld_const"], 16)
            own.step(V.memset(node_rows[:, :], 0.0))
            own.step(V.memset(node_bias[:, :], 0.0))
            own.link(V.tensor_copy(idf[:, :, :], ids[:, :, :]))
            iota = kc[:, K_IOTA:K_IOTA + 1]
            own.link(V.tensor_scalar(lang_hot[:, :], idf[:, 0, :], iota, None, ALU.is_equal))
            V.tensor_scalar(cat_hot[:, :], idf[:, 1, :], iota, None, ALU.is_equal).then_inc(S_["p_hot"], 1)
            V.tensor_scalar(type_hot[:, :], idf[:, 2, :], iota, None, ALU.is_equal).then_inc(S_["p_hot"], 1)
            V.tensor_copy(lang_tok[:, :, :], spread(lang_hot[0:16, :], S)).then_inc(S_["p_hot"], 1)
            for c in range(LCH):
                own.step(V.tensor_scalar(lang_mask[:, c, :], idf[:, 0, :], kc[:, K_LANG + c:K_LANG + c + 1], None,
                                         ALU.is_equal))
            for t in range(TYPES):
                own.step(V.tensor_scalar(type_mask[:, t, :], idf[:, 2, :], float(t), None, ALU.is_equal))
            own.step(V.tensor_copy(leaf_val[:, :], kc[:, K_SLOT:K_SLOT + 1].to_broadcast([P, P])))
            own.sync()

            def stats(h, src, res, sem="var"):
                own.link(V.tensor_tensor(yt[:, h].rearrange("p i d -> p (i d)"), src, res, ALU.add))
                for i in range(TILES):
                    own.step(V.bn_stats(stat[:, h, i, :], yt[:, h, i, :]))
                own.sync()
                own.step(V.memset(after_stats[:, :], 0.0))
                for i in range(TILES):
                    ins = V.bn_aggr(mv[:, h, i, :], stat[:, h, i, :])
                    if i < TILES - 1:
                        own.step(ins)
                ins.then_inc(S_[sem], 1)

            def normalise(n, h):
                dve.wait_ge(S_["var"], n)
                dve.wait_ge(S_["rstd"], n)
                for i in range(TILES):
                    ins = V.tensor_scalar(xn[:, h, i, :], yt[:, h, i, :], mv[:, h, i, 0:1], rstd[:, h, i:i + 1],
                                          ALU.subtract, ALU.mult)
                    if i < TILES - 1:
                        own.step(ins)
                ins.then_inc(S_["xn"], 1)

            for c in range(LCH):
                m = min(P, LANGS * ADIM - c * P)
                for h in HALVES:
                    dve.wait_ge(S_["a_relu"], 2 * c + h + 1)
                    mask = spread(lang_mask[0:m, c, h * HB:(h + 1) * HB], S)
                    V.tensor_tensor(by_batch(z(h, c)[0:m, :]), by_batch(z(h, c)[0:m, :]), mask, ALU.mult
                                    ).then_inc(S_["a_mask"], 1)
            for h in HALVES:
                dve.wait_ge(S_["a_out"], h + 1)
                stats(h, ps[h][:, 3, :], xt[0][:, h].rearrange("p i d -> p (i d)"))
            for h in HALVES:
                normalise(h + 1, h)
            dve.wait_ge(S_["p_batc"], 1)
            for h in HALVES:
                dve.wait_ge(S_["a_tr"], h + 1)
                bs = slice(h * HB, (h + 1) * HB)
                own.link(V.tensor_tensor(by_batch(cf[:, h]), by_batch(ps[h][:, 0, :]), spread(gamma_b[:, bs], S), ALU.mult))
                V.tensor_tensor(by_batch(cf[:, h]), by_batch(cf[:, h]), spread(beta_b[:, bs], S), ALU.add
                                ).then_inc(S_["a_cond"], 1)

            dve.wait_ge(S_["p_ropec"], 1)
            V.tensor_scalar(key_bias[:, :], vmask[:, 0:QUAD:HD], rope_bias[:, 1:2], None, ALU.mult).then_inc(S_["p_keyb"], 1)
            for h in HALVES:
                dve.wait_ge(S_["b_qk"], h + 1)
                qe = z(h, 8, 4).rearrange("p g (b j s) -> p (g b) j s", b=GB, j=HPQ)
                for j in range(HPQ):
                    ins = V.tensor_scalar(qe[:, :, j, :], by_batch(ps[h][:, 0, :]), rope_bias[:, 0:1],
                                          kc[:, K_HEAD + j:K_HEAD + j + 1], ALU.add, ALU.mult)
                    if j < HPQ - 1:
                        own.step(ins)
                ins.then_inc(S_["b_qe"], 1)

            def grouped(ap, n=S):
                return ap.rearrange("p (a s) -> p a s", s=n)

            def values_and_scores(n):
                h, g = n % 2, n // 2
                dve.wait_ge(S_["b_vr"], n + 1)
                V.tensor_tensor(grouped(z(h, 12 + g), P), grouped(ps[h][:, 2, :], P),
                                vmask.unsqueeze(1).to_broadcast([P, GB, P]), ALU.mult).then_inc(S_["b_vx"], 1)
                dve.wait_ge(S_["b_sc"], n + 1)
                sc = ps[h][:, (3, 0)[g % 2], :]
                own.link(V.tensor_reduce(small[:, h, 0:16], grouped(sc), AX_X, ALU.max))
                V.tensor_tensor(grouped(z(h, 4 + g)), grouped(sc), spread(small[:, h, 0:16], S), ALU.subtract
                                ).then_inc(S_["b_sub"], 1)

            def probabilities(n):
                h, g = n % 2, n // 2
                dve.wait_ge(S_["b_exp"], n + 1)
                own.link(V.tensor_reduce(small[:, h, 16:32], grouped(z(h, 4 + g)), AX_X, ALU.add))
                own.link(V.reciprocal(small[:, h, 32:48], small[:, h, 16:32]))
                own.link(V.tensor_tensor(grouped(z(h, 4 + g)), grouped(z(h, 4 + g)), spread(small[:, h, 32:48], S), ALU.mult))
                V.transpose(z(h, 8 + g), z(h, 4 + g)).then_inc(S_["b_pt"], 1)

            for n in range(2 * NG + 1):
                if n < 2 * NG:
                    values_and_scores(n)
                if n >= 1:
                    probabilities(n - 1)

            def residual(h, src, old, new, sem):
                V.tensor_tensor(new[:, h].rearrange("p i d -> p (i d)"), src, old[:, h].rearrange("p i d -> p (i d)"),
                                ALU.add).then_inc(S_[sem], 1)

            for h in HALVES:
                dve.wait_ge(S_["b_out"], h + 1)
                residual(h, ps[h][:, 2, :], xt[0], xt[1], "b_res")

            for h in HALVES:
                dve.wait_ge(S_["c_mm"], h + 1)
                V.tensor_tensor(by_batch(cf[:, h]), by_batch(ps[h][:, 0, :]), spread(cbias_b[:, h * HB:(h + 1) * HB], S),
                                ALU.add).then_inc(S_["c_out"], 1)

            def mixture(r):
                zr = [ps[h][:, (1, 0)[r], :].rearrange("p (i k) -> p i k", i=TILES) for h in HALVES]
                for h in HALVES:
                    dve.wait_ge(S_[("d_r1", "d_r2")[r]], h + 1)
                    own.link(V.tensor_reduce(small[:, h, 0:TILES], zr[h][:, :, MER:MER + ME], AX_X, ALU.max))
                    V.tensor_tensor(logit[:, h], zr[h][:, :, MER:MER + ME], spread(small[:, h, 0:TILES], ME), ALU.subtract
                                    ).then_inc(S_["d_z"], 1)
                    dve.wait_ge(S_["d_e"], 2 * r + h + 1)
                    own.link(V.tensor_reduce(small[:, h, 4:4 + TILES], logit[:, h], AX_X, ALU.add))
                    own.link(V.reciprocal(small[:, h, 8:8 + TILES], small[:, h, 4:4 + TILES]))
                    own.link(V.scalar_tensor_tensor(logit[:, h], logit[:, h], 1.0 / MR,
                                                    spread(small[:, h, 8:8 + TILES], ME), ALU.mult, ALU.mult))
                    if r == 1:
                        dve.wait_ge(S_["d_zt"], h + 1)
                    V.tensor_tensor(zg[:, h, :, 0:MER].rearrange("p i (e r) -> p i e r", e=ME),
                                    zr[h][:, :, 0:MER].rearrange("p i (e r) -> p i e r", e=ME),
                                    spread(logit[:, h], MR), ALU.mult).then_inc(S_["d_z"], 1)

            dve.wait_ge(S_["k_mem"], 7)
            mixture(0)
            mixture(1)
            for h in HALVES:
                dve.wait_ge(S_["d_out"], h + 1)
                residual(h, ps[h][:, 1, :], xt[1], xt[0], "d_res")

            dve.wait_ge(S_["ld_e"], 16 * (5 + L1S + L1E))
            own.link(V.tensor_reduce(gred[:, 0:1], gvec[:, 0, :], AX_X, ALU.max))
            V.tensor_scalar(gvec[:, 1, :], gvec[:, 0, :], gred[:, 0:1], None, ALU.subtract).then_inc(S_["p_gw"], 1)
            dve.wait_ge(S_["p_gw"], 2)
            own.link(V.reciprocal(gred[:, 2:3], gred[:, 1:2]))
            own.link(V.scalar_tensor_tensor(gvec[:, 2, :], gvec[:, 1, :], gred[:, 2:3], kc[0:TYPES, K_BAND:K_BAND + L1E],
                                            ALU.mult, ALU.mult))
            V.tensor_copy(gwide[:, :, :], spread(gvec[:, 2, :], P)).then_inc(S_["p_gw"], 1)

            def experts(k, items, shares, coef):
                kinds = counts_of(items)
                for n, (j, e, c, first, last) in enumerate(items):
                    if e is None:
                        continue
                    for h in HALVES:
                        dve.wait_ge(S_[k + "_hid"], 2 * n + h + 1)
                        V.scalar_tensor_tensor(by_batch(z(h, 4 + n % 4)), by_batch(ps[h][:, n % 2, :]), 0.0,
                                               spread(coef[:, e, h * HB:(h + 1) * HB], S), ALU.max, ALU.mult
                                               ).then_inc(S_[k + "_rd"], 1)
                m = shares + 1
                for h in HALVES:
                    dve.wait_ge(S_[k + "_g2"], 2 * h + 1)
                    V.tensor_reduce(gsm[:, h, 8:9], ps[h][0:HB, 1, 0:m], AX_X, ALU.max, negate=True
                                    ).then_inc(S_[k + "_g2"], 1)
                for h in HALVES:
                    dve.wait_ge(S_[k + "_ge"], h + 1)
                    own.link(V.reciprocal(gsm[:, h, 10:11], gsm[:, h, 9:10]))
                    own.link(V.tensor_scalar(gsm[:, h, 0:m], gsm[:, h, 4:4 + m], gsm[:, h, 10:11], None, ALU.mult))
                    V.tensor_copy(gwb[:, h, 0:m, :], spread(gsm[:, h, 0:m], P)).then_inc(S_[k + "_gw"], 1)
                for h in HALVES:
                    dve.wait_ge(S_[k + "_gbc"], h + 1)
                    for j in range(m):
                        g = shares if j == 0 else j - 1
                        own.step(V.tensor_tensor(by_batch(z(h, g)), by_batch(z(h, g)), spread(gcol[:, h, j, :], S), ALU.mult))
                    own.sync()
                    for j in range(1, m - 1):
                        own.link(V.tensor_tensor(z(h, 0), z(h, 0), z(h, j), ALU.add))
                    V.tensor_tensor(cf[:, h], z(h, 0), z(h, m - 1), ALU.add).then_inc(S_[k + "_out"], 1)

            dve.wait_ge(S_["p_coefc"], 1)
            experts("e", E_ITEMS, L1S, type_coef)

            def col(r, s):
                return vl[s][:, r:r + 1]

            def keys(l, h, s):
                dve.wait_ge(S_["f_exp"], l * 8 + (4 * h + 2))
                own.link(V.scalar_tensor_tensor(z(h, 8), z(h, 6), 1.0, z(h, 7), ALU.min, ALU.add))
                own.link(V.scalar_tensor_tensor(z(h, 9), ps[h][:, 2, :], col(V_BV, s), z(h, 8), ALU.add, ALU.mult))
                own.link(V.tensor_reduce(small[:, h, 0:2 * HB], z(h, 8, 2).rearrange("p a (b s) -> p (a b) s", s=S),
                                         AX_X, ALU.add))
                dve.wait_ge(S_["f_exp"], l * 8 + (4 * h + 4))
                own.link(V.tensor_scalar(z(h, 4), z(h, 4), 1.0, 1.0, ALU.min, ALU.subtract))
                own.link(V.scalar_tensor_tensor(z(h, 11), z(h, 4), 1.0, z(h, 5), ALU.add, ALU.add))
                V.tensor_tensor(by_batch(z(h, 10)), by_batch(z(h, 11)), spread(small[:, h, 0:HB], S), ALU.mult
                                ).then_inc(S_["f_den"], 1)
                own.link(V.reciprocal(small2[:, h, 0:HB], small[:, h, 0:HB]))
                own.link(V.scalar_tensor_tensor(small2[:, h, HB:2 * HB], small2[:, h, 0:HB], -1.0,
                                                small[:, h, HB:2 * HB], ALU.mult, ALU.mult))

            def values(l, h):
                dve.wait_ge(S_["f_lnexp"], l * 2 + (h + 1))
                V.scalar_tensor_tensor(by_batch(z(h, 12)), by_batch(z(h, 10)), 1.0, spread(small2[:, h, HB:2 * HB], S),
                                       ALU.subtract, ALU.mult).then_inc(S_["f_v"], 1)

            def norm_stats(l, h, n):
                dve.wait_ge(S_[("f_og", "f_w2g")[n]], l * 2 + (h + 1))
                dve.wait_ge(S_["f_ft"], ft_count(l, h, n))
                stats(h, ps[h][:, 3, :], z(h, 4))

            def norm(l, h, n):
                normalise(tr_count(l, h, n) + 2, h)

            before = own.n
            keys(0, 0, 0)
            values(0, 0)
            norm_stats(0, 0, 0)
            norm(0, 0, 0)
            lead = own.n
            per = 2 * (lead - before) + 2 * (2 + 2 * TILES - 1 + TILES - 1)

            def segment(l, a, sa, m, b):
                keys(l, a, sa)
                values(l, a)
                norm_stats(m, b, 1)
                norm(m, b, 1)
                norm_stats(l, a, 0)
                norm(l, a, 0)

            def layer(l, s):
                segment(l, 1, s, l, 0)
                segment(l + 1, 0, 1 - s, l, 1)

            with dve.Fori(0, LAYERS // 2 - 1) as it:
                own.base, own.n = it * (2 * per) + lead, 0
                layer(it * 2, 0)
                layer(it * 2 + 1, 1)
                assert own.n == 2 * per, (own.n, per)
            own.base, own.n = None, lead + (LAYERS - 2) * per
            layer(LAYERS - 2, 0)
            last = LAYERS - 1
            segment(last, 1, 1, last, 0)
            norm_stats(last, 1, 1)
            norm(last, 1, 1)

            for h in HALVES:
                dve.wait_ge(S_["f_ft"], ft_count(LAYERS, h, 0) + 0)
                residual(h, ps[h][:, 3, :], xt[0], xt[1], "g_res")

            experts("g", G_ITEMS, L2S, type_mask)

            own.step(V.memset(sel[:, :, :, :, :], 0.0))
            for h in HALVES:
                dve.wait_ge(S_["h_sc"], h + 1)
                sc = ps[h][:, 0, 0:TILES * 64].rearrange("p (i k) -> p i k", i=TILES)[:, :, 0:TREES * LEAVES]
                d = dec[:, h]
                own.link(V.tensor_scalar(d.rearrange("p (i t) k -> p i (t k)", i=TILES), sc, 0.0, None, ALU.is_ge))
                r = reach[:, h]
                own.step(V.tensor_copy(r[:, :, 1], d[:, :, 0]))
                own.link(V.tensor_scalar(r[:, :, 0], d[:, :, 0], -1.0, 1.0, ALU.mult, ALU.add))
                at, new, first = 0, 2, 1
                while first < NODES:
                    k = first + 1
                    src = r[:, :, at:at + k]
                    if 2 * k == LEAVES:
                        dst = sel[:, h].rearrange("p i t k -> p (i t) k")[:, :, 0:LEAVES]
                    else:
                        dst = r[:, :, new:new + 2 * k]
                    pair = dst.rearrange("p n (k two) -> p n k two", two=2)
                    own.link(V.tensor_tensor(pair[:, :, :, 1], src, d[:, :, first:first + k], ALU.mult))
                    ins = V.tensor_tensor(pair[:, :, :, 0], src, pair[:, :, :, 1], ALU.subtract)
                    if 2 * k == LEAVES:
                        ins.then_inc(S_["h_sel"], 1)
                    else:
                        own.link(ins)
                    at, new, first = new, new + 2 * k, first + k
            for h in HALVES:
                dve.wait_ge(S_["h_stc"], h + 1)
                V.tensor_copy(selb[:, h], selt[:, h]).then_inc(S_["h_stb"], 1)
            for n in range(TREES * LFC):
                t, c = divmod(n, LFC)
                for h in HALVES:
                    dve.wait_ge(S_["h_lbc"], 2 * t + h + 1)
                    dve.wait_ge(S_["h_relu"], 2 * n + h + 1)
                    V.scalar_tensor_tensor(z(h, 8 + n % 3), z(h, 12 + t), kc[:, K_LEAF + c:K_LEAF + c + 1], z(h, 4 + n % 3),
                                           ALU.is_equal, ALU.mult).then_inc(S_["h_mask"], 1)
            for h in HALVES:
                own.step(V.memset(z(h, 12), 0.0))
            for h in HALVES:
                dve.wait_ge(S_["h_s"], h + 1)
                sc = grouped(ps[h][:, 0, 0:TILES * S])
                own.link(V.tensor_reduce(small[:, h, 0:TILES], sc, AX_X, ALU.max))
                V.tensor_tensor(grouped(z(h, 3)[:, 0:TILES * S]), sc, spread(small[:, h, 0:TILES], S), ALU.subtract
                                ).then_inc(S_["h_sub"], 1)
            for h in HALVES:
                dve.wait_ge(S_["h_exp"], h + 1)
                e = grouped(z(h, 3)[:, 0:TILES * S])
                own.link(V.tensor_reduce(small[:, h, 4:4 + TILES], e, AX_X, ALU.add))
                own.link(V.reciprocal(small[:, h, 8:8 + TILES], small[:, h, 4:4 + TILES]))
                own.link(V.tensor_tensor(e, e, spread(small[:, h, 8:8 + TILES], S), ALU.mult))
                for q in range(P // QUAD):
                    rows_q = slice(q * QUAD, (q + 1) * QUAD)
                    pt = z(h, 12).rearrange("p (i n) -> p i n", i=TILES)
                    ins = V.transpose(pt[rows_q, :, rows_q], e[rows_q])
                    if q < P // QUAD - 1:
                        own.step(ins)
                ins.then_inc(S_["h_pt"], 1)
            for h in HALVES:
                dve.wait_ge(S_["h_o"], h + 1)
                residual(h, ps[h][:, 1, :], xt[1], yt, "h_fin")

        @block.tensor
        def _(pe):
            T = nc.tensor

            def turn(dst, srcs, sem, n=P, m=P):
                for i, s in enumerate(srcs):
                    ins = T.transpose(dst[:, i * P:(i + 1) * P], s, ident)
                ins.then_inc(S_[sem], 1)

            pe.wait_ge(S_["ld_const"], 16)
            pe.wait_ge(S_["ld_x"], 16)
            for h in HALVES:
                turn(ps[h][:, 3, :], [xt[0][:, h, i, :] for i in range(TILES)], "x_tr")
            pe.wait_ge(S_["ld_rows"], 16 * (2 + 3 + LV + TREES))
            turn(ps[0][:, 0, :], [rows[:, :]], "p_cols")
            pe.wait_ge(S_["ld_b"], 16 * 5)
            for n, turned in enumerate((rope_q, rope_k, ident, ident)):
                ins = T.matmul(ps[1][:, 0, n * D:(n + 1) * D], w_nat[:, n, :], turned, start=True, stop=True)
            ins.then_inc(S_["p_watt"], 1)
            pe.wait_ge(S_["p_colsc"], 1)
            T.matmul(ps[0][:, 1, 0:1], rope_q, cols[:, R_L0Q:R_L0Q + 1], start=True, stop=True)
            T.matmul(ps[0][:, 1, 1:2], rope_k, cols[:, R_L0K:R_L0K + 1], start=True, stop=True).then_inc(S_["p_rope"], 1)
            pe.wait_ge(S_["p_hot"], 3)
            pe.wait_ge(S_["ld_a"], 16 * 6)
            pe.wait_ge(S_["ld_c"], 16)
            T.matmul(ps[0][:, 2, 0:B], lang_rows[:, 1, :], lang_hot[0:LANGS, :], start=True, stop=True)
            T.matmul(ps[0][:, 2, B:2 * B], lang_rows[:, 2, :], lang_hot[0:LANGS, :], start=True, stop=True)
            T.matmul(ps[0][:, 2, 2 * B:3 * B], cat_bias[:, :], cat_hot[0:CATS, :], start=True, stop=True
                     ).then_inc(S_["p_bat"], 1)
            pe.wait_ge(S_["p_ropec"], 1)
            pe.wait_ge(S_["p_wattc"], 1)
            pe.wait_ge(S_["p_batc"], 1)

            for c in range(LCH):
                m = min(P, LANGS * ADIM - c * P)
                for h in HALVES:
                    if c == 0:
                        pe.wait_ge(S_["x_f"], h + 1)
                    T.matmul(ps[h][0:m, c, :], w1a[:, c * P:c * P + m], xf[:, h], start=True, stop=True
                             ).then_inc(S_["a_hid"], 1)
            for h in HALVES:
                pe.wait_ge(S_["a_mask"], 2 * (LCH - 1) + h + 1)
                for i in range(TILES):
                    dst = ps[h][:, 3, tok(h, i)]
                    for c in range(LCH):
                        m = min(P, LANGS * ADIM - c * P)
                        T.matmul(dst, z(h, c)[0:m, tok(h, i)], w2a[0:m, c, :], start=(c == 0), stop=False)
                    b0 = h * HB + i * (P // S)
                    ins = T.matmul(dst, lang_tok[0:LANGS, b0:b0 + P // S, :].rearrange("p b s -> p (b s)"),
                                   lang_rows[:, 0, :], start=False, stop=True)
                ins.then_inc(S_["a_out"], 1)
            for h in HALVES:
                pe.wait_ge(S_["xn"], h + 1)
                turn(ps[h][:, 0, :], [xn[:, h, i, :] for i in range(TILES)], "a_tr")

            for h in HALVES:
                pe.wait_ge(S_["a_cond"], h + 1)
                T.matmul(ps[h][:, 1, :], w_att[:, 1, :], cf[:, h], start=True, stop=True)
                T.matmul(ps[h][:, 0, :], w_att[:, 0, :], cf[:, h], start=True, stop=True).then_inc(S_["b_qk"], 1)

            def batch(ap, b):
                return ap[:, b * S:(b + 1) * S]

            def values_and_scores(n):
                h, g = n % 2, n // 2
                pe.wait_ge(S_["b_rep"], n + 1)
                if n >= 2:
                    pe.wait_ge(S_["b_vx"], n - 1)
                for b in range(GB):
                    ins = T.matmul(ps[h][:, 2, b * D:(b + 1) * D], z(h, g % 3)[:, b * P:(b + 1) * P], w_att[:, 2, :],
                                   start=True, stop=True)
                ins.then_inc(S_["b_vr"], 1)
                if g == 0:
                    pe.wait_ge(S_["b_k"], h + 1)
                    pe.wait_ge(S_["b_qe"], h + 1)
                if n >= 4:
                    pe.wait_ge(S_["b_sub"], n - 3)
                for b in range(GB):
                    r = slice(b * P, (b + 1) * P)
                    ins = T.matmul(ps[h][:, (3, 0)[g % 2], r], z(h, 8 + g)[:, r], z(h, 4 + g)[:, r], start=True, stop=True)
                ins.then_inc(S_["b_sc"], 1)

            def context(n):
                h, g = n % 2, n // 2
                pe.wait_ge(S_["b_pt"], n + 1)
                for b in range(GB):
                    for q in range(HG):
                        r = slice(q * QUAD, (q + 1) * QUAD)
                        at = (b * HG + q) * S
                        col = (g * GB + b) * S
                        ins = T.matmul(ps[h][r, 1, col:col + S], z(h, 12 + g)[:, b * D + q * QUAD:b * D + (q + 1) * QUAD],
                                       z(h, 8 + g)[:, at:at + S], start=True, stop=True, tile_position=(0, q * QUAD))
                if g == NG - 1:
                    ins.then_inc(S_["b_ctx"], 1)

            for n in range(2 * NG + 2):
                if n < 2 * NG:
                    values_and_scores(n)
                if n >= 2:
                    context(n - 2)
            for h in HALVES:
                pe.wait_ge(S_["b_ctxc"], h + 1)
                for i in range(TILES):
                    dst = ps[h][:, 2, tok(h, i)]
                    T.matmul(dst, z(h, 0)[:, tok(h, i)], w_att[:, 3, :], start=True, stop=False)
                    ins = T.matmul(dst, ones[:, :], token_bias[:, :], start=False, stop=True)
                ins.then_inc(S_["b_out"], 1)
            for h in HALVES:
                pe.wait_ge(S_["b_res"], h + 1)
                turn(ps[h][:, 3, :], [xt[1][:, h, i, :] for i in range(TILES)], "b_tr")

            pe.wait_ge(S_["ld_cat"], 16 * B)
            for h in HALVES:
                pe.wait_ge(S_["b_xf"], h + 1)
                for b in range(HB):
                    ins = T.matmul(batch(ps[h][:, 0, :], b), w_cat[:, h * HB + b, :], batch(xf[:, h], b),
                                   start=True, stop=True)
                ins.then_inc(S_["c_mm"], 1)

            pe.wait_ge(S_["ld_d"], 16 * (2 * ME + 8))
            for h in HALVES:
                pe.wait_ge(S_["c_out"], h + 1)
                for i in range(TILES):
                    ins = T.matmul(ps[h][:, 1, i * P:i * P + MER + ME], cf[:, h][:, tok(h, i)], ar1[:, :], start=True, stop=True)
                ins.then_inc(S_["d_r1"], 1)

            def turn_parts(r):
                for h in HALVES:
                    pe.wait_ge(S_["d_z"], 2 * (2 * r + h) + 2)
                    turn(ps[h][0:QUAD, 3, :], [zg[:, h, i, :] for i in range(TILES)], "d_zt")

            turn_parts(0)
            for c in range(FC):
                for h in HALVES:
                    if c == 0:
                        pe.wait_ge(S_["d_ztc"], h + 1)
                    if c >= 3:
                        pe.wait_ge(S_["d_relu"], 2 * (c - 3) + h + 1)
                    dst = ps[h][:, c % 3, :]
                    T.matmul(dst, w1f[:, c * P:(c + 1) * P], cf[:, h], start=True, stop=False)
                    T.matmul(dst, b1aug[:, c * P:(c + 1) * P], zgt[0:MER + 1, h], start=False, stop=True
                             ).then_inc(S_["d_hid"], 1)
            for h in HALVES:
                pe.wait_ge(S_["d_relu"], 2 * (FC - 1) + h + 1)
                for i in range(TILES):
                    for c in range(FC):
                        ins = T.matmul(ps[h][:, 0, i * P:i * P + MER + ME], z(h, c)[:, tok(h, i)], ar2[:, c, :],
                                       start=(c == 0), stop=(c == FC - 1))
                ins.then_inc(S_["d_r2"], 1)
            turn_parts(1)
            for h in HALVES:
                pe.wait_ge(S_["d_ztc"], 2 + h + 1)
                for i in range(TILES):
                    dst = ps[h][:, 1, tok(h, i)]
                    for c in range(FC):
                        T.matmul(dst, z(h, c)[:, tok(h, i)], w2f[:, c, :], start=(c == 0), stop=False)
                    ins = T.matmul(dst, zgt[0:MER + 1, h, tok(h, i)], b2aug[:, :], start=False, stop=True)
                ins.then_inc(S_["d_out"], 1)
            for h in HALVES:
                pe.wait_ge(S_["d_res"], h + 1)
                turn(ps[h][:, 3, :], [xt[0][:, h, i, :] for i in range(TILES)], "d_tr")

            def experts(k, items, shares, xin, g1, g2):
                kinds = counts_of(items)

                def hidden(n):
                    j, e, c, first, last = items[n]
                    slot = j if e is None else shares + e
                    for h in HALVES:
                        if n == 0:
                            pe.wait_ge(S_[xin], h + 1)
                        if n >= 2:
                            kind, at = kinds[n - 2]
                            pe.wait_ge(S_[k + ("_ra", "_rd")[kind]], 2 * at + h + 1)
                        T.matmul(ps[h][:, n % 2, :], arena[:, slot, 0, c * P:(c + 1) * P], xf[:, h], start=True, stop=True
                                 ).then_inc(S_[k + "_hid"], 1)

                def output(n):
                    j, e, c, first, last = items[n]
                    slot = j if e is None else shares + e
                    kind, at = kinds[n]
                    for h in HALVES:
                        pe.wait_ge(S_[k + ("_ra", "_rd")[kind]], 2 * at + h + 1)
                        if first and j >= 2:
                            pe.wait_ge(S_[k + "_accc"], 2 * (j - 2) + h + 1)
                        ins = T.matmul(ps[h][:, 2 + j % 2, :], arena[:, slot, 1, c * P:(c + 1) * P], z(h, 4 + n % 4),
                                       start=first, stop=last)
                        if last:
                            ins.then_inc(S_[k + "_acc"], 1)

                for n in range(len(items) + 1):
                    if n < len(items):
                        hidden(n)
                    if n >= 1:
                        output(n - 1)
                for h in HALVES:
                    pe.wait_ge(S_[k + "_accc"], 2 * shares + h + 1)
                    for j in range(shares + 1):
                        g = shares if j == 0 else j - 1
                        ins = T.matmul(ps[h][:, 0, 0:HB], g1[:, j, :], by_batch(z(h, g))[:, :, 0],
                                       start=(j == 0), stop=(j == shares))
                    ins.then_inc(S_[k + "_g1"], 1)
                for h in HALVES:
                    pe.wait_ge(S_[k + "_g1c"], h + 1)
                    if h == 1:
                        pe.wait_ge(S_[k + "_g2"], 2)
                    T.matmul(ps[h][0:HB, 1, 0:shares + 1], grel[:, h], g2[:, :], start=True, stop=True
                             ).then_inc(S_[k + "_g2"], 1)
                for h in HALVES:
                    pe.wait_ge(S_[k + "_gw"], h + 1)
                    for j in range(shares + 1):
                        ins = T.matmul(ps[h][:, 2, j * HB:(j + 1) * HB], gwb[:, h, j, :], ident[0:HB, 0:HB],
                                       start=True, stop=True)
                    ins.then_inc(S_[k + "_gb"], 1)

            pe.wait_ge(S_["p_gw"], 3)
            pe.wait_ge(S_["d_xf"], 1)
            for e in range(L1E):
                ins = T.matmul(ps[0][:, 3, e * B:(e + 1) * B], gwide[:, e, :], type_hot[0:TYPES, :], start=True, stop=True)
            ins.then_inc(S_["p_coef"], 1)
            pe.wait_ge(S_["p_coefc"], 1)
            pe.wait_ge(S_["ld_e"], 16 * (5 + L1S + L1E))
            experts("e", E_ITEMS, L1S, "d_xf", gate1, gate2)

            for h in HALVES:
                pe.wait_ge(S_["e_out"], h + 1)
                turn(ps[h][:, 3, :], [cf[:, h][:, tok(h, i)] for i in range(TILES)], "f_ft")

            def qkv(l, h, s):
                for n in (1, 0, 2):
                    ins = T.matmul(ps[h][:, n, :], wl[s][:, n * D:(n + 1) * D], cf[:, h], start=True, stop=True)
                ins.then_inc(S_["f_qkv"], 1)

            def bias_rows(h, bank, s, n):
                T.matmul(ps[h][:, bank, :], ones[:, :], bl[s][:, n:n + 1, :].to_broadcast([1, TILES, D]),
                         start=True, stop=False)

            def attn_out(l, h, s):
                pe.wait_ge(S_["f_v"], l * 2 + (h + 1))
                bias_rows(h, 0, s, 0)
                for i in range(TILES):
                    ins = T.matmul(ps[h][:, 0, tok(h, i)], z(h, 12)[:, tok(h, i)], wl[s][:, 3 * D:4 * D], start=False,
                                   stop=(i == TILES - 1))
                ins.then_inc(S_["f_o"], 1)

            def turns(l, h, n):
                pe.wait_ge(S_["xn"], tr_count(l, h, n) + 2)
                turn(ps[h][:, 1 + n, :], [xn[:, h, i, :] for i in range(TILES)], "f_tr")

            def turns_back(l, h, n):
                pe.wait_ge(S_["f_x"], tr_count(l, h, n))
                turn(ps[h][:, 3, :], [cf[:, h][:, tok(h, i)] for i in range(TILES)], "f_ft")

            def ffn_in(l, h, s):
                for c in range(FC):
                    if c >= 3:
                        pe.wait_ge(S_["f_h"], l * (2 * FC) + (h * FC + c - 2))
                    T.matmul(ps[h][:, c % 3, :], wl[s][:, 4 * D + c * P:4 * D + (c + 1) * P], cf[:, h],
                             start=True, stop=True).then_inc(S_["f_w1"], 1)

            def ffn_out(l, h, s):
                pe.wait_ge(S_["f_h"], l * (2 * FC) + (h * FC + 2))
                bias_rows(h, 1, s, 1)
                for c in range(FC):
                    if c >= 2:
                        pe.wait_ge(S_["f_h"], l * (2 * FC) + (h * FC + c + 1))
                    for i in range(TILES):
                        ins = T.matmul(ps[h][:, 1, tok(h, i)], z(h, c)[:, tok(h, i)],
                                       wl[s][:, 4 * D + FF + c * D:4 * D + FF + (c + 1) * D], start=False,
                                       stop=(c == FC - 1 and i == TILES - 1))
                ins.then_inc(S_["f_w2"], 1)

            def arrived(s, k):
                pe.wait_ge(S_[f"ld_f{s}"], k)

            arrived(0, 16 * 9)
            qkv(0, 0, 0)
            attn_out(0, 0, 0)
            turns(0, 0, 0)

            def segment(l, a, sa, m, b, sb_):
                qkv(l, a, sa)
                turns_back(m, b, 0)
                ffn_in(m, b, sb_)
                attn_out(l, a, sa)
                ffn_out(m, b, sb_)
                turns(m, b, 1)
                turns_back(m, b, 1)
                turns(l, a, 0)

            def layer(l, s, s_next, next_loaded):
                segment(l, 1, s, l, 0, s)
                arrived(s_next, next_loaded)
                segment(l + 1, 0, s_next, l, 1, s)

            with pe.Fori(0, LAYERS // 2 - 1) as it:
                layer(it * 2, 0, 1, it * (16 * 9) + 16 * 9)
                layer(it * 2 + 1, 1, 0, it * (16 * 9) + 2 * 16 * 9)
            layer(LAYERS - 2, 0, 1, 16 * 9 * (LAYERS // 2))
            last = LAYERS - 1
            segment(last, 1, 1, last, 0, 1)
            turns_back(last, 1, 0)
            ffn_in(last, 1, 1)
            ffn_out(last, 1, 1)
            turns(last, 1, 1)
            turns_back(last, 1, 1)

            for h in HALVES:
                pe.wait_ge(S_["g_res"], h + 1)
                turn(ps[h][:, 2, :], [xt[1][:, h, i, :] for i in range(TILES)], "g_tr")

            pe.wait_ge(S_["ld_g"], 16 * (4 + L2S + TYPES))
            experts("g", G_ITEMS, L2S, "g_xf", gate1b, gate2b)

            pe.wait_ge(S_["ld_h"], 16 * 15)
            pe.wait_ge(S_["g_gbc"], 2)
            T.transpose(ps[1][:, 1, 0:TREES * LEAVES], node_rows[:, :], ident[0:TREES * LEAVES, 0:TREES * LEAVES]
                        ).then_inc(S_["p_node"], 1)
            pe.wait_ge(S_["p_nodec"], 1)
            for h in HALVES:
                pe.wait_ge(S_["g_out"], h + 1)
                for i in range(TILES):
                    dst = ps[h][:, 0, i * 64:i * 64 + TREES * LEAVES]
                    T.matmul(dst, cf[:, h][:, tok(h, i)], node_t[:, :], start=True, stop=False)
                    ins = T.matmul(dst, ones[:, :], node_bias[:, :], start=False, stop=True)
                ins.then_inc(S_["h_sc"], 1)
            for h in HALVES:
                pe.wait_ge(S_["h_sel"], h + 1)
                turn(ps[h][0:TREES * QUAD, 3, :],
                     [sel[:, h, i].rearrange("p t k -> p (t k)") for i in range(TILES)], "h_st")
            for t in range(TREES):
                r = slice(t * QUAD, t * QUAD + LEAVES)
                for h in HALVES:
                    pe.wait_ge(S_["h_stb"], h + 1)
                    T.matmul(ps[h][:, t, :], leaf_val[r, :], selb[r, h], start=True, stop=True).then_inc(S_["h_lb"], 1)

            def leaf_hidden(n):
                t, c = divmod(n, LFC)
                for h in HALVES:
                    if n < 2:
                        pe.wait_ge(S_["h_lbc"], 2 * TREES - 1 + h)
                    else:
                        pe.wait_ge(S_["h_relu"], 2 * (n - 2) + h + 1)
                    T.matmul(ps[h][:, n % 2, :], w_tree(t)[:, 0, c, :], cf[:, h], start=True, stop=True
                             ).then_inc(S_["h_hid"], 1)

            def leaf_output(n):
                t, c = divmod(n, LFC)
                r = slice(t * QUAD, t * QUAD + LEAVES)
                for h in HALVES:
                    bank = ps[h][:, 2 + t % 2, :]
                    if c == 0:
                        pe.wait_ge(S_["h_stc"], h + 1)
                        if t == 2:
                            pe.wait_ge(S_["h_accc"], h + 1)
                    pe.wait_ge(S_["h_mask"], 2 * n + h + 1)
                    hm = z(h, 8 + n % 3)
                    if t < 2:
                        ins = T.matmul(bank, w_tree(t)[:, 1, c, :], hm, start=(c == 0), stop=False)
                        if c == LFC - 1:
                            ins = T.matmul(bank, leaf_b2[r, :], selt[r, h], start=False, stop=True)
                    else:
                        for i in range(TILES):
                            ins = T.matmul(bank[:, tok(h, i)], hm[:, tok(h, i)], w_tree(t)[:, 1, c, :],
                                           start=(c == 0 and i == 0), stop=False, skip_group_check=True)
                        if c == LFC - 1:
                            for i in range(TILES):
                                ins = T.matmul(bank[:, tok(h, i)], selt[r, h, tok(h, i)], leaf_b2[r, :],
                                               start=False, stop=(i == TILES - 1), skip_group_check=True)
                    if c == LFC - 1:
                        ins.then_inc(S_["h_acc"], 1)

            for n in range(TREES * LFC + 1):
                if n < TREES * LFC:
                    leaf_hidden(n)
                if n >= 1:
                    leaf_output(n - 1)
            for h in HALVES:
                pe.wait_ge(S_["h_accc"], 2 + h + 1)
                for b in range(HB):
                    i, q = divmod(b, P // S)
                    r = slice(q * QUAD, (q + 1) * QUAD)
                    ins = T.matmul(ps[h][r, 0, i * S:(i + 1) * S], batch(z(h, 0), b), batch(z(h, 1), b),
                                   start=True, stop=True, tile_position=(0, q * QUAD))
                ins.then_inc(S_["h_s"], 1)
            for h in HALVES:
                pe.wait_ge(S_["h_pt"], h + 1)
                pe.wait_ge(S_["h_accc"], 4 + h + 1)
                for i in range(TILES):
                    ins = T.matmul(ps[h][:, 1, tok(h, i)], z(h, 12)[:, tok(h, i)], z(h, 2)[:, tok(h, i)],
                                   start=True, stop=True)
                ins.then_inc(S_["h_o"], 1)


def kernel(**inputs):
    import concourse.bacc as _bacc
    from concourse.bass_utils import run_bass_kernel_spmd as _run

    nc = _bacc.Bacc("TRN2", target_bir_lowering=False, num_devices=1)
    arrays, aps = {}, {}
    for name, value in inputs.items():
        a = np.ascontiguousarray(value)
        arrays[f"in_{name}"] = a
        aps[name] = nc.dram_tensor(f"in_{name}", a.shape, mybir.dt.from_np(a.dtype), kind="ExternalInput").ap()
    k = shape_constants()
    arrays["shape_constants"] = k
    konst = nc.dram_tensor("shape_constants", k.shape, F32, kind="ExternalInput").ap()
    out = nc.dram_tensor("out", (B, S, D), F32, kind="ExternalOutput").ap()
    network(nc, aps, konst, out)
    r = _run(nc, [arrays], core_ids=[0])
    return r.results[0]["out"]
```

```python
from contextlib import ExitStack

import numpy as np

import concourse.bass as bass
from concourse import mybir

F32 = mybir.dt.float32
BF16 = mybir.dt.bfloat16
I32 = mybir.dt.int32
ALU = mybir.AluOpType
ACT = mybir.ActivationFunctionType
AX_X = mybir.AxisListType.X

P = 128
B, S, D = 32, 32, 128
HALVES = (0, 1)
HB = B // 2
HT = HB * S
TILES = HT // P
BANKS = 4

LANGS, ADIM = 10, 32
LCH = -(-LANGS * ADIM // P)
HEADS, HD = 16, 8
QUAD = 32
HPQ = QUAD // HD
HG = HEADS // HPQ
GB = 4
NG = HB // GB
CATS = 64
FF = 512
FC = FF // P
ME, MR = 3, 8
MER = ME * MR
L1E, L1S = 4, 3
TYPES = 3
L2S = 2
LAYERS = 8
TREES, LEAVES, LEAFW = 3, 16, 64
NODES = LEAVES - 1
LFC = LEAVES * LEAFW // P

EPS_COND = 1e-5
EPS_ATTN = 1e-6
EPS_LN = 1e-6

LV = 7 + FC
V_BQ, V_BK, V_BV, V_S1, V_B1, V_S2, V_B2, V_FF = range(8)
R_LEAF = LV * LAYERS
R_ADAPT = 0
R_L0Q, R_L0K, R_L0V = LCH, LCH + 1, LCH + 2
R_END0 = R_L0V + 1

WARM = (16, 22, 8, 0, 0, 12, 2)

FFN_BANK = (0, 2, 1, 0)

K_IOTA, K_LANG, K_HEAD, K_LEAF, K_SLOT, K_BAND = 0, 1, 4, 8, 16, 18
K_IDENT, K_ROPEQ, K_ROPEK, K_VMASK = 32, 32 + P, 32 + 2 * P, 32 + 3 * P
K_END = 32 + 4 * P


def shape_constants():
    k = np.zeros((P, K_END), np.float32)
    p = np.arange(P)
    k[:, K_IOTA] = p
    for c in range(LCH):
        k[:, K_LANG + c] = c * (P // ADIM) + p // ADIM
    for j in range(HPQ):
        k[:, K_HEAD + j] = (p % QUAD) // HD == j
    for c in range(LFC):
        k[:, K_LEAF + c] = c * (P // LEAFW) + p // LEAFW
    k[:, K_SLOT] = p % QUAD
    for t in range(TYPES):
        k[t, K_BAND + t:K_BAND + t + 2] = 1.0
    k[:, K_IDENT:K_IDENT + P] = np.eye(P)
    inv = 1.0 / 10000.0 ** (np.arange(0, HD, 2, dtype=np.float64) / HD)
    rot = np.zeros((P, P))
    for h in range(HEADS):
        ang = np.concatenate([h * inv, h * inv])
        for d in range(HD):
            row = h * HD + d
            rot[row, row] = np.cos(ang[d])
            rot[row, row + 1 if d % 2 == 0 else row - 1] = -np.sin(ang[d]) if d % 2 == 0 else np.sin(ang[d])
    k[:, K_ROPEQ:K_ROPEQ + P] = rot.T / np.sqrt(HD)
    k[:, K_ROPEK:K_ROPEK + P] = rot.T
    for f in range(P):
        k[:, K_VMASK + f] = p // QUAD == (f % QUAD) // HD
    return k


class Chain:

    def __init__(self, eng, sem):
        self.eng, self.sem, self.n, self.base = eng, sem, 0, None

    def step(self, ins):
        ins.then_inc(self.sem, 1)
        self.n += 1

    def sync(self):
        self.eng.wait_ge(self.sem, self.n if self.base is None else self.base + self.n)

    def link(self, ins):
        self.step(ins)
        self.sync()

    def mark(self, ins):
        self.step(ins)
        return self.n

    def after(self, place):
        self.eng.wait_ge(self.sem, place if self.base is None else self.base + place)


def expert_items(shares, experts):
    items = [(j, None, c, c == 0, c == FC - 1) for j in range(shares) for c in range(FC)]
    items += [(shares, e, c, e == 0 and c == 0, e == experts - 1 and c == FC - 1)
              for e in range(experts) for c in range(FC)]
    return items


def counts_of(items):
    seen = [0, 0]
    out = []
    for it in items:
        kind = int(it[1] is not None)
        out.append((kind, seen[kind]))
        seen[kind] += 1
    return out


def network(nc, I, konst, out):
    ctx = ExitStack()
    with ctx:
        def sb(name, shape, dt=F32):
            return ctx.enter_context(nc.sbuf_tensor(name, shape, dt))

        kc = sb("kc", [P, K_END])
        ident, rope_q, rope_k = (kc[:, k:k + P] for k in (K_IDENT, K_ROPEQ, K_ROPEK))
        vmask = kc[:, K_VMASK:K_VMASK + P]
        rows0 = sb("rows0", [R_END0, P])
        cols0 = sb("cols0", [P, R_END0])
        rows = sb("rows", [P, P])
        cols = sb("cols", [P, P])
        ids = sb("ids", [P, 3, B], I32)
        idf = sb("idf", [P, 3, B])
        ones = sb("ones", [1, P])
        minus_half = sb("minus_half", [P, TILES])
        ones3 = sb("ones3", [3, P], BF16)
        lang_hot = sb("lang_hot", [P, B])
        cat_hot = sb("cat_hot", [P, B])
        type_hot = sb("type_hot", [P, B])
        lang_mask = sb("lang_mask", [P, LCH, B])
        type_mask = sb("type_mask", [P, TYPES, B])
        batch_cols = sb("batch_cols", [P, 3, B])
        gamma_b, beta_b, cbias_b = (batch_cols[:, n, :] for n in range(3))
        w1a = sb("w1a", [P, LANGS * ADIM])
        w2a = sb("w2a", [P, LCH, D])
        lang_rows = sb("lang_rows", [LANGS, 3, D])
        w_att = sb("w_att", [P, 4, D])
        rope_bias = sb("rope_bias", [P, 2])
        key_bias = sb("key_bias", [P, HG])
        token_bias = sb("token_bias", [1, D])
        cat_bias = sb("cat_bias", [CATS, D])
        big = sb("big", [P, B * D])
        w_cat = big[:, :].rearrange("p (b n) -> p b n", b=B)
        ar1 = sb("ar1", [P, MER + ME])
        ar2 = sb("ar2", [P, FC, MER + ME])
        b1aug = sb("b1aug", [MER + 1, FF])
        b2aug = sb("b2aug", [MER + 1, D])
        w1f = sb("w1f", [P, FF])
        w2f = sb("w2f", [P, FC, D])
        NE1 = L1S + L1E
        arena = sb("arena", [P, NE1, 2, FF])
        gate1 = sb("gate1", [P, L1S + 1, D])
        gate2 = sb("gate2", [P, L1S + 1])
        gate1b = sb("gate1b", [P, L2S + 1, D])
        gate2b = sb("gate2b", [P, L2S + 1])
        gvec = sb("gvec", [TYPES, 3, L1E])
        gred = sb("gred", [TYPES, 4])
        type_coef = sb("type_coef", [P, L1E, B])
        wl = [sb(f"wl{s}", [P, 4 * D + 2 * FF]) for s in range(2)]
        vl = [sb(f"vl{s}", [P, LV]) for s in range(2)]
        bias3 = sb("bias3", [3, 2 * LAYERS, D], BF16)
        rl = [sb(f"rl{s}", [3, 2, D], BF16) for s in range(2)]
        tree_v = sb("tree_v", [P, 2 * LFC * P])
        node_rows = sb("node_rows", [TREES * LEAVES, D])
        node_t = sb("node_t", [P, TREES * LEAVES])
        node_bias = sb("node_bias", [1, TREES * LEAVES])
        leaf_b2 = sb("leaf_b2", [TREES * QUAD, D])
        leaf_val = sb("leaf_val", [P, P], BF16)
        filler = sb("filler", [P, 1], BF16)

        xt = [sb(f"xt{n}", [P, 2, TILES, D]) for n in range(2)]
        xf = sb("xf", [P, 2, HT])
        cf = sb("cf", [P, 2, HT])
        yt = sb("yt", [P, 2, TILES, D])
        xn = sb("xn", [P, 2, TILES, D])
        stat = sb("stat", [P, 2, TILES, 6])
        after_stats = sb("after_stats", [P, 1])
        mv = sb("mv", [P, 2, TILES, 2])
        rv = sb("rv", [P, 2, TILES])
        rstd = sb("rstd", [P, 2, TILES])
        small = sb("small", [P, 2, 64])
        small2 = sb("small2", [P, 2, 64])
        logit = sb("logit", [P, 2, TILES, ME])
        zg = sb("zg", [P, 2, TILES, QUAD])
        zgt = sb("zgt", [QUAD, 2, HT])
        gsm = sb("gsm", [HB, 2, 16])
        gwb = sb("gwb", [HB, 2, 4, P])
        gcol = sb("gcol", [P, 2, 4, HB])
        grel = sb("grel", [P, 2, HB])
        dec = sb("dec", [P, 2, TILES * TREES, LEAVES])
        reach = sb("reach", [P, 2, TILES * TREES, 16])
        sel = sb("sel", [P, 2, TILES, TREES, QUAD])
        selt = sb("selt", [TREES * QUAD, 2, HT])
        selb = sb("selb", [TREES * QUAD, 2, HT], BF16)
        Z = [sb(f"z{h}", [P, 16, HT]) for h in HALVES]
        lang_tok = Z[0][0:16, 14:16, :].rearrange("p a (b s) -> p (a b) s", s=S)
        w_nat = Z[1][:, 14, :].rearrange("p (n d) -> p n d", n=4)
        row_bias = Z[1][0:1, 4:8, :].rearrange("p a n -> p (a n)")
        row_parts = Z[1][0:1, 8:14, :].bitcast(BF16).rearrange("p a n -> p (a n)")
        gwide = Z[0][0:TYPES, 15, :].rearrange("p (e n) -> p e n", e=L1E)

        ps = [ctx.enter_context(nc.psum_tensor(f"ps{h}", [P, BANKS, HT], F32)) for h in HALVES]

        class Sems(dict):
            def __missing__(self, name):
                self[name] = ctx.enter_context(nc.semaphore(name))
                return self[name]

        S_ = Sems()
        names = """ld_rb p_rb p_fill ld_const ld_ids ld_x ld_rows0 ld_rows ld_a1 ld_rowsb ld_a ld_b ld_cat ld_c ld_d ld_e ld_f0 ld_f1 ld_g ld_h st_out
            dve pool act_own k_mem p_cols0 p_cols0c p_cols p_colsc p_watt p_wattc p_rope p_ropec p_keyb p_node p_nodec p_hot p_bat p_batc
            p_gw p_coef p_coefc
            x_tr x_f a_hid a_relu a_mask a_out a_tr a_cond var rstd xn
            b_qk b_k b_rep b_qe b_vr b_vx b_sc b_sub b_exp b_pt b_ctx b_ctxc b_out b_res b_tr b_xf
            c_mm c_out d_r1 d_z d_e d_zt d_ztc d_hid d_relu d_r2 d_out d_res d_tr d_xf
            e_hid e_ra e_rd e_acc e_accc e_g1 e_g1c e_g2 e_ge e_gw e_gb e_gbc e_out e_tr0
            f_q f_k f_v f_vb f_exp f_ln f_den f_ratio f_u f_o f_og f_tr f_x f_y f_ft f_w1 f_h f_w2 f_w2g
            g_res g_tr g_xf
            g_hid g_ra g_rd g_acc g_accc g_g1 g_g1c g_g2 g_ge g_gw g_gb g_gbc g_out
            h_sc h_sel h_st h_stc h_stb h_lb h_lbc h_hid h_relu h_mask h_acc h_accc h_s h_sub h_exp h_pt h_o h_fin"""
        for n in names.split():
            S_[n]
        block = ctx.enter_context(nc.Block())

        def w_tree(t):
            w = tree_v[:, :] if t == 2 else big[:, t * 2 * LFC * P:(t + 1) * 2 * LFC * P]
            return w.rearrange("p (a c n) -> p a c n", a=2, c=LFC)

        def tok(h, i):
            return slice(i * P, (i + 1) * P)

        def z(h, n, k=1):
            return Z[h][:, n, :] if k == 1 else Z[h][:, n:n + k, :]

        def by_batch(ap):
            return ap.rearrange("p (b s) -> p b s", s=S)

        def row_part(n):
            return row_parts[:, n * 2 * LAYERS * D:(n + 1) * 2 * LAYERS * D]

        def spread(ap, n):
            return ap.unsqueeze(len(ap.shape)).to_broadcast([*ap.shape, n])

        def keys_by_quadrant(h):
            return z(h, 4, 4).rearrange("p g (b q s) -> p (g b) q s", b=GB, q=HG)

        def norm_count(l, h, n):
            first = isinstance(l, int) and l == 0
            last = isinstance(l, int) and l == LAYERS - 1
            if h == 0:
                return (1 if first else l * 4) if n == 0 else l * 4 + 3
            return l * 4 + 2 if n == 0 else l * 4 + (4 if last else 5)

        def back_count(l, h, n):
            if n == 1:
                return norm_count(l, h, 0) + 2
            if isinstance(l, int):
                return h + 1 if l == 0 else norm_count(l - 1, h, 1) + 2
            return l * 4 + (1 + 2 * h)

        E_ITEMS, G_ITEMS = expert_items(L1S, L1E), expert_items(L2S, TYPES)

        @block.sync
        def _(sp):
            def load(dst, src, sem):
                sp.dma_start(dst, src).then_inc(S_[sem], 16)

            def row(name):
                return I[name].rearrange("(a n) -> a n", a=1)

            load(kc[:, :], konst, "ld_const")
            load(xt[0][:, :, :, :].rearrange("p h i d -> p (h i) d"),
                 I["x"].rearrange("b s d -> (b s) d").rearrange("(n p) d -> p n d", p=P), "ld_x")
            for n, name in enumerate(("itok_B_0_8", "itok_B_2_61", "itok_B_0_2")):
                load(ids[:, n, :], row(name).to_broadcast([P, B]), "ld_ids")
            sp.wait_ge(S_["k_mem"], 2)
            full = LANGS * ADIM // P
            b1a = I["L0_cond_b1"].rearrange("l a -> (l a)")
            load(rows0[R_ADAPT:R_ADAPT + full, :], b1a[0:full * P].rearrange("(n p) -> n p", p=P), "ld_rows0")
            load(rows0[R_ADAPT + full:R_ADAPT + full + 1, 0:LANGS * ADIM - full * P],
                 b1a[full * P:LANGS * ADIM].rearrange("(a n) -> a n", a=1), "ld_rows0")
            for r, name in ((R_L0Q, "bq"), (R_L0K, "bk"), (R_L0V, "bv")):
                load(rows0[r:r + 1, :], row("L0_attn_" + name), "ld_rows0")
            load(w1a[:, :].rearrange("p (l a) -> p l a", l=LANGS), I["L0_cond_W1"].rearrange("l d a -> d l a"), "ld_a1")
            w2 = I["L0_cond_W2"].rearrange("l a d -> (l a) d")
            load(w2a[:, 0:full, :], w2[0:full * P, :].rearrange("(c p) d -> p c d", p=P), "ld_a")
            load(w2a[0:LANGS * ADIM - full * P, full, :], w2[full * P:LANGS * ADIM, :], "ld_a")
            for n, name in enumerate(("b2", "gamma", "beta")):
                load(lang_rows[:, n, :], I["L0_cond_" + name], "ld_a")
            for n, q in enumerate("qkvo"):
                load(w_nat[:, n, :], I["L0_attn_W" + q], "ld_b")
            load(token_bias[:, :], row("L0_attn_bo"), "ld_b")
            load(cat_bias[:, :], I["L0_cond2_bias"], "ld_c")
            for n, name in enumerate(("bo", "b2")):
                load(row_bias[:, n * LAYERS * D:(n + 1) * LAYERS * D],
                     I["L1_attn_" + name].rearrange("(a l) d -> a (l d)", a=1), "ld_rb")
            for r, name in ((V_BQ, "bq"), (V_BK, "bk"), (V_BV, "bv"), (V_S1, "ln1_s"), (V_B1, "ln1_b"),
                            (V_S2, "ln2_s"), (V_B2, "ln2_b")):
                load(rows[r:r + LV * (LAYERS - 1) + 1:LV, :], I["L1_attn_" + name], "ld_rows")
            for c in range(FC):
                load(rows[V_FF + c:V_FF + c + LV * (LAYERS - 1) + 1:LV, :], I["L1_attn_b1"][:, c * P:(c + 1) * P], "ld_rows")
            for t, q in enumerate("qkv"):
                load(rows[R_LEAF + t * LFC:R_LEAF + (t + 1) * LFC, :],
                     I[f"L1_ffn_{q}_b1"].rearrange("(c a) n -> c (a n)", a=P // LEAFW), "ld_rows")
            sp.wait_ge(S_["p_rb"], 5)
            for part in range(3):
                load(bias3[part:part + 1, :, :].rearrange("p l d -> p (l d)"), row_part(part), "ld_rb")
            sp.wait_ge(S_["ld_ids"], 48)
            with sp.Fori(0, B) as b:
                cat = sp.value_load(ids[0:1, 1, bass.ds(b, 1)], min_val=0, max_val=CATS - 1)
                sp.dma_start(w_cat[:, bass.ds(b, 1), :],
                             I["L0_cond2_weight"][bass.ds(cat, 1), :, :].rearrange("a p n -> p a n")
                             ).then_inc(S_["ld_cat"], 16)
            for e in range(ME):
                load(ar1[:, e * MR:(e + 1) * MR], I["L0_ffn_A1"][e], "ld_d")
                load(ar2[:, :, e * MR:(e + 1) * MR], I["L0_ffn_A2"][e].rearrange("(c p) r -> p c r", p=P), "ld_d")
            load(ar1[:, MER:MER + ME], I["L0_ffn_R1"], "ld_d")
            load(ar2[:, :, MER:MER + ME], I["L0_ffn_R2"].rearrange("(c p) e -> p c e", p=P), "ld_d")
            load(b1aug[0:MER, :], I["L0_ffn_B1"].rearrange("e r n -> (e r) n"), "ld_d")
            load(b1aug[MER:MER + 1, :], row("L0_ffn_b1"), "ld_d")
            load(b2aug[0:MER, :], I["L0_ffn_B2"].rearrange("e r n -> (e r) n"), "ld_d")
            load(b2aug[MER:MER + 1, :], row("L0_ffn_b2"), "ld_d")
            load(w1f[:, :], I["L0_ffn_W1"], "ld_d")
            load(w2f[:, :, :], I["L0_ffn_W2"].rearrange("(c p) n -> p c n", p=P), "ld_d")

            def load_ffns(wi, wo, n, at, sem):
                load(arena[:, at:at + n, 0, :], I[wi][0:n].rearrange("e d f -> d e f"), sem)
                for e in range(n):
                    load(arena[:, at + e, 1, :].rearrange("p (c n) -> p c n", c=FC),
                         I[wo][e].rearrange("(c p) n -> p c n", p=P), sem)

            load(gvec[:, 0, :], I["L1_cond_gate_vecs"], "ld_e")
            load_ffns("L1_cond_share_wi", "L1_cond_share_wo", L1S, 0, "ld_e")
            load_ffns("L1_cond_expert_wi", "L1_cond_expert_wo", L1E, L1S, "ld_e")
            load(gate1[:, :, :], I["L1_cond_gate_w1"].rearrange("(c p) n -> p c n", p=P), "ld_e")
            load(gate2[:, :], I["L1_cond_gate_w2"], "ld_e")

            def load_layer(l, s):
                one = bass.ds(l, 1)
                for n, q in enumerate("qkvo"):
                    load(wl[s][:, n * D:(n + 1) * D].rearrange("p (a n) -> p a n", a=1),
                         I["L1_attn_W" + q][one].rearrange("a p n -> p a n"), f"ld_f{s}")
                load(wl[s][:, 4 * D:4 * D + FF].rearrange("p (a n) -> p a n", a=1),
                     I["L1_attn_W1"][one].rearrange("a p n -> p a n"), f"ld_f{s}")
                load(wl[s][:, 4 * D + FF:].rearrange("p (c n) -> p c n", c=FC),
                     I["L1_attn_W2"][one].rearrange("a (c p) n -> p (a c) n", p=P), f"ld_f{s}")
                load(vl[s][:, :].rearrange("p (a n) -> p a n", a=1),
                     cols[:, 0:LV * LAYERS].rearrange("p (l n) -> p l n", l=LAYERS)[:, one, :], f"ld_f{s}")

                for n in range(2):
                    load(rl[s][:, n:n + 1, :], bias3[:, bass.ds(l + n * LAYERS, 1), :], f"ld_f{s}")

            sp.wait_ge(S_["ld_rb"], 16 * 5)
            sp.wait_ge(S_["p_colsc"], 1)
            for s in range(2):
                load_layer(s, s)
            load(gate1b[:, :, :], I["L1_cond2_g1"].rearrange("(c p) n -> p c n", p=P), "ld_g")
            load(gate2b[:, :], I["L1_cond2_g2"], "ld_g")
            sp.wait_ge(S_["dve"], 2)
            for t, q in enumerate("qkv"):
                load(node_rows[t * LEAVES:t * LEAVES + NODES, :], I[f"L1_ffn_{q}_node_w"], "ld_h")
                load(node_bias[0:1, t * LEAVES:t * LEAVES + NODES], row(f"L1_ffn_{q}_node_b"), "ld_h")
                load(leaf_b2[t * QUAD:t * QUAD + LEAVES, :], I[f"L1_ffn_{q}_b2"], "ld_h")
            sp.wait_ge(S_["c_mm"], 2)
            for t, q in enumerate("qkv"):
                load(w_tree(t)[:, 0].rearrange("p c (a n) -> p (c a) n", a=P // LEAFW),
                     I[f"L1_ffn_{q}_w1"].rearrange("l d n -> d l n"), "ld_h")
                load(w_tree(t)[:, 1], I[f"L1_ffn_{q}_w2"].rearrange("(c a) n d -> (a n) c d", a=P // LEAFW), "ld_h")
            sp.wait_ge(S_["e_acc"], 2 * (L1S + 1))
            load_ffns("L1_cond2_swi", "L1_cond2_swo", L2S, 0, "ld_g")
            load_ffns("L1_cond2_wi", "L1_cond2_wo", TYPES, L2S, "ld_g")
            with sp.Fori(0, LAYERS // 2 - 1) as it:
                for s in range(2):
                    sp.wait_ge(S_["f_y"], it * 4 + (2 * s + 2))
                    load_layer(it * 2 + (2 + s), s)
            for h in HALVES:
                sp.wait_ge(S_["h_fin"], h + 1)
                sp.dma_start(out.rearrange("b s d -> (b s) d").rearrange("(n p) d -> p n d", p=P)
                             [:, h * TILES:(h + 1) * TILES, :], yt[:, h]).then_inc(S_["st_out"], 16)
            sp.wait_ge(S_["st_out"], 32)

        @block.gpsimd
        def _(pool):
            nc.gpsimd.memset(filler[:, :], 0.0).then_inc(S_["p_fill"], 1)
            nc.gpsimd.memset(rows0[:, :], 0.0).then_inc(S_["k_mem"], 1)
            nc.gpsimd.memset(rows[:, :], 0.0).then_inc(S_["k_mem"], 1)
            nc.gpsimd.memset(ones[:, :], 1.0).then_inc(S_["k_mem"], 1)
            nc.gpsimd.memset(minus_half[:, :], -0.5).then_inc(S_["k_mem"], 1)
            nc.gpsimd.memset(zg[:, :, :, :], 0.0).then_inc(S_["k_mem"], 1)
            nc.gpsimd.memset(ones3[:, :], 1.0).then_inc(S_["k_mem"], 1)
            pool.wait_ge(S_["k_mem"], 6)
            nc.gpsimd.memset(zg[:, :, :, MER:MER + 1], 1.0).then_inc(S_["k_mem"], 1)

            def root(n, half):
                pool.wait_ge(S_["var"], n)
                nc.gpsimd.tensor_tensor(rstd[:, half, :], rv[:, half, :], minus_half[:, :], ALU.pow
                                        ).then_inc(S_["rstd"], 1)

            for h in HALVES:
                root(h + 1, h)

            for n in range(2 * NG):
                h, g = n % 2, n // 2
                if g == 0:
                    pool.wait_ge(S_["a_cond"], h + 1)
                if g >= 3:
                    pool.wait_ge(S_["b_vr"], n - 5)
                src = cf[:, h][:, g * GB * S:(g + 1) * GB * S].rearrange("p (b s) -> p b s", s=S)
                nc.gpsimd.tensor_copy(z(h, g % 3).rearrange("p (b j s) -> p b j s", b=GB, j=HPQ),
                                      src.unsqueeze(2).to_broadcast([P, GB, HPQ, S])).then_inc(S_["b_rep"], 1)

            def layer(l):
                for h, m, n in ((1, l, 0), (0, l, 1), (0, l + 1, 0), (1, l, 1)):
                    root(norm_count(m, h, n) + 2, h)

            root(norm_count(0, 0, 0) + 2, 0)
            layer(0)
            with pool.Fori(0, LAYERS // 2 - 1) as it:
                layer(it * 2 + 1)
                layer(it * 2 + 2)
            last = LAYERS - 1
            for h, n in ((1, 0), (0, 1), (1, 1)):
                root(norm_count(last, h, n) + 2, h)

        @block.scalar
        def _(act):
            def copy(dst, src, sem):
                nc.scalar.activation(dst, src, ACT.Copy).then_inc(S_[sem], 1)

            def linear(dst, src, bias, scale=1.0):
                return nc.scalar.activation(dst, src, ACT.Identity, bias=bias, scale=scale)

            for h in HALVES:
                act.wait_ge(S_["x_tr"], h + 1)
                copy(xf[:, h], ps[h][:, 3, :], "x_f")
            act.wait_ge(S_["p_cols0"], 1)
            copy(cols0[:, :], ps[0][:, 0, 0:R_END0], "p_cols0c")

            for c in range(LCH):
                m = min(P, LANGS * ADIM - c * P)
                for h in HALVES:
                    act.wait_ge(S_["a_hid"], 2 * c + h + 1)
                    nc.scalar.activation(z(h, c)[0:m, :], ps[h][0:m, c, :], ACT.Relu,
                                         bias=cols0[0:m, R_ADAPT + c:R_ADAPT + c + 1]).then_inc(S_["a_relu"], 1)
            act.wait_ge(S_["p_watt"], 1)
            copy(w_att[:, :, :].rearrange("p a n -> p (a n)"), ps[1][:, 0, :], "p_wattc")
            act.wait_ge(S_["p_rope"], 1)
            copy(rope_bias[:, :], ps[0][:, 1, 0:2], "p_ropec")
            act.wait_ge(S_["p_bat"], 1)
            copy(batch_cols[:, :, :].rearrange("p a b -> p (a b)"), ps[0][:, 2, 0:3 * B], "p_batc")
            act.wait_ge(S_["p_cols"], 1)
            copy(cols[:, :], ps[1][:, 1, 0:P], "p_colsc")

            act.wait_ge(S_["p_keyb"], 1)
            for h in HALVES:
                act.wait_ge(S_["b_qk"], h + 1)
                for q in range(HG):
                    ins = linear(keys_by_quadrant(h)[:, :, q, :], by_batch(ps[h][:, 1, :]), key_bias[:, q:q + 1],
                                 vmask[:, q * HD:q * HD + 1])
                ins.then_inc(S_["b_k"], 1)
            for n in range(2 * NG):
                h, g = n % 2, n // 2
                act.wait_ge(S_["b_sub"], n + 1)
                nc.scalar.activation(z(h, 4 + g), z(h, 4 + g), ACT.Exp).then_inc(S_["b_exp"], 1)
            for h in HALVES:
                act.wait_ge(S_["b_ctx"], h + 1)
                linear(z(h, 0), ps[h][:, 1, :], cols0[:, R_L0V:R_L0V + 1]).then_inc(S_["b_ctxc"], 1)
            for h in HALVES:
                act.wait_ge(S_["b_tr"], h + 1)
                copy(xf[:, h], ps[h][:, 3, :], "b_xf")

            def mixture(r):
                for h in HALVES:
                    act.wait_ge(S_["d_z"], 2 * (2 * r + h) + 1)
                    nc.scalar.activation(logit[:, h], logit[:, h], ACT.Exp).then_inc(S_["d_e"], 1)
                for h in HALVES:
                    act.wait_ge(S_["d_zt"], 2 * r + h + 1)
                    copy(zgt[:, h], ps[h][0:QUAD, 3, :], "d_ztc")

            mixture(0)
            for c in range(FC):
                for h in HALVES:
                    act.wait_ge(S_["d_hid"], 2 * c + h + 1)
                    nc.scalar.activation(z(h, c), ps[h][:, c % 3, :], ACT.Relu).then_inc(S_["d_relu"], 1)
            mixture(1)
            for h in HALVES:
                act.wait_ge(S_["d_tr"], h + 1)
                copy(xf[:, h], ps[h][:, 3, :], "d_xf")

            def experts(k, items, shares):
                for n, (j, e, c, first, last) in enumerate(items):
                    for h in HALVES:
                        if e is None:
                            act.wait_ge(S_[k + "_hid"], 2 * n + h + 1)
                            nc.scalar.activation(z(h, 4 + n % 4), ps[h][:, n % 2, :], ACT.Relu
                                                 ).then_inc(S_[k + "_ra"], 1)
                    if (n + 1 < len(items) and c == 0 and first and j > 0) or n + 1 == len(items):
                        g = j if n + 1 == len(items) else j - 1
                        for h in HALVES:
                            act.wait_ge(S_[k + "_acc"], 2 * g + h + 1)
                            copy(z(h, g), ps[h][:, 2 + g % 2, :], k + "_accc")
                for h in HALVES:
                    act.wait_ge(S_[k + "_g1"], h + 1)
                    nc.scalar.activation(grel[:, h], ps[h][:, 0, 0:HB], ACT.Relu).then_inc(S_[k + "_g1c"], 1)
                for h in HALVES:
                    act.wait_ge(S_[k + "_g2"], 2 * h + 2)
                    nc.scalar.activation(gsm[:, h, 4:5 + shares], ps[h][0:HB, 1, 0:shares + 1], ACT.Exp,
                                         bias=gsm[:, h, 8:9], accum_out=gsm[:, h, 9:10]).then_inc(S_[k + "_ge"], 1)
                for h in HALVES:
                    act.wait_ge(S_[k + "_gb"], h + 1)
                    copy(gcol[:, h, 0:shares + 1, :].rearrange("p a b -> p (a b)"),
                         ps[h][:, 2, 0:(shares + 1) * HB], k + "_gbc")

            act.wait_ge(S_["p_gw"], 1)
            nc.scalar.activation(gvec[:, 1, :], gvec[:, 1, :], ACT.Exp, scale=10.0,
                                 accum_out=gred[:, 1:2]).then_inc(S_["p_gw"], 1)
            act.wait_ge(S_["p_coef"], 1)
            copy(type_coef[:, :, :].rearrange("p e b -> p (e b)"), ps[0][:, 3, 0:L1E * B], "p_coefc")
            experts("e", E_ITEMS, L1S)

            def col(r, s):
                return vl[s][:, r:r + 1]

            def feature_maps(l, h, s):
                nc.scalar.preload_act_table_set("natural_log_exp_and_others")
                for bank, bias, dst, sem in ((2, V_BK, 6, "f_k"), (0, V_BQ, 4, "f_q")):
                    act.wait_ge(S_[sem], l * 2 + (h + 1))
                    nc.scalar.activation(z(h, dst), ps[h][:, bank, :], ACT.Exp, bias=col(bias, s)).then_inc(S_["f_exp"], 1)

            def value_bias(l, h, s):
                act.wait_ge(S_["f_v"], l * 2 + (h + 1))
                linear(z(h, 7), ps[h][:, 1, :], col(V_BV, s)).then_inc(S_["f_vb"], 1)

            def ratio(l, h):
                act.wait_ge(S_["f_den"], l * 2 + (h + 1))
                nc.scalar.activation(z(h, 10), z(h, 10), ACT.Ln, scale=1.0 / EPS_ATTN, bias=1.0
                                     ).then_inc(S_["f_ln"], 1)
                act.wait_ge(S_["f_ln"], l * 2 + (h + 1))
                nc.scalar.activation(z(h, 10), z(h, 10), ACT.Exp, scale=-1.0).then_inc(S_["f_ratio"], 1)

            def gelu_o(l, h):
                act.wait_ge(S_["f_o"], l * 2 + (h + 1))
                nc.scalar.activation(z(h, 4), ps[h][:, 0, :], ACT.Gelu_apprx_tanh).then_inc(S_["f_og"], 1)

            def affine(l, h, s):
                act.wait_ge(S_["f_tr"], norm_count(l, h, 0))
                linear(cf[:, h], ps[h][:, 1, :], col(V_B1, s), col(V_S1, s)).then_inc(S_["f_x"], 1)

            def gelu_h(l, h, s, chunks):
                for c in chunks:
                    act.wait_ge(S_["f_w1"], l * (2 * FC) + (h * FC + c + 1))
                    nc.scalar.activation(z(h, c), ps[h][:, FFN_BANK[c], :], ACT.Gelu_apprx_tanh,
                                         bias=col(V_FF + c, s)).then_inc(S_["f_h"], 1)

            def gelu_f(l, h):
                act.wait_ge(S_["f_w2"], l * 2 + (h + 1))
                nc.scalar.activation(z(h, 5), ps[h][:, 2, :], ACT.Gelu_apprx_tanh).then_inc(S_["f_w2g"], 1)

            def segment(l, a, sa, m, b, sb_):
                if m is not None:
                    affine(m, b, sb_)
                    gelu_h(m, b, sb_, (0, 1))
                if l is not None:
                    feature_maps(l, a, sa)
                    value_bias(l, a, sa)
                    ratio(l, a)
                if m is not None:
                    gelu_h(m, b, sb_, (2,))
                if l is not None:
                    gelu_o(l, a)
                if m is not None:
                    gelu_h(m, b, sb_, (3,))
                    gelu_f(m, b)

            def layer(l, s):
                segment(l, 1, s, l, 0, s)
                segment(l + 1, 0, 1 - s, l, 1, s)

            segment(0, 0, 0, None, None, None)
            layer(0, 0)
            with act.Fori(0, LAYERS // 2 - 1) as it:
                layer(it * 2 + 1, 1)
                layer(it * 2 + 2, 0)
            last = LAYERS - 1
            segment(last, 1, 1, last, 0, 1)
            affine(last, 1, 1)
            gelu_h(last, 1, 1, range(FC))
            gelu_f(last, 1)

            for h in HALVES:
                act.wait_ge(S_["g_tr"], h + 1)
                copy(xf[:, h], ps[h][:, 2, :], "g_xf")
            experts("g", G_ITEMS, L2S)

            act.wait_ge(S_["p_node"], 1)
            copy(node_t[:, :], ps[1][:, 1, 0:TREES * LEAVES], "p_nodec")
            for h in HALVES:
                act.wait_ge(S_["h_st"], h + 1)
                copy(selt[:, h], ps[h][0:TREES * QUAD, 3, :], "h_stc")
            for t in range(TREES):
                for h in HALVES:
                    act.wait_ge(S_["h_lb"], 2 * t + h + 1)
                    copy(z(h, 12 + t), ps[h][:, t, :], "h_lbc")
            for n in range(TREES * LFC):
                t, c = divmod(n, LFC)
                for h in HALVES:
                    act.wait_ge(S_["h_hid"], 2 * n + h + 1)
                    if n >= 3:
                        act.wait_ge(S_["h_mask"], 2 * (n - 3) + h + 1)
                    nc.scalar.activation(z(h, 4 + n % 3), ps[h][:, n % 2, :], ACT.Relu,
                                         bias=cols[:, R_LEAF + n:R_LEAF + n + 1]).then_inc(S_["h_relu"], 1)
                if n % LFC == 1 and t > 0 or n == TREES * LFC - 1:
                    g = t if n == TREES * LFC - 1 else t - 1
                    for h in HALVES:
                        act.wait_ge(S_["h_acc"], 2 * g + h + 1)
                        copy(z(h, g), ps[h][:, 2 + g % 2, :], "h_accc")
            for h in HALVES:
                act.wait_ge(S_["h_sub"], h + 1)
                nc.scalar.activation(z(h, 3)[:, 0:HT // 4], z(h, 3)[:, 0:HT // 4], ACT.Exp,
                                     scale=float(1.0 / np.sqrt(D))).then_inc(S_["h_exp"], 1)

        @block.vector
        def _(dve):
            own = Chain(dve, S_["dve"])
            V = nc.vector

            dve.wait_ge(S_["ld_ids"], 48)
            dve.wait_ge(S_["ld_const"], 16)
            own.step(V.memset(node_rows[:, :], 0.0))
            own.step(V.memset(node_bias[:, :], 0.0))
            own.link(V.tensor_copy(idf[:, :, :], ids[:, :, :]))
            iota = kc[:, K_IOTA:K_IOTA + 1]
            own.link(V.tensor_scalar(lang_hot[:, :], idf[:, 0, :], iota, None, ALU.is_equal))
            V.tensor_scalar(cat_hot[:, :], idf[:, 1, :], iota, None, ALU.is_equal).then_inc(S_["p_hot"], 1)
            V.tensor_scalar(type_hot[:, :], idf[:, 2, :], iota, None, ALU.is_equal).then_inc(S_["p_hot"], 1)
            V.tensor_copy(lang_tok[:, :, :], spread(lang_hot[0:16, :], S)).then_inc(S_["p_hot"], 1)
            for c in range(LCH):
                own.step(V.tensor_scalar(lang_mask[:, c, :], idf[:, 0, :], kc[:, K_LANG + c:K_LANG + c + 1], None,
                                         ALU.is_equal))
            for t in range(TYPES):
                own.step(V.tensor_scalar(type_mask[:, t, :], idf[:, 2, :], float(t), None, ALU.is_equal))
            own.step(V.tensor_copy(leaf_val[:, :], kc[:, K_SLOT:K_SLOT + 1].to_broadcast([P, P])))
            own.sync()

            def add_residual(h, src, res):
                own.step(V.tensor_tensor(yt[:, h].rearrange("p i d -> p (i d)"), src, res, ALU.add))

            def stats(h, eps):
                own.sync()
                for i in range(TILES):
                    own.step(V.bn_stats(stat[:, h, i, :], yt[:, h, i, :]))
                own.sync()
                own.step(V.memset(after_stats[:, :], 0.0))
                for i in range(TILES):
                    own.step(V.bn_aggr(mv[:, h, i, :], stat[:, h, i, :]))
                own.sync()
                V.tensor_scalar(rv[:, h, :], mv[:, h, :, 1], eps, None, ALU.add).then_inc(S_["var"], 1)
                own.step(V.tensor_tensor(yt[:, h], yt[:, h], spread(mv[:, h, :, 0], D), ALU.subtract))

            def normalise(n, h):
                own.sync()
                dve.wait_ge(S_["rstd"], n)
                V.tensor_tensor(xn[:, h], yt[:, h], spread(rstd[:, h, :], D), ALU.mult).then_inc(S_["xn"], 1)

            for c in range(LCH):
                m = min(P, LANGS * ADIM - c * P)
                for h in HALVES:
                    dve.wait_ge(S_["a_relu"], 2 * c + h + 1)
                    mask = spread(lang_mask[0:m, c, h * HB:(h + 1) * HB], S)
                    V.tensor_tensor(by_batch(z(h, c)[0:m, :]), by_batch(z(h, c)[0:m, :]), mask, ALU.mult
                                    ).then_inc(S_["a_mask"], 1)
            dve.wait_ge(S_["ld_rb"], 32)
            for part in range(3):
                V.tensor_copy(row_part(part), row_bias).then_inc(S_["p_rb"], 1)
                if part < 2:
                    dve.wait_ge(S_["p_rb"], 2 * part + 1)
                    V.tensor_tensor(row_bias, row_bias, row_part(part), ALU.subtract).then_inc(S_["p_rb"], 1)
                    dve.wait_ge(S_["p_rb"], 2 * part + 2)
            for h in HALVES:
                dve.wait_ge(S_["a_out"], h + 1)
                add_residual(h, ps[h][:, 3, :], xt[0][:, h].rearrange("p i d -> p (i d)"))
                stats(h, EPS_COND)
            for h in HALVES:
                normalise(h + 1, h)
            dve.wait_ge(S_["p_batc"], 1)
            for h in HALVES:
                dve.wait_ge(S_["a_tr"], h + 1)
                bs = slice(h * HB, (h + 1) * HB)
                own.link(V.tensor_tensor(by_batch(cf[:, h]), by_batch(ps[h][:, 0, :]), spread(gamma_b[:, bs], S), ALU.mult))
                V.tensor_tensor(by_batch(cf[:, h]), by_batch(cf[:, h]), spread(beta_b[:, bs], S), ALU.add
                                ).then_inc(S_["a_cond"], 1)

            dve.wait_ge(S_["ld_rb"], 16 * 5)
            dve.wait_ge(S_["p_ropec"], 1)
            V.tensor_scalar(key_bias[:, :], vmask[:, 0:QUAD:HD], rope_bias[:, 1:2], None, ALU.mult).then_inc(S_["p_keyb"], 1)
            for h in HALVES:
                dve.wait_ge(S_["b_qk"], h + 1)
                qe = z(h, 8, 4).rearrange("p g (b j s) -> p (g b) j s", b=GB, j=HPQ)
                for j in range(HPQ):
                    ins = V.tensor_scalar(qe[:, :, j, :], by_batch(ps[h][:, 0, :]), rope_bias[:, 0:1],
                                          kc[:, K_HEAD + j:K_HEAD + j + 1], ALU.add, ALU.mult)
                    if j < HPQ - 1:
                        own.step(ins)
                ins.then_inc(S_["b_qe"], 1)

            def grouped(ap, n=S):
                return ap.rearrange("p (a s) -> p a s", s=n)

            def values_and_scores(n):
                h, g = n % 2, n // 2
                dve.wait_ge(S_["b_vr"], n + 1)
                V.tensor_tensor(grouped(z(h, 12 + g), P), grouped(ps[h][:, 2, :], P),
                                vmask.unsqueeze(1).to_broadcast([P, GB, P]), ALU.mult).then_inc(S_["b_vx"], 1)
                dve.wait_ge(S_["b_sc"], n + 1)
                sc = ps[h][:, (3, 0)[g % 2], :]
                own.link(V.tensor_reduce(small[:, h, 0:16], grouped(sc), AX_X, ALU.max))
                V.tensor_tensor(grouped(z(h, 4 + g)), grouped(sc), spread(small[:, h, 0:16], S), ALU.subtract
                                ).then_inc(S_["b_sub"], 1)

            def probabilities(n):
                h, g = n % 2, n // 2
                dve.wait_ge(S_["b_exp"], n + 1)
                own.link(V.tensor_reduce(small[:, h, 16:32], grouped(z(h, 4 + g)), AX_X, ALU.add))
                own.link(V.reciprocal(small[:, h, 32:48], small[:, h, 16:32]))
                own.link(V.tensor_tensor(grouped(z(h, 4 + g)), grouped(z(h, 4 + g)), spread(small[:, h, 32:48], S), ALU.mult))
                V.transpose(z(h, 8 + g), z(h, 4 + g)).then_inc(S_["b_pt"], 1)

            for n in range(2 * NG + 1):
                if n < 2 * NG:
                    values_and_scores(n)
                if n >= 1:
                    probabilities(n - 1)

            def residual(h, src, old, new, sem):
                V.tensor_tensor(new[:, h].rearrange("p i d -> p (i d)"), src, old[:, h].rearrange("p i d -> p (i d)"),
                                ALU.add).then_inc(S_[sem], 1)

            for h in HALVES:
                dve.wait_ge(S_["b_out"], h + 1)
                residual(h, ps[h][:, 2, :], xt[0], xt[1], "b_res")

            for h in HALVES:
                dve.wait_ge(S_["c_mm"], h + 1)
                V.tensor_tensor(by_batch(cf[:, h]), by_batch(ps[h][:, 0, :]), spread(cbias_b[:, h * HB:(h + 1) * HB], S),
                                ALU.add).then_inc(S_["c_out"], 1)

            def mixture(r):
                zr = [ps[h][:, (1, 0)[r], :].rearrange("p (i k) -> p i k", i=TILES) for h in HALVES]
                for h in HALVES:
                    dve.wait_ge(S_[("d_r1", "d_r2")[r]], h + 1)
                    own.link(V.tensor_reduce(small[:, h, 0:TILES], zr[h][:, :, MER:MER + ME], AX_X, ALU.max))
                    V.tensor_tensor(logit[:, h], zr[h][:, :, MER:MER + ME], spread(small[:, h, 0:TILES], ME), ALU.subtract
                                    ).then_inc(S_["d_z"], 1)
                    dve.wait_ge(S_["d_e"], 2 * r + h + 1)
                    own.link(V.tensor_reduce(small[:, h, 4:4 + TILES], logit[:, h], AX_X, ALU.add))
                    own.link(V.reciprocal(small[:, h, 8:8 + TILES], small[:, h, 4:4 + TILES]))
                    own.link(V.scalar_tensor_tensor(logit[:, h], logit[:, h], 1.0 / MR,
                                                    spread(small[:, h, 8:8 + TILES], ME), ALU.mult, ALU.mult))
                    if r == 1:
                        dve.wait_ge(S_["d_zt"], h + 1)
                    V.tensor_tensor(zg[:, h, :, 0:MER].rearrange("p i (e r) -> p i e r", e=ME),
                                    zr[h][:, :, 0:MER].rearrange("p i (e r) -> p i e r", e=ME),
                                    spread(logit[:, h], MR), ALU.mult).then_inc(S_["d_z"], 1)

            dve.wait_ge(S_["k_mem"], 7)
            mixture(0)
            mixture(1)
            for h in HALVES:
                dve.wait_ge(S_["d_out"], h + 1)
                residual(h, ps[h][:, 1, :], xt[1], xt[0], "d_res")

            dve.wait_ge(S_["ld_e"], 16 * (5 + L1S + L1E))
            own.link(V.tensor_reduce(gred[:, 0:1], gvec[:, 0, :], AX_X, ALU.max))
            V.tensor_scalar(gvec[:, 1, :], gvec[:, 0, :], gred[:, 0:1], None, ALU.subtract).then_inc(S_["p_gw"], 1)
            dve.wait_ge(S_["p_gw"], 2)
            own.link(V.reciprocal(gred[:, 2:3], gred[:, 1:2]))
            own.link(V.scalar_tensor_tensor(gvec[:, 2, :], gvec[:, 1, :], gred[:, 2:3], kc[0:TYPES, K_BAND:K_BAND + L1E],
                                            ALU.mult, ALU.mult))
            V.tensor_copy(gwide[:, :, :], spread(gvec[:, 2, :], P)).then_inc(S_["p_gw"], 1)

            def experts(k, items, shares, coef):
                kinds = counts_of(items)
                for n, (j, e, c, first, last) in enumerate(items):
                    if e is None:
                        continue
                    for h in HALVES:
                        dve.wait_ge(S_[k + "_hid"], 2 * n + h + 1)
                        V.scalar_tensor_tensor(by_batch(z(h, 4 + n % 4)), by_batch(ps[h][:, n % 2, :]), 0.0,
                                               spread(coef[:, e, h * HB:(h + 1) * HB], S), ALU.max, ALU.mult
                                               ).then_inc(S_[k + "_rd"], 1)
                m = shares + 1
                for h in HALVES:
                    dve.wait_ge(S_[k + "_g2"], 2 * h + 1)
                    V.tensor_reduce(gsm[:, h, 8:9], ps[h][0:HB, 1, 0:m], AX_X, ALU.max, negate=True
                                    ).then_inc(S_[k + "_g2"], 1)
                for h in HALVES:
                    dve.wait_ge(S_[k + "_ge"], h + 1)
                    own.link(V.reciprocal(gsm[:, h, 10:11], gsm[:, h, 9:10]))
                    own.link(V.tensor_scalar(gsm[:, h, 0:m], gsm[:, h, 4:4 + m], gsm[:, h, 10:11], None, ALU.mult))
                    V.tensor_copy(gwb[:, h, 0:m, :], spread(gsm[:, h, 0:m], P)).then_inc(S_[k + "_gw"], 1)
                for h in HALVES:
                    dve.wait_ge(S_[k + "_gbc"], h + 1)
                    for j in range(m):
                        g = shares if j == 0 else j - 1
                        own.step(V.tensor_tensor(by_batch(z(h, g)), by_batch(z(h, g)), spread(gcol[:, h, j, :], S), ALU.mult))
                    own.sync()
                    for j in range(1, m - 1):
                        own.link(V.tensor_tensor(z(h, 0), z(h, 0), z(h, j), ALU.add))
                    V.tensor_tensor(cf[:, h], z(h, 0), z(h, m - 1), ALU.add).then_inc(S_[k + "_out"], 1)

            dve.wait_ge(S_["p_coefc"], 1)
            experts("e", E_ITEMS, L1S, type_coef)

            def col(r, s):
                return vl[s][:, r:r + 1]

            def keys(l, h, s):
                ksum, kv = small[:, h, 0:HB], small[:, h, HB:2 * HB]
                dve.wait_ge(S_["f_exp"], l * 4 + (2 * h + 1))
                own.link(V.tensor_scalar(z(h, 6), z(h, 6), 1.0, 1.0, ALU.min, ALU.subtract))
                k_done = own.mark(V.scalar_tensor_tensor(z(h, 8), ps[h][:, 2, :], col(V_BK, s), z(h, 6), ALU.add, ALU.max))
                dve.wait_ge(S_["f_exp"], l * 4 + (2 * h + 2))
                q_less = own.mark(V.tensor_scalar(z(h, 4), z(h, 4), 1.0, 1.0, ALU.min, ALU.subtract))
                own.after(k_done)
                sums = own.mark(V.tensor_reduce(small2[:, h, 0:HB], by_batch(z(h, 8)), AX_X, ALU.add))
                own.after(q_less)
                own.step(V.scalar_tensor_tensor(z(h, 11), ps[h][:, 0, :], col(V_BQ, s), z(h, 4), ALU.add, ALU.max))
                own.after(sums)
                own.link(V.tensor_scalar(ksum, small2[:, h, 0:HB], float(S), None, ALU.add))
                V.scalar_tensor_tensor(by_batch(z(h, 10)), by_batch(z(h, 11)), 1.0, spread(ksum, S), ALU.add, ALU.mult
                                       ).then_inc(S_["f_den"], 1)
                dve.wait_ge(S_["f_vb"], l * 2 + (h + 1))
                products = own.mark(V.scalar_tensor_tensor(z(h, 9), z(h, 8), 1.0, z(h, 7), ALU.add, ALU.mult))
                own.step(V.reciprocal(small2[:, h, HB:2 * HB], ksum))
                own.after(products)
                own.link(V.tensor_reduce(kv, by_batch(z(h, 9)), AX_X, ALU.add))
                own.link(V.scalar_tensor_tensor(small2[:, h, 2 * HB:3 * HB], small2[:, h, HB:2 * HB], -1.0, kv,
                                                ALU.mult, ALU.mult))

            def values(l, h):
                dve.wait_ge(S_["f_ratio"], l * 2 + (h + 1))
                V.scalar_tensor_tensor(by_batch(z(h, 12)), by_batch(z(h, 10)), 1.0, spread(small2[:, h, 2 * HB:3 * HB], S),
                                       ALU.subtract, ALU.mult).then_inc(S_["f_u"], 1)

            def affine(l, h, s):
                dve.wait_ge(S_["f_tr"], norm_count(l, h, 1))
                V.tensor_scalar(cf[:, h], ps[h][:, 1, :], col(V_S2, s), col(V_B2, s), ALU.mult, ALU.add
                                ).then_inc(S_["f_y"], 1)

            def norm_sum(l, h, n):
                dve.wait_ge(S_["f_ft"], back_count(l, h, n))
                dve.wait_ge(S_[("f_og", "f_w2g")[n]], l * 2 + (h + 1))
                add_residual(h, ps[h][:, 3, :], z(h, 4 + n))

            def norm_scale(l, h, n):
                normalise(norm_count(l, h, n) + 2, h)

            def segment(l, a, sa, m, b, sb_):
                keys(l, a, sa)
                values(l, a)
                norm_sum(l, a, 0)
                stats(a, EPS_LN)
                if m is not None:
                    norm_sum(m, b, 1)
                norm_scale(l, a, 0)
                if m is not None:
                    stats(b, EPS_LN)
                    norm_scale(m, b, 1)
                    affine(m, b, sb_)

            def layer(l, s):
                segment(l, 1, s, l, 0, s)
                segment(l + 1, 0, 1 - s, l, 1, s)

            segment(0, 0, 0, None, None, None)
            lead = own.n
            layer(0, 0)
            per = own.n - lead
            with dve.Fori(0, LAYERS // 2 - 1) as it:
                own.base, own.n = it * (2 * per) + (lead + per), 0
                layer(it * 2 + 1, 1)
                layer(it * 2 + 2, 0)
                assert own.n == 2 * per, (own.n, per)
            own.base, own.n = None, lead + (LAYERS - 1) * per
            last = LAYERS - 1
            segment(last, 1, 1, last, 0, 1)
            norm_sum(last, 1, 1)
            stats(1, EPS_LN)
            norm_scale(last, 1, 1)
            affine(last, 1, 1)

            for h in HALVES:
                dve.wait_ge(S_["f_ft"], norm_count(last, h, 1) + 2)
                residual(h, ps[h][:, 3, :], xt[0], xt[1], "g_res")

            experts("g", G_ITEMS, L2S, type_mask)

            own.step(V.memset(sel[:, :, :, :, :], 0.0))
            for h in HALVES:
                dve.wait_ge(S_["h_sc"], h + 1)
                sc = ps[h][:, 0, 0:TILES * 64].rearrange("p (i k) -> p i k", i=TILES)[:, :, 0:TREES * LEAVES]
                d = dec[:, h]
                own.link(V.tensor_scalar(d.rearrange("p (i t) k -> p i (t k)", i=TILES), sc, 0.0, None, ALU.is_ge))
                r = reach[:, h]
                own.step(V.tensor_copy(r[:, :, 1], d[:, :, 0]))
                own.link(V.tensor_scalar(r[:, :, 0], d[:, :, 0], -1.0, 1.0, ALU.mult, ALU.add))
                at, new, first = 0, 2, 1
                while first < NODES:
                    k = first + 1
                    src = r[:, :, at:at + k]
                    if 2 * k == LEAVES:
                        dst = sel[:, h].rearrange("p i t k -> p (i t) k")[:, :, 0:LEAVES]
                    else:
                        dst = r[:, :, new:new + 2 * k]
                    pair = dst.rearrange("p n (k two) -> p n k two", two=2)
                    own.link(V.tensor_tensor(pair[:, :, :, 1], src, d[:, :, first:first + k], ALU.mult))
                    ins = V.tensor_tensor(pair[:, :, :, 0], src, pair[:, :, :, 1], ALU.subtract)
                    if 2 * k == LEAVES:
                        ins.then_inc(S_["h_sel"], 1)
                    else:
                        own.link(ins)
                    at, new, first = new, new + 2 * k, first + k
            for h in HALVES:
                dve.wait_ge(S_["h_stc"], h + 1)
                V.tensor_copy(selb[:, h], selt[:, h]).then_inc(S_["h_stb"], 1)
            for n in range(TREES * LFC):
                t, c = divmod(n, LFC)
                for h in HALVES:
                    dve.wait_ge(S_["h_lbc"], 2 * t + h + 1)
                    dve.wait_ge(S_["h_relu"], 2 * n + h + 1)
                    V.scalar_tensor_tensor(z(h, 8 + n % 3), z(h, 12 + t), kc[:, K_LEAF + c:K_LEAF + c + 1], z(h, 4 + n % 3),
                                           ALU.is_equal, ALU.mult).then_inc(S_["h_mask"], 1)
            for h in HALVES:
                own.step(V.memset(z(h, 12), 0.0))
            for h in HALVES:
                dve.wait_ge(S_["h_s"], h + 1)
                sc = grouped(ps[h][:, 0, 0:TILES * S])
                own.link(V.tensor_reduce(small[:, h, 0:TILES], sc, AX_X, ALU.max))
                V.tensor_tensor(grouped(z(h, 3)[:, 0:TILES * S]), sc, spread(small[:, h, 0:TILES], S), ALU.subtract
                                ).then_inc(S_["h_sub"], 1)
            for h in HALVES:
                dve.wait_ge(S_["h_exp"], h + 1)
                e = grouped(z(h, 3)[:, 0:TILES * S])
                own.link(V.tensor_reduce(small[:, h, 4:4 + TILES], e, AX_X, ALU.add))
                own.link(V.reciprocal(small[:, h, 8:8 + TILES], small[:, h, 4:4 + TILES]))
                own.link(V.tensor_tensor(e, e, spread(small[:, h, 8:8 + TILES], S), ALU.mult))
                for q in range(P // QUAD):
                    rows_q = slice(q * QUAD, (q + 1) * QUAD)
                    pt = z(h, 12).rearrange("p (i n) -> p i n", i=TILES)
                    ins = V.transpose(pt[rows_q, :, rows_q], e[rows_q])
                    if q < P // QUAD - 1:
                        own.step(ins)
                ins.then_inc(S_["h_pt"], 1)
            for h in HALVES:
                dve.wait_ge(S_["h_o"], h + 1)
                residual(h, ps[h][:, 1, :], xt[1], yt, "h_fin")

        @block.tensor
        def _(pe):
            T = nc.tensor

            def turn(dst, srcs, sem, n=P, m=P):
                for i, s in enumerate(srcs):
                    ins = T.transpose(dst[:, i * P:(i + 1) * P], s, ident)
                ins.then_inc(S_[sem], 1)

            def keep_warm(n, bank):
                for _ in range(n):
                    T.matmul(bank, filler[:, :].to_broadcast([P, P]), filler[:, :].to_broadcast([P, HT]), start=True, stop=True)

            pe.wait_ge(S_["p_fill"], 1)
            keep_warm(WARM[0], ps[0][:, 1, :])
            pe.wait_ge(S_["ld_const"], 16)
            pe.wait_ge(S_["ld_x"], 16)
            for h in HALVES:
                turn(ps[h][:, 3, :], [xt[0][:, h, i, :] for i in range(TILES)], "x_tr")
            pe.wait_ge(S_["ld_rows0"], 16 * 5)
            T.transpose(ps[0][:, 0, 0:R_END0], rows0[:, :], ident[0:R_END0, 0:R_END0]).then_inc(S_["p_cols0"], 1)
            pe.wait_ge(S_["p_cols0c"], 1)

            pe.wait_ge(S_["ld_a1"], 16)
            for c in range(LCH):
                m = min(P, LANGS * ADIM - c * P)
                for h in HALVES:
                    if c == 0:
                        pe.wait_ge(S_["x_f"], h + 1)
                    T.matmul(ps[h][0:m, c, :], w1a[:, c * P:c * P + m], xf[:, h], start=True, stop=True
                             ).then_inc(S_["a_hid"], 1)

            pe.wait_ge(S_["a_relu"], 2)
            pe.wait_ge(S_["ld_b"], 16 * 5)
            for n, turned in enumerate((rope_q, rope_k, ident, ident)):
                ins = T.matmul(ps[1][:, 0, n * D:(n + 1) * D], w_nat[:, n, :], turned, start=True, stop=True)
            ins.then_inc(S_["p_watt"], 1)
            pe.wait_ge(S_["a_relu"], 3)
            T.matmul(ps[0][:, 1, 0:1], rope_q, cols0[:, R_L0Q:R_L0Q + 1], start=True, stop=True)
            T.matmul(ps[0][:, 1, 1:2], rope_k, cols0[:, R_L0K:R_L0K + 1], start=True, stop=True).then_inc(S_["p_rope"], 1)
            pe.wait_ge(S_["p_hot"], 3)
            pe.wait_ge(S_["ld_a"], 16 * 5)
            pe.wait_ge(S_["ld_c"], 16)
            pe.wait_ge(S_["a_relu"], 5)
            T.matmul(ps[0][:, 2, 0:B], lang_rows[:, 1, :], lang_hot[0:LANGS, :], start=True, stop=True)
            T.matmul(ps[0][:, 2, B:2 * B], lang_rows[:, 2, :], lang_hot[0:LANGS, :], start=True, stop=True)
            T.matmul(ps[0][:, 2, 2 * B:3 * B], cat_bias[:, :], cat_hot[0:CATS, :], start=True, stop=True
                     ).then_inc(S_["p_bat"], 1)
            for h in HALVES:
                pe.wait_ge(S_["a_mask"], 2 * (LCH - 1) + h + 1)
                for i in range(TILES):
                    dst = ps[h][:, 3, tok(h, i)]
                    for c in range(LCH):
                        m = min(P, LANGS * ADIM - c * P)
                        T.matmul(dst, z(h, c)[0:m, tok(h, i)], w2a[0:m, c, :], start=(c == 0), stop=False)
                    b0 = h * HB + i * (P // S)
                    ins = T.matmul(dst, lang_tok[0:LANGS, b0:b0 + P // S, :].rearrange("p b s -> p (b s)"),
                                   lang_rows[:, 0, :], start=False, stop=True)
                ins.then_inc(S_["a_out"], 1)
            pe.wait_ge(S_["ld_rows"], 16 * (LV + TREES))
            turn(ps[1][:, 1, :], [rows[:, :]], "p_cols")
            pe.wait_ge(S_["p_colsc"], 1)
            keep_warm(WARM[1], ps[0][:, 1, :])
            for h in HALVES:
                pe.wait_ge(S_["xn"], h + 1)
                turn(ps[h][:, 0, :], [xn[:, h, i, :] for i in range(TILES)], "a_tr")

            for h in HALVES:
                pe.wait_ge(S_["a_cond"], h + 1)
                T.matmul(ps[h][:, 1, :], w_att[:, 1, :], cf[:, h], start=True, stop=True)
                T.matmul(ps[h][:, 0, :], w_att[:, 0, :], cf[:, h], start=True, stop=True).then_inc(S_["b_qk"], 1)

            def batch(ap, b):
                return ap[:, b * S:(b + 1) * S]

            def values_and_scores(n):
                h, g = n % 2, n // 2
                pe.wait_ge(S_["b_rep"], n + 1)
                if n >= 2:
                    pe.wait_ge(S_["b_vx"], n - 1)
                for b in range(GB):
                    ins = T.matmul(ps[h][:, 2, b * D:(b + 1) * D], z(h, g % 3)[:, b * P:(b + 1) * P], w_att[:, 2, :],
                                   start=True, stop=True)
                ins.then_inc(S_["b_vr"], 1)
                if g == 0:
                    pe.wait_ge(S_["b_k"], h + 1)
                    pe.wait_ge(S_["b_qe"], h + 1)
                if n >= 4:
                    pe.wait_ge(S_["b_sub"], n - 3)
                for b in range(GB):
                    r = slice(b * P, (b + 1) * P)
                    ins = T.matmul(ps[h][:, (3, 0)[g % 2], r], z(h, 8 + g)[:, r], z(h, 4 + g)[:, r], start=True, stop=True)
                ins.then_inc(S_["b_sc"], 1)

            def context(n):
                h, g = n % 2, n // 2
                pe.wait_ge(S_["b_pt"], n + 1)
                for b in range(GB):
                    for q in range(HG):
                        r = slice(q * QUAD, (q + 1) * QUAD)
                        at = (b * HG + q) * S
                        col = (g * GB + b) * S
                        ins = T.matmul(ps[h][r, 1, col:col + S], z(h, 12 + g)[:, b * D + q * QUAD:b * D + (q + 1) * QUAD],
                                       z(h, 8 + g)[:, at:at + S], start=True, stop=True, tile_position=(0, q * QUAD))
                if g == NG - 1:
                    ins.then_inc(S_["b_ctx"], 1)

            for n in range(2 * NG + 2):
                if n < 2 * NG:
                    values_and_scores(n)
                if n >= 2:
                    if n >= 2 * NG:
                        keep_warm(WARM[2], ps[0][:, 0, :])
                    context(n - 2)
            for h in HALVES:
                pe.wait_ge(S_["b_ctxc"], h + 1)
                for i in range(TILES):
                    dst = ps[h][:, 2, tok(h, i)]
                    T.matmul(dst, z(h, 0)[:, tok(h, i)], w_att[:, 3, :], start=True, stop=False)
                    ins = T.matmul(dst, ones[:, :], token_bias[:, :], start=False, stop=True)
                ins.then_inc(S_["b_out"], 1)
            for h in HALVES:
                pe.wait_ge(S_["b_res"], h + 1)
                turn(ps[h][:, 3, :], [xt[1][:, h, i, :] for i in range(TILES)], "b_tr")

            pe.wait_ge(S_["ld_cat"], 16 * B)
            keep_warm(WARM[3], ps[0][:, 1, :])
            for h in HALVES:
                pe.wait_ge(S_["b_xf"], h + 1)
                for b in range(HB):
                    ins = T.matmul(batch(ps[h][:, 0, :], b), w_cat[:, h * HB + b, :], batch(xf[:, h], b),
                                   start=True, stop=True)
                ins.then_inc(S_["c_mm"], 1)

            pe.wait_ge(S_["ld_d"], 16 * (2 * ME + 8))
            for h in HALVES:
                pe.wait_ge(S_["c_out"], h + 1)
                for i in range(TILES):
                    ins = T.matmul(ps[h][:, 1, i * P:i * P + MER + ME], cf[:, h][:, tok(h, i)], ar1[:, :], start=True, stop=True)
                ins.then_inc(S_["d_r1"], 1)

            def turn_parts(r):
                for h in HALVES:
                    pe.wait_ge(S_["d_z"], 2 * (2 * r + h) + 2)
                    turn(ps[h][0:QUAD, 3, :], [zg[:, h, i, :] for i in range(TILES)], "d_zt")

            turn_parts(0)
            for c in range(FC):
                for h in HALVES:
                    if c == 0:
                        pe.wait_ge(S_["d_ztc"], h + 1)
                    if c >= 3:
                        pe.wait_ge(S_["d_relu"], 2 * (c - 3) + h + 1)
                    dst = ps[h][:, c % 3, :]
                    T.matmul(dst, w1f[:, c * P:(c + 1) * P], cf[:, h], start=True, stop=False)
                    T.matmul(dst, b1aug[:, c * P:(c + 1) * P], zgt[0:MER + 1, h], start=False, stop=True
                             ).then_inc(S_["d_hid"], 1)
            for h in HALVES:
                pe.wait_ge(S_["d_relu"], 2 * (FC - 1) + h + 1)
                for i in range(TILES):
                    for c in range(FC):
                        ins = T.matmul(ps[h][:, 0, i * P:i * P + MER + ME], z(h, c)[:, tok(h, i)], ar2[:, c, :],
                                       start=(c == 0), stop=(c == FC - 1))
                ins.then_inc(S_["d_r2"], 1)
            turn_parts(1)
            for h in HALVES:
                pe.wait_ge(S_["d_ztc"], 2 + h + 1)
                for i in range(TILES):
                    dst = ps[h][:, 1, tok(h, i)]
                    for c in range(FC):
                        T.matmul(dst, z(h, c)[:, tok(h, i)], w2f[:, c, :], start=(c == 0), stop=False)
                    ins = T.matmul(dst, zgt[0:MER + 1, h, tok(h, i)], b2aug[:, :], start=False, stop=True)
                ins.then_inc(S_["d_out"], 1)
            for h in HALVES:
                pe.wait_ge(S_["d_res"], h + 1)
                turn(ps[h][:, 3, :], [xt[0][:, h, i, :] for i in range(TILES)], "d_tr")

            def experts(k, items, shares, xin, g1, g2):
                kinds = counts_of(items)

                def hidden(n):
                    j, e, c, first, last = items[n]
                    slot = j if e is None else shares + e
                    for h in HALVES:
                        if n == 0:
                            pe.wait_ge(S_[xin], h + 1)
                        if n >= 2:
                            kind, at = kinds[n - 2]
                            pe.wait_ge(S_[k + ("_ra", "_rd")[kind]], 2 * at + h + 1)
                        T.matmul(ps[h][:, n % 2, :], arena[:, slot, 0, c * P:(c + 1) * P], xf[:, h], start=True, stop=True
                                 ).then_inc(S_[k + "_hid"], 1)

                def output(n):
                    j, e, c, first, last = items[n]
                    slot = j if e is None else shares + e
                    kind, at = kinds[n]
                    for h in HALVES:
                        pe.wait_ge(S_[k + ("_ra", "_rd")[kind]], 2 * at + h + 1)
                        if first and j >= 2:
                            pe.wait_ge(S_[k + "_accc"], 2 * (j - 2) + h + 1)
                        ins = T.matmul(ps[h][:, 2 + j % 2, :], arena[:, slot, 1, c * P:(c + 1) * P], z(h, 4 + n % 4),
                                       start=first, stop=last)
                        if last:
                            ins.then_inc(S_[k + "_acc"], 1)

                for n in range(len(items) + 1):
                    if n < len(items):
                        hidden(n)
                    if n >= 1:
                        output(n - 1)
                for h in HALVES:
                    pe.wait_ge(S_[k + "_accc"], 2 * shares + h + 1)
                    for j in range(shares + 1):
                        g = shares if j == 0 else j - 1
                        ins = T.matmul(ps[h][:, 0, 0:HB], g1[:, j, :], by_batch(z(h, g))[:, :, 0],
                                       start=(j == 0), stop=(j == shares))
                    ins.then_inc(S_[k + "_g1"], 1)
                for h in HALVES:
                    pe.wait_ge(S_[k + "_g1c"], h + 1)
                    if h == 1:
                        pe.wait_ge(S_[k + "_g2"], 2)
                    T.matmul(ps[h][0:HB, 1, 0:shares + 1], grel[:, h], g2[:, :], start=True, stop=True
                             ).then_inc(S_[k + "_g2"], 1)
                for h in HALVES:
                    pe.wait_ge(S_[k + "_gw"], h + 1)
                    for j in range(shares + 1):
                        ins = T.matmul(ps[h][:, 2, j * HB:(j + 1) * HB], gwb[:, h, j, :], ident[0:HB, 0:HB],
                                       start=True, stop=True)
                    ins.then_inc(S_[k + "_gb"], 1)

            pe.wait_ge(S_["p_gw"], 3)
            pe.wait_ge(S_["d_xf"], 1)
            for e in range(L1E):
                ins = T.matmul(ps[0][:, 3, e * B:(e + 1) * B], gwide[:, e, :], type_hot[0:TYPES, :], start=True, stop=True)
            ins.then_inc(S_["p_coef"], 1)
            pe.wait_ge(S_["p_coefc"], 1)
            pe.wait_ge(S_["ld_e"], 16 * (5 + L1S + L1E))
            experts("e", E_ITEMS, L1S, "d_xf", gate1, gate2)

            for h in HALVES:
                pe.wait_ge(S_["e_out"], h + 1)
                turn(ps[h][:, 3, :], [cf[:, h][:, tok(h, i)] for i in range(TILES)], "f_ft")

            def project(l, h, s, n):
                T.matmul(ps[h][:, (0, 2, 1)[n], :], wl[s][:, n * D:(n + 1) * D], cf[:, h], start=True, stop=True
                         ).then_inc(S_[("f_q", "f_k", "f_v")[n]], 1)

            def bias_rows(h, bank, n, s):
                T.matmul(ps[h][:, bank, :], ones3[:, :], rl[s][:, n:n + 1, :].to_broadcast([3, TILES, D]),
                         start=True, stop=False)

            def attn_out(l, h, s):
                pe.wait_ge(S_["f_den"], l * 2 + (h + 1))
                bias_rows(h, 0, 0, s)
                pe.wait_ge(S_["f_u"], l * 2 + (h + 1))
                for i in range(TILES):
                    ins = T.matmul(ps[h][:, 0, tok(h, i)], z(h, 12)[:, tok(h, i)], wl[s][:, 3 * D:4 * D], start=False,
                                   stop=(i == TILES - 1))
                ins.then_inc(S_["f_o"], 1)

            def turns(l, h, n):
                pe.wait_ge(S_["xn"], norm_count(l, h, n) + 2)
                turn(ps[h][:, 1, :], [xn[:, h, i, :] for i in range(TILES)], "f_tr")

            def scaled(l, h, n):
                pe.wait_ge(S_[("f_x", "f_y")[n]], l * 2 + (h + 1))

            def turns_back(l, h, n):
                scaled(l, h, n)
                turn(ps[h][:, 3, :], [cf[:, h][:, tok(h, i)] for i in range(TILES)], "f_ft")

            def ffn_in(l, h, s, chunks):
                for c in chunks:
                    if c == 3:
                        pe.wait_ge(S_["f_h"], l * (2 * FC) + (h * FC + 1))
                    T.matmul(ps[h][:, FFN_BANK[c], :], wl[s][:, 4 * D + c * P:4 * D + (c + 1) * P], cf[:, h],
                             start=True, stop=True).then_inc(S_["f_w1"], 1)

            def ffn_out(l, h, s, chunks):
                if 0 in chunks:
                    pe.wait_ge(S_["f_h"], l * (2 * FC) + (h * FC + 2))
                    bias_rows(h, 2, 1, s)
                for c in chunks:
                    if c >= 2:
                        pe.wait_ge(S_["f_h"], l * (2 * FC) + (h * FC + c + 1))
                    for i in range(TILES):
                        ins = T.matmul(ps[h][:, 2, tok(h, i)], z(h, c)[:, tok(h, i)],
                                       wl[s][:, 4 * D + FF + c * D:4 * D + FF + (c + 1) * D], start=False,
                                       stop=(c == FC - 1 and i == TILES - 1))
                if FC - 1 in chunks:
                    ins.then_inc(S_["f_w2"], 1)

            def arrived(s, k):
                pe.wait_ge(S_[f"ld_f{s}"], k)

            def segment(l, a, sa, m, b, sb_):
                if m is not None:
                    turns(m, b, 0)
                    keep_warm(WARM[6], ps[b][:, 0, :])
                    scaled(m, b, 0)
                    ffn_in(m, b, sb_, (0, 1))
                if l is not None:
                    if not (isinstance(l, int) and l == 0):
                        turns(l - 1, a, 1)
                        keep_warm(WARM[6], ps[a][:, 0, :])
                        scaled(l - 1, a, 1)
                    project(l, a, sa, 1)
                    project(l, a, sa, 0)
                    project(l, a, sa, 2)
                if m is not None:
                    ffn_in(m, b, sb_, (2, 3))
                    turns_back(m, b, 0)
                if l is not None:
                    if not (isinstance(l, int) and l == 0):
                        turns_back(l - 1, a, 1)
                if m is not None:
                    ffn_out(m, b, sb_, (0, 1))
                if l is not None:
                    attn_out(l, a, sa)
                if m is not None:
                    ffn_out(m, b, sb_, (2, 3))
                    keep_warm(WARM[5], ps[b][:, 0, :])

            def layer(l, s, next_loaded):
                segment(l, 1, s, l, 0, s)
                arrived(1 - s, next_loaded)
                segment(l + 1, 0, 1 - s, l, 1, s)

            loaded = 16 * 9
            arrived(0, loaded)
            segment(0, 0, 0, None, None, None)
            layer(0, 0, loaded)
            with pe.Fori(0, LAYERS // 2 - 1) as it:
                layer(it * 2 + 1, 1, it * loaded + 2 * loaded)
                layer(it * 2 + 2, 0, it * loaded + 2 * loaded)
            last = LAYERS - 1
            segment(last, 1, 1, last, 0, 1)
            turns(last, 1, 0)
            scaled(last, 1, 0)
            ffn_in(last, 1, 1, (0, 1))
            turns(last, 0, 1)
            ffn_in(last, 1, 1, (2, 3))
            turns_back(last, 1, 0)
            turns_back(last, 0, 1)
            ffn_out(last, 1, 1, (0, 1, 2, 3))
            turns(last, 1, 1)
            turns_back(last, 1, 1)

            for h in HALVES:
                pe.wait_ge(S_["g_res"], h + 1)
                turn(ps[h][:, 2, :], [xt[1][:, h, i, :] for i in range(TILES)], "g_tr")

            pe.wait_ge(S_["ld_g"], 16 * (4 + L2S + TYPES))
            experts("g", G_ITEMS, L2S, "g_xf", gate1b, gate2b)

            pe.wait_ge(S_["ld_h"], 16 * 15)
            pe.wait_ge(S_["g_gbc"], 2)
            T.transpose(ps[1][:, 1, 0:TREES * LEAVES], node_rows[:, :], ident[0:TREES * LEAVES, 0:TREES * LEAVES]
                        ).then_inc(S_["p_node"], 1)
            pe.wait_ge(S_["p_nodec"], 1)
            for h in HALVES:
                pe.wait_ge(S_["g_out"], h + 1)
                for i in range(TILES):
                    dst = ps[h][:, 0, i * 64:i * 64 + TREES * LEAVES]
                    T.matmul(dst, cf[:, h][:, tok(h, i)], node_t[:, :], start=True, stop=False)
                    ins = T.matmul(dst, ones[:, :], node_bias[:, :], start=False, stop=True)
                ins.then_inc(S_["h_sc"], 1)
            for h in HALVES:
                pe.wait_ge(S_["h_sel"], h + 1)
                turn(ps[h][0:TREES * QUAD, 3, :],
                     [sel[:, h, i].rearrange("p t k -> p (t k)") for i in range(TILES)], "h_st")
            for t in range(TREES):
                r = slice(t * QUAD, t * QUAD + LEAVES)
                for h in HALVES:
                    pe.wait_ge(S_["h_stb"], h + 1)
                    T.matmul(ps[h][:, t, :], leaf_val[r, :], selb[r, h], start=True, stop=True).then_inc(S_["h_lb"], 1)

            def leaf_hidden(n):
                t, c = divmod(n, LFC)
                for h in HALVES:
                    if n < 2:
                        pe.wait_ge(S_["h_lbc"], 2 * TREES - 1 + h)
                    else:
                        pe.wait_ge(S_["h_relu"], 2 * (n - 2) + h + 1)
                    T.matmul(ps[h][:, n % 2, :], w_tree(t)[:, 0, c, :], cf[:, h], start=True, stop=True
                             ).then_inc(S_["h_hid"], 1)

            def leaf_output(n):
                t, c = divmod(n, LFC)
                r = slice(t * QUAD, t * QUAD + LEAVES)
                for h in HALVES:
                    bank = ps[h][:, 2 + t % 2, :]
                    if c == 0:
                        pe.wait_ge(S_["h_stc"], h + 1)
                        if t == 2:
                            pe.wait_ge(S_["h_accc"], h + 1)
                    pe.wait_ge(S_["h_mask"], 2 * n + h + 1)
                    hm = z(h, 8 + n % 3)
                    if t < 2:
                        ins = T.matmul(bank, w_tree(t)[:, 1, c, :], hm, start=(c == 0), stop=False)
                        if c == LFC - 1:
                            ins = T.matmul(bank, leaf_b2[r, :], selt[r, h], start=False, stop=True)
                    else:
                        for i in range(TILES):
                            ins = T.matmul(bank[:, tok(h, i)], hm[:, tok(h, i)], w_tree(t)[:, 1, c, :],
                                           start=(c == 0 and i == 0), stop=False, skip_group_check=True)
                        if c == LFC - 1:
                            for i in range(TILES):
                                ins = T.matmul(bank[:, tok(h, i)], selt[r, h, tok(h, i)], leaf_b2[r, :],
                                               start=False, stop=(i == TILES - 1), skip_group_check=True)
                    if c == LFC - 1:
                        ins.then_inc(S_["h_acc"], 1)

            for n in range(TREES * LFC + 1):
                if n < TREES * LFC:
                    leaf_hidden(n)
                if n >= 1:
                    leaf_output(n - 1)
            for h in HALVES:
                pe.wait_ge(S_["h_accc"], 2 + h + 1)
                for b in range(HB):
                    i, q = divmod(b, P // S)
                    r = slice(q * QUAD, (q + 1) * QUAD)
                    ins = T.matmul(ps[h][r, 0, i * S:(i + 1) * S], batch(z(h, 0), b), batch(z(h, 1), b),
                                   start=True, stop=True, tile_position=(0, q * QUAD))
                ins.then_inc(S_["h_s"], 1)
            for h in HALVES:
                pe.wait_ge(S_["h_pt"], h + 1)
                pe.wait_ge(S_["h_accc"], 4 + h + 1)
                for i in range(TILES):
                    ins = T.matmul(ps[h][:, 1, tok(h, i)], z(h, 12)[:, tok(h, i)], z(h, 2)[:, tok(h, i)],
                                   start=True, stop=True)
                ins.then_inc(S_["h_o"], 1)


def kernel(**inputs):
    import concourse.bacc as _bacc
    from concourse.bass_utils import run_bass_kernel_spmd as _run

    nc = _bacc.Bacc("TRN2", target_bir_lowering=False, num_devices=1)
    arrays, aps = {}, {}
    for name, value in inputs.items():
        a = np.ascontiguousarray(value)
        arrays[f"in_{name}"] = a
        aps[name] = nc.dram_tensor(f"in_{name}", a.shape, mybir.dt.from_np(a.dtype), kind="ExternalInput").ap()
    k = shape_constants()
    arrays["shape_constants"] = k
    konst = nc.dram_tensor("shape_constants", k.shape, F32, kind="ExternalInput").ap()
    out = nc.dram_tensor("out", (B, S, D), F32, kind="ExternalOutput").ap()
    network(nc, aps, konst, out)
    r = _run(nc, [arrays], core_ids=[0])
    return r.results[0]["out"]
```

```python
from contextlib import ExitStack

import numpy as np

import concourse.bass as bass
from concourse import mybir

F32 = mybir.dt.float32
BF16 = mybir.dt.bfloat16
F32R = mybir.dt.float32r
I32 = mybir.dt.int32
ALU = mybir.AluOpType
ACT = mybir.ActivationFunctionType
AX_X = mybir.AxisListType.X

P = 128
B, S, D = 32, 32, 128
HALVES = (0, 1)
HB = B // 2
HT = HB * S
TILES = HT // P
BANKS = 4

LANGS, ADIM = 10, 32
LCH = -(-LANGS * ADIM // P)
HEADS, HD = 16, 8
QUAD = 32
HPQ = QUAD // HD
HG = HEADS // HPQ
GB = 4
NG = HB // GB
CATS = 64
FF = 512
FC = FF // P
ME, MR = 3, 8
MER = ME * MR
L1E, L1S = 4, 3
TYPES = 3
L2S = 2
LAYERS = 8
TREES, LEAVES, LEAFW = 3, 16, 64
NODES = LEAVES - 1
LFC = LEAVES * LEAFW // P

EPS_COND = 1e-5
EPS_ATTN = 1e-6
EPS_LN = 1e-6

LV = 7 + FC
V_BQ, V_BK, V_BV, V_S1, V_B1, V_S2, V_B2, V_FF = range(8)
R_LEAF = LV * LAYERS
R_ADAPT = 0
R_L0Q, R_L0K, R_L0V = LCH, LCH + 1, LCH + 2
R_END0 = R_L0V + 1


CROSS = ((0, 0), (0, 1), (1, 0))

FFN_BANK = (0, 2, 1, 0)

K_IOTA, K_LANG, K_HEAD, K_LEAF, K_SLOT, K_BAND = 0, 1, 4, 8, 16, 18
K_IDENT, K_ROPEQ, K_ROPEK, K_VMASK = 32, 32 + P, 32 + 2 * P, 32 + 3 * P
K_END = 32 + 4 * P


def shape_constants():
    k = np.zeros((P, K_END), np.float32)
    p = np.arange(P)
    k[:, K_IOTA] = p
    for c in range(LCH):
        k[:, K_LANG + c] = c * (P // ADIM) + p // ADIM
    for j in range(HPQ):
        k[:, K_HEAD + j] = (p % QUAD) // HD == j
    for c in range(LFC):
        k[:, K_LEAF + c] = c * (P // LEAFW) + p // LEAFW
    k[:, K_SLOT] = p % QUAD
    for t in range(TYPES):
        k[t, K_BAND + t:K_BAND + t + 2] = 1.0
    k[:, K_IDENT:K_IDENT + P] = np.eye(P)
    inv = 1.0 / 10000.0 ** (np.arange(0, HD, 2, dtype=np.float64) / HD)
    rot = np.zeros((P, P))
    for h in range(HEADS):
        ang = np.concatenate([h * inv, h * inv])
        for d in range(HD):
            row = h * HD + d
            rot[row, row] = np.cos(ang[d])
            rot[row, row + 1 if d % 2 == 0 else row - 1] = -np.sin(ang[d]) if d % 2 == 0 else np.sin(ang[d])
    k[:, K_ROPEQ:K_ROPEQ + P] = rot.T / np.sqrt(HD)
    k[:, K_ROPEK:K_ROPEK + P] = rot.T
    for f in range(P):
        k[:, K_VMASK + f] = p // QUAD == (f % QUAD) // HD
    return k


class Chain:

    def __init__(self, eng, sem):
        self.eng, self.sem, self.n, self.base = eng, sem, 0, None

    def step(self, ins):
        ins.then_inc(self.sem, 1)
        self.n += 1

    def sync(self):
        self.eng.wait_ge(self.sem, self.n if self.base is None else self.base + self.n)

    def link(self, ins):
        self.step(ins)
        self.sync()

    def mark(self, ins):
        self.step(ins)
        return self.n

    def after(self, place):
        self.eng.wait_ge(self.sem, place if self.base is None else self.base + place)


def ffn_items(n):
    return [(f, c) for f in range(n) for c in range(FC)]


def network(nc, I, konst, out):
    ctx = ExitStack()
    with ctx:
        def sb(name, shape, dt=F32):
            return ctx.enter_context(nc.sbuf_tensor(name, shape, dt))

        kc = sb("kc", [P, K_END])
        ident, rope_q, rope_k = (kc[:, k:k + P] for k in (K_IDENT, K_ROPEQ, K_ROPEK))
        vmask = kc[:, K_VMASK:K_VMASK + P]
        rows0 = sb("rows0", [R_END0, P])
        cols0 = sb("cols0", [P, R_END0])
        rows = sb("rows", [P, P])
        cols = sb("cols", [P, P])
        ids = sb("ids", [P, 3, B], I32)
        idf = sb("idf", [P, 3, B])
        ones = sb("ones", [1, P])
        minus_half = sb("minus_half", [P, TILES])
        ones3 = sb("ones3", [3, P], BF16)
        lang_hot = sb("lang_hot", [P, B])
        cat_hot = sb("cat_hot", [P, B])
        type_hot = sb("type_hot", [P, B])
        lang_mask = sb("lang_mask", [P, LCH, B])
        type_mask = sb("type_mask", [P, TYPES, B])
        batch_cols = sb("batch_cols", [P, 3, B])
        gamma_b, beta_b, cbias_b = (batch_cols[:, n, :] for n in range(3))
        w1a = sb("w1a", [P, LANGS * ADIM])
        w2a = sb("w2a", [P, LCH, D])
        lang_rows = sb("lang_rows", [LANGS, 3, D])
        w_att = sb("w_att", [P, 4, D])
        rope_bias = sb("rope_bias", [P, 2])
        key_bias = sb("key_bias", [P, HG])
        token_bias = sb("token_bias", [1, D])
        cat_bias = sb("cat_bias", [CATS, D])
        ar1 = sb("ar1", [P, MER + ME])
        ar2 = sb("ar2", [P, FC, MER + ME])
        b1aug = sb("b1aug", [MER + 1, FF])
        b2aug = sb("b2aug", [MER + 1, D])
        w1f = sb("w1f", [P, FF])
        w2f = sb("w2f", [P, FC, D])
        NE1 = L1S + L1E
        gate1 = sb("gate1", [P, L1S + 1, D])
        gate2 = sb("gate2", [P, L1S + 1])
        gate1b = sb("gate1b", [P, L2S + 1, D])
        gate2b = sb("gate2b", [P, L2S + 1])
        gvec = sb("gvec", [TYPES, 3, L1E])
        gred = sb("gred", [TYPES, 4])
        type_coef = sb("type_coef", [P, L1E, B])
        wl = [sb(f"wl{s}", [P, 4 * D + 2 * FF]) for s in range(2)]
        vl = [sb(f"vl{s}", [P, LV]) for s in range(2)]
        bias3 = sb("bias3", [3, 2 * LAYERS, D], BF16)
        rl = [sb(f"rl{s}", [3, 2, D], BF16) for s in range(2)]
        node_rows = sb("node_rows", [TREES * LEAVES, D])
        node_t = sb("node_t", [P, TREES * LEAVES])
        node_bias = sb("node_bias", [1, TREES * LEAVES])
        leaf_b2 = sb("leaf_b2", [TREES * QUAD, D])
        leaf_val = sb("leaf_val", [P, P], BF16)
        filler = sb("filler", [P, 1], BF16)

        xt = [sb(f"xt{n}", [P, 2, TILES, D]) for n in range(2)]
        cf = sb("cf", [P, 2, HT])
        yt = sb("yt", [P, 2, TILES, D])
        stat = sb("stat", [P, 2, TILES, 6])
        after_stats = sb("after_stats", [P, 1])
        mv = sb("mv", [P, 2, TILES, 2])
        rv = sb("rv", [P, 2, TILES])
        rstd = sb("rstd", [P, 2, TILES])
        small = sb("small", [P, 2, 64])
        small2 = sb("small2", [P, 2, 64])
        logit = sb("logit", [P, 2, TILES, ME])
        zg = sb("zg", [P, 2, TILES, QUAD])
        zgt = sb("zgt", [QUAD, 2, HT])
        gsm = sb("gsm", [HB, 2, 16])
        gwb = sb("gwb", [HB, 2, 4, P])
        gcol = sb("gcol", [P, 2, 4, HB])
        grel = sb("grel", [P, 2, HB])
        dec = sb("dec", [P, 2, TILES * TREES, LEAVES])
        reach = sb("reach", [P, 2, TILES * TREES, 16])
        sel = sb("sel", [P, 2, TILES, TREES, QUAD])
        selt = sb("selt", [TREES * QUAD, 2, HT])
        selb = sb("selb", [TREES * QUAD, 2, HT], BF16)
        with ExitStack() as once:
            def sb_once(name, shape):
                return once.enter_context(nc.sbuf_tensor(name, shape, F32))

            big = sb_once("big", [P, B * D])
            tree_v = sb_once("tree_v", [P, 2 * LFC * P])
            xf = sb_once("xf", [P, 2, HT])
            xn = sb_once("xn", [P, 2, TILES, D])
            arena = sb_once("arena", [P, NE1, 2, FF])
            Z = [sb_once(f"z{h}", [P, 16, HT]) for h in HALVES]
        big_r = sb("big_r", [P, B * D], F32R)
        tree_v_r = sb("tree_v_r", [P, 2 * LFC * P], F32R)
        xf_r = sb("xf_r", [P, 2, HT], F32R)
        xn_r = sb("xn_r", [P, 2, HT], F32R)
        w_cat = big[:, :].rearrange("p (b n) -> p b n", b=B)
        arena_r = sb("arena_r", [P, NE1, 2, FF], F32R)
        Z_R = []
        for h in HALVES:
            sb(f"z_low{h}", [P, 4, HT])
            Z_R.append(sb(f"zr{h}", [P, 12, HT], F32R))
        lang_tok = Z[0][0:16, 14:16, :].rearrange("p a (b s) -> p (a b) s", s=S)
        w_nat = Z[1][:, 14, :].rearrange("p (n d) -> p n d", n=4)
        row_bias = Z[1][0:1, 4:8, :].rearrange("p a n -> p (a n)")
        row_parts = Z[1][0:1, 8:14, :].bitcast(BF16).rearrange("p a n -> p (a n)")
        gwide = Z[0][0:TYPES, 11, :].rearrange("p (e n) -> p e n", e=L1E)

        ps = [ctx.enter_context(nc.psum_tensor(f"ps{h}", [P, BANKS, HT], F32)) for h in HALVES]

        class Sems(dict):
            def __missing__(self, name):
                self[name] = ctx.enter_context(nc.semaphore(name))
                return self[name]

        S_ = Sems()
        names = """ld_rb p_rb p_own ld_const ld_ids ld_x ld_rows0 ld_rows ld_a1 ld_a ld_b ld_cat ld_c ld_d ld_gv ld_e ld_f0 ld_f1 ld_g ld_h st_out
            dve k_mem p_cols0 p_cols0c p_cols p_colsc p_watt p_wattc p_rope p_ropec p_keyb p_node p_nodec p_hot p_bat p_batc
            p_gw p_coef p_coefc
            x_tr x_f a_hid a_relu a_mask a_out a_tr a_cond var rstd xn
            b_qk b_k b_rep b_qe b_vr b_vx b_sc b_sub b_exp b_pt b_ctx b_ctxc b_out b_res b_tr b_xf
            c_mm c_out d_r1 d_z d_e d_zt d_ztc d_hid d_relu d_r2 d_out d_res d_tr d_xf
            e_xl e_w e_hid e_hi e_lo e_acc e_accc e_accd e_sum e_g1 e_g1c e_g2 e_ge e_gw e_gb e_gbc e_out
            f_q f_k f_v f_vb f_exp f_ln f_den f_ratio f_u f_o f_og f_tr f_x f_y f_ft f_w1 f_h f_w2 f_w2g
            g_res g_tr g_xf
            g_xl g_w g_hid g_hi g_lo g_acc g_accc g_accd g_sum g_g1 g_g1c g_g2 g_ge g_gw g_gb g_gbc g_out
            h_w h_xl h_sc h_sel h_st h_stc h_stb h_lb h_lbc h_hid h_relu h_mask h_acc h_accc h_s h_sub h_exp h_pt h_o h_fin"""
        for n in names.split():
            S_[n]
        block = ctx.enter_context(nc.Block())

        def w_tree(t):
            w = tree_v[:, :] if t == 2 else big[:, t * 2 * LFC * P:(t + 1) * 2 * LFC * P]
            return w.rearrange("p (a c n) -> p a c n", a=2, c=LFC)

        def tok(h, i):
            return slice(i * P, (i + 1) * P)

        def z(h, n, k=1):
            return Z[h][:, n, :] if k == 1 else Z[h][:, n:n + k, :]

        def by_batch(ap):
            return ap.rearrange("p (b s) -> p b s", s=S)

        def row_part(n):
            return row_parts[:, n * 2 * LAYERS * D:(n + 1) * 2 * LAYERS * D]

        def spread(ap, n):
            return ap.unsqueeze(len(ap.shape)).to_broadcast([*ap.shape, n])

        def keys_by_quadrant(h):
            return z(h, 4, 4).rearrange("p g (b q s) -> p (g b) q s", b=GB, q=HG)

        def by_head(ap, j):
            return ap.rearrange("p (bq j d) -> p bq j d", j=HPQ, d=HD)[:, :, j, :]

        def norm_count(l, h, n):
            first = isinstance(l, int) and l == 0
            last = isinstance(l, int) and l == LAYERS - 1
            if h == 0:
                return (1 if first else l * 4) if n == 0 else l * 4 + 3
            return l * 4 + 2 if n == 0 else l * 4 + (4 if last else 5)

        def back_count(l, h, n):
            if n == 1:
                return norm_count(l, h, 0) + 2
            if isinstance(l, int):
                return h + 1 if l == 0 else norm_count(l - 1, h, 1) + 2
            return l * 4 + (1 + 2 * h)

        def x_part(h, part):
            return Z_R[h][:, (12, 15)[part] - 4, :]

        def hidden_part(h, n, part):
            return Z_R[h][:, 4 * part + n % 4, :]

        def w_part(f, part):
            return (arena_r[:, f] if part else Z_R[f % 2][:, 13 - 4:15 - 4, :]).rearrange("p a n -> p (a n)")

        def tree_part(t, part):
            n = LFC * P
            if part == 0:
                return arena_r[:, (NE1 - 2, NE1 - 1, 0)[t]].rearrange("p a n -> p (a n)")
            return tree_v_r[:, 0:n] if t == 2 else big_r[:, 2 * t * n:(2 * t + 1) * n]

        @block.sync
        def _(sp):
            def load(dst, src, sem):
                sp.dma_start(dst, src).then_inc(S_[sem], 16)

            def row(name):
                return I[name].rearrange("(a n) -> a n", a=1)

            load(kc[:, :], konst, "ld_const")
            load(xt[0][:, :, :, :].rearrange("p h i d -> p (h i) d"),
                 I["x"].rearrange("b s d -> (b s) d").rearrange("(n p) d -> p n d", p=P), "ld_x")
            for n, name in enumerate(("itok_B_0_8", "itok_B_2_61", "itok_B_0_2")):
                load(ids[:, n, :], row(name).to_broadcast([P, B]), "ld_ids")
            sp.wait_ge(S_["k_mem"], 3)
            full = LANGS * ADIM // P
            b1a = I["L0_cond_b1"].rearrange("l a -> (l a)")
            load(rows0[R_ADAPT:R_ADAPT + full, :], b1a[0:full * P].rearrange("(n p) -> n p", p=P), "ld_rows0")
            load(rows0[R_ADAPT + full:R_ADAPT + full + 1, 0:LANGS * ADIM - full * P],
                 b1a[full * P:LANGS * ADIM].rearrange("(a n) -> a n", a=1), "ld_rows0")
            for r, name in ((R_L0Q, "bq"), (R_L0K, "bk"), (R_L0V, "bv")):
                load(rows0[r:r + 1, :], row("L0_attn_" + name), "ld_rows0")
            load(w1a[:, :].rearrange("p (l a) -> p l a", l=LANGS), I["L0_cond_W1"].rearrange("l d a -> d l a"), "ld_a1")
            w2 = I["L0_cond_W2"].rearrange("l a d -> (l a) d")
            load(w2a[:, 0:full, :], w2[0:full * P, :].rearrange("(c p) d -> p c d", p=P), "ld_a")
            load(w2a[0:LANGS * ADIM - full * P, full, :], w2[full * P:LANGS * ADIM, :], "ld_a")
            for n, name in enumerate(("b2", "gamma", "beta")):
                load(lang_rows[:, n, :], I["L0_cond_" + name], "ld_a")
            for n, q in enumerate("qkvo"):
                load(w_nat[:, n, :], I["L0_attn_W" + q], "ld_b")
            load(token_bias[:, :], row("L0_attn_bo"), "ld_b")
            load(cat_bias[:, :], I["L0_cond2_bias"], "ld_c")
            for n, name in enumerate(("bo", "b2")):
                load(row_bias[:, n * LAYERS * D:(n + 1) * LAYERS * D],
                     I["L1_attn_" + name].rearrange("(a l) d -> a (l d)", a=1), "ld_rb")
            for r, name in ((V_BQ, "bq"), (V_BK, "bk"), (V_BV, "bv"), (V_S1, "ln1_s"), (V_B1, "ln1_b"),
                            (V_S2, "ln2_s"), (V_B2, "ln2_b")):
                load(rows[r:r + LV * (LAYERS - 1) + 1:LV, :], I["L1_attn_" + name], "ld_rows")
            for c in range(FC):
                load(rows[V_FF + c:V_FF + c + LV * (LAYERS - 1) + 1:LV, :], I["L1_attn_b1"][:, c * P:(c + 1) * P], "ld_rows")
            for t, q in enumerate("qkv"):
                load(rows[R_LEAF + t * LFC:R_LEAF + (t + 1) * LFC, :],
                     I[f"L1_ffn_{q}_b1"].rearrange("(c a) n -> c (a n)", a=P // LEAFW), "ld_rows")
            sp.wait_ge(S_["p_rb"], 5)
            for part in range(3):
                load(bias3[part:part + 1, :, :].rearrange("p l d -> p (l d)"), row_part(part), "ld_rb")
            sp.wait_ge(S_["ld_ids"], 48)
            with sp.Fori(0, B) as b:
                cat = sp.value_load(ids[0:1, 1, bass.ds(b, 1)], min_val=0, max_val=CATS - 1)
                sp.dma_start(w_cat[:, bass.ds(b, 1), :],
                             I["L0_cond2_weight"][bass.ds(cat, 1), :, :].rearrange("a p n -> p a n")
                             ).then_inc(S_["ld_cat"], 16)
            load(gvec[:, 0, :], I["L1_cond_gate_vecs"], "ld_gv")
            for e in range(ME):
                load(ar1[:, e * MR:(e + 1) * MR], I["L0_ffn_A1"][e], "ld_d")
                load(ar2[:, :, e * MR:(e + 1) * MR], I["L0_ffn_A2"][e].rearrange("(c p) r -> p c r", p=P), "ld_d")
            load(ar1[:, MER:MER + ME], I["L0_ffn_R1"], "ld_d")
            load(ar2[:, :, MER:MER + ME], I["L0_ffn_R2"].rearrange("(c p) e -> p c e", p=P), "ld_d")
            load(b1aug[0:MER, :], I["L0_ffn_B1"].rearrange("e r n -> (e r) n"), "ld_d")
            load(b1aug[MER:MER + 1, :], row("L0_ffn_b1"), "ld_d")
            load(b2aug[0:MER, :], I["L0_ffn_B2"].rearrange("e r n -> (e r) n"), "ld_d")
            load(b2aug[MER:MER + 1, :], row("L0_ffn_b2"), "ld_d")
            load(w1f[:, :], I["L0_ffn_W1"], "ld_d")
            load(w2f[:, :, :], I["L0_ffn_W2"].rearrange("(c p) n -> p c n", p=P), "ld_d")

            def load_ffns(wi, wo, n, at, sem):
                load(arena[:, at:at + n, 0, :], I[wi][0:n].rearrange("e d f -> d e f"), sem)
                for e in range(n):
                    load(arena[:, at + e, 1, :].rearrange("p (c n) -> p c n", c=FC),
                         I[wo][e].rearrange("(c p) n -> p c n", p=P), sem)

            load_ffns("L1_cond_share_wi", "L1_cond_share_wo", L1S, 0, "ld_e")
            load_ffns("L1_cond_expert_wi", "L1_cond_expert_wo", L1E, L1S, "ld_e")
            load(gate1[:, :, :], I["L1_cond_gate_w1"].rearrange("(c p) n -> p c n", p=P), "ld_e")
            load(gate2[:, :], I["L1_cond_gate_w2"], "ld_e")

            def load_layer(l, s):
                one = bass.ds(l, 1)
                for n, q in enumerate("qkvo"):
                    load(wl[s][:, n * D:(n + 1) * D].rearrange("p (a n) -> p a n", a=1),
                         I["L1_attn_W" + q][one].rearrange("a p n -> p a n"), f"ld_f{s}")
                load(wl[s][:, 4 * D:4 * D + FF].rearrange("p (a n) -> p a n", a=1),
                     I["L1_attn_W1"][one].rearrange("a p n -> p a n"), f"ld_f{s}")
                load(wl[s][:, 4 * D + FF:].rearrange("p (c n) -> p c n", c=FC),
                     I["L1_attn_W2"][one].rearrange("a (c p) n -> p (a c) n", p=P), f"ld_f{s}")
                load(vl[s][:, :].rearrange("p (a n) -> p a n", a=1),
                     cols[:, 0:LV * LAYERS].rearrange("p (l n) -> p l n", l=LAYERS)[:, one, :], f"ld_f{s}")

                for n in range(2):
                    load(rl[s][:, n:n + 1, :], bias3[:, bass.ds(l + n * LAYERS, 1), :], f"ld_f{s}")

            sp.wait_ge(S_["ld_rb"], 16 * 5)
            sp.wait_ge(S_["p_colsc"], 1)
            for s in range(2):
                load_layer(s, s)
            load(gate1b[:, :, :], I["L1_cond2_g1"].rearrange("(c p) n -> p c n", p=P), "ld_g")
            load(gate2b[:, :], I["L1_cond2_g2"], "ld_g")
            sp.wait_ge(S_["dve"], 2)
            for t, q in enumerate("qkv"):
                load(node_rows[t * LEAVES:t * LEAVES + NODES, :], I[f"L1_ffn_{q}_node_w"], "ld_h")
                load(node_bias[0:1, t * LEAVES:t * LEAVES + NODES], row(f"L1_ffn_{q}_node_b"), "ld_h")
                load(leaf_b2[t * QUAD:t * QUAD + LEAVES, :], I[f"L1_ffn_{q}_b2"], "ld_h")
            sp.wait_ge(S_["c_mm"], 2)
            for t, q in enumerate("qkv"):
                load(w_tree(t)[:, 0].rearrange("p c (a n) -> p (c a) n", a=P // LEAFW),
                     I[f"L1_ffn_{q}_w1"].rearrange("l d n -> d l n"), "ld_h")
                load(w_tree(t)[:, 1], I[f"L1_ffn_{q}_w2"].rearrange("(c a) n d -> (a n) c d", a=P // LEAFW), "ld_h")
            sp.wait_ge(S_["e_acc"], 2 * NE1)
            load_ffns("L1_cond2_swi", "L1_cond2_swo", L2S, 0, "ld_g")
            load_ffns("L1_cond2_wi", "L1_cond2_wo", TYPES, L2S, "ld_g")
            with sp.Fori(0, LAYERS // 2 - 1) as it:
                for s in range(2):
                    sp.wait_ge(S_["f_y"], it * 4 + (2 * s + 2))
                    load_layer(it * 2 + (2 + s), s)
            for h in HALVES:
                sp.wait_ge(S_["h_fin"], h + 1)
                sp.dma_start(out.rearrange("b s d -> (b s) d").rearrange("(n p) d -> p n d", p=P)
                             [:, h * TILES:(h + 1) * TILES, :], yt[:, h]).then_inc(S_["st_out"], 16)
            sp.wait_ge(S_["st_out"], 32)

        @block.gpsimd
        def _(pool):
            nc.gpsimd.memset(filler[:, :], 0.0).then_inc(S_["k_mem"], 1)
            nc.gpsimd.memset(rows0[:, :], 0.0).then_inc(S_["k_mem"], 1)
            nc.gpsimd.memset(rows[:, :], 0.0).then_inc(S_["k_mem"], 1)
            nc.gpsimd.memset(ones[:, :], 1.0).then_inc(S_["k_mem"], 1)
            nc.gpsimd.memset(minus_half[:, :], -0.5).then_inc(S_["k_mem"], 1)
            nc.gpsimd.memset(zg[:, :, :, :], 0.0).then_inc(S_["k_mem"], 1)
            nc.gpsimd.memset(ones3[:, :], 1.0).then_inc(S_["k_mem"], 1)
            pool.wait_ge(S_["k_mem"], 7)
            nc.gpsimd.memset(zg[:, :, :, MER:MER + 1], 1.0).then_inc(S_["k_mem"], 1)

            def root(n, half):
                pool.wait_ge(S_["var"], n)
                nc.gpsimd.tensor_tensor(rstd[:, half, :], rv[:, half, :], minus_half[:, :], ALU.pow
                                        ).then_inc(S_["rstd"], 1)

            for h in HALVES:
                root(h + 1, h)

            for n in range(2 * NG):
                h, g = n % 2, n // 2
                if g == 0:
                    pool.wait_ge(S_["a_cond"], h + 1)
                if g >= 3:
                    pool.wait_ge(S_["b_vr"], n - 5)
                src = cf[:, h][:, g * GB * S:(g + 1) * GB * S].rearrange("p (b s) -> p b s", s=S)
                nc.gpsimd.tensor_copy(z(h, g % 3).rearrange("p (b j s) -> p b j s", b=GB, j=HPQ),
                                      src.unsqueeze(2).to_broadcast([P, GB, HPQ, S])).then_inc(S_["b_rep"], 1)

            own = Chain(pool, S_["p_own"])

            def split(whole, part, sem):
                own.link(nc.gpsimd.tensor_copy(part(0), whole))
                nc.gpsimd.tensor_tensor(part(1), whole, part(0), ALU.subtract).then_inc(S_[sem], 1)

            def split_weights(k, ffns):
                for f in ffns:
                    if f >= 2:
                        pool.wait_ge(S_[k + "_acc"], 2 * (f - 1))
                    split(arena[:, f].rearrange("p a n -> p (a n)"), lambda part: w_part(f, part), k + "_w")

            pool.wait_ge(S_["b_ctx"], 2)
            pool.wait_ge(S_["ld_e"], 16 * (4 + L1S + L1E))
            split_weights("e", range(NE1))

            def layer(l):
                for h, m, n in ((1, l, 0), (0, l, 1), (0, l + 1, 0), (1, l, 1)):
                    root(norm_count(m, h, n) + 2, h)

            root(norm_count(0, 0, 0) + 2, 0)
            layer(0)
            with pool.Fori(0, LAYERS // 2 - 1) as it:
                layer(it * 2 + 1)
                layer(it * 2 + 2)
            last = LAYERS - 1
            for h, n in ((1, 0), (0, 1)):
                root(norm_count(last, h, n) + 2, h)
            pool.wait_ge(S_["ld_g"], 16 * (4 + L2S + TYPES))
            split_weights("g", range(1))
            root(norm_count(last, 1, 1) + 2, 1)
            split_weights("g", range(1, L2S + TYPES))

            pool.wait_ge(S_["ld_h"], 16 * 15)
            for t in range(TREES):
                split(w_tree(t)[:, 0].rearrange("p c n -> p (c n)"), lambda part: tree_part(t, part), "h_w")
            for h in HALVES:
                pool.wait_ge(S_["g_out"], h + 1)
                split(cf[:, h], lambda part: (xn_r, xf_r)[part][:, h], "h_xl")

        @block.scalar
        def _(act):
            def copy(dst, src, sem):
                nc.scalar.activation(dst, src, ACT.Copy).then_inc(S_[sem], 1)

            def linear(dst, src, bias, scale=1.0):
                return nc.scalar.activation(dst, src, ACT.Identity, bias=bias, scale=scale)

            for h in HALVES:
                act.wait_ge(S_["x_tr"], h + 1)
                copy(xf[:, h], ps[h][:, 3, :], "x_f")
            act.wait_ge(S_["p_cols0"], 1)
            copy(cols0[:, :], ps[0][:, 0, 0:R_END0], "p_cols0c")

            for c in range(LCH):
                m = min(P, LANGS * ADIM - c * P)
                for h in HALVES:
                    act.wait_ge(S_["a_hid"], 2 * c + h + 1)
                    nc.scalar.activation(z(h, c)[0:m, :], ps[h][0:m, c, :], ACT.Relu,
                                         bias=cols0[0:m, R_ADAPT + c:R_ADAPT + c + 1]).then_inc(S_["a_relu"], 1)
            act.wait_ge(S_["p_watt"], 1)
            copy(w_att[:, :, :].rearrange("p a n -> p (a n)"), ps[1][:, 0, :], "p_wattc")
            act.wait_ge(S_["p_rope"], 1)
            copy(rope_bias[:, :], ps[0][:, 1, 0:2], "p_ropec")
            act.wait_ge(S_["p_bat"], 1)
            copy(batch_cols[:, :, :].rearrange("p a b -> p (a b)"), ps[0][:, 2, 0:3 * B], "p_batc")
            act.wait_ge(S_["p_cols"], 1)
            copy(cols[:, :], ps[1][:, 1, 0:P], "p_colsc")

            act.wait_ge(S_["p_keyb"], 1)
            for h in HALVES:
                act.wait_ge(S_["b_qk"], h + 1)
                for q in range(HG):
                    ins = linear(keys_by_quadrant(h)[:, :, q, :], by_batch(ps[h][:, 1, :]), key_bias[:, q:q + 1],
                                 vmask[:, q * HD:q * HD + 1])
                ins.then_inc(S_["b_k"], 1)
            for n in range(2 * NG):
                h, g = n % 2, n // 2
                act.wait_ge(S_["b_vr"], n + 1)
                for j in range(HPQ):
                    ins = nc.scalar.activation(by_head(z(h, 12 + g), j), by_head(ps[h][:, 2, :], j), ACT.Copy,
                                               scale=vmask[:, j * HD:j * HD + 1])
                ins.then_inc(S_["b_vx"], 1)
                act.wait_ge(S_["b_sub"], n + 1)
                nc.scalar.activation(z(h, 4 + g), z(h, 4 + g), ACT.Exp).then_inc(S_["b_exp"], 1)
            for h in HALVES:
                act.wait_ge(S_["b_ctx"], h + 1)
                linear(z(h, 0), ps[h][:, 1, :], cols0[:, R_L0V:R_L0V + 1]).then_inc(S_["b_ctxc"], 1)
            for h in HALVES:
                act.wait_ge(S_["b_tr"], h + 1)
                copy(xf[:, h], ps[h][:, 3, :], "b_xf")

            def mixture(r):
                for h in HALVES:
                    act.wait_ge(S_["d_z"], 2 * (2 * r + h) + 1)
                    nc.scalar.activation(logit[:, h], logit[:, h], ACT.Exp).then_inc(S_["d_e"], 1)
                for h in HALVES:
                    act.wait_ge(S_["d_zt"], 2 * r + h + 1)
                    copy(zgt[:, h], ps[h][0:QUAD, 3, :], "d_ztc")

            mixture(0)
            act.wait_ge(S_["p_gw"], 1)
            nc.scalar.activation(gvec[:, 1, :], gvec[:, 1, :], ACT.Exp, scale=10.0,
                                 accum_out=gred[:, 1:2]).then_inc(S_["p_gw"], 1)
            for c in range(FC):
                for h in HALVES:
                    act.wait_ge(S_["d_hid"], 2 * c + h + 1)
                    nc.scalar.activation(z(h, c), ps[h][:, c % 3, :], ACT.Relu).then_inc(S_["d_relu"], 1)
            mixture(1)
            act.wait_ge(S_["p_coef"], 1)
            copy(type_coef[:, :, :].rearrange("p e b -> p (e b)"), ps[0][:, 2, 0:L1E * B], "p_coefc")
            for h in HALVES:
                act.wait_ge(S_["d_tr"], h + 1)
                copy(x_part(h, 0), ps[h][:, 3, :], "d_xf")

            def experts(k, n_ffns, shares):
                for n, (f, c) in enumerate(ffn_items(n_ffns)):
                    for h in HALVES:
                        act.wait_ge(S_[k + "_hid"], 2 * n + h + 1)
                        nc.scalar.activation(hidden_part(h, n, 0), ps[h][:, n % 2, :], ACT.Relu).then_inc(S_[k + "_hi"], 1)
                    if c == 0 and 0 < f <= shares:
                        for h in HALVES:
                            act.wait_ge(S_[k + "_acc"], 2 * (f - 1) + h + 1)
                            copy(z(h, f - 1), ps[h][:, 2 + (f - 1) % 2, :], k + "_accc")
                for h in HALVES:
                    act.wait_ge(S_[k + "_g1"], h + 1)
                    nc.scalar.activation(grel[:, h], ps[h][:, 0, 0:HB], ACT.Relu).then_inc(S_[k + "_g1c"], 1)
                for h in HALVES:
                    act.wait_ge(S_[k + "_g2"], 2 * h + 2)
                    nc.scalar.activation(gsm[:, h, 4:5 + shares], ps[h][0:HB, 1, 0:shares + 1], ACT.Exp,
                                         bias=gsm[:, h, 8:9], accum_out=gsm[:, h, 9:10]).then_inc(S_[k + "_ge"], 1)
                for h in HALVES:
                    act.wait_ge(S_[k + "_gb"], h + 1)
                    copy(gcol[:, h, 0:shares + 1, :].rearrange("p a b -> p (a b)"),
                         ps[h][:, 2, 0:(shares + 1) * HB], k + "_gbc")

            experts("e", NE1, L1S)

            def col(r, s):
                return vl[s][:, r:r + 1]

            def feature_maps(l, h, s):
                nc.scalar.preload_act_table_set("natural_log_exp_and_others")
                for bank, bias, dst, sem in ((2, V_BK, 6, "f_k"), (0, V_BQ, 4, "f_q")):
                    act.wait_ge(S_[sem], l * 2 + (h + 1))
                    nc.scalar.activation(z(h, dst), ps[h][:, bank, :], ACT.Exp, bias=col(bias, s)).then_inc(S_["f_exp"], 1)

            def value_bias(l, h, s):
                act.wait_ge(S_["f_v"], l * 2 + (h + 1))
                linear(z(h, 7), ps[h][:, 1, :], col(V_BV, s)).then_inc(S_["f_vb"], 1)

            def ratio(l, h):
                act.wait_ge(S_["f_den"], l * 2 + (h + 1))
                nc.scalar.activation(z(h, 10), z(h, 10), ACT.Ln, scale=1.0 / EPS_ATTN, bias=1.0
                                     ).then_inc(S_["f_ln"], 1)
                act.wait_ge(S_["f_ln"], l * 2 + (h + 1))
                nc.scalar.activation(z(h, 10), z(h, 10), ACT.Exp, scale=-1.0).then_inc(S_["f_ratio"], 1)

            def gelu_o(l, h):
                act.wait_ge(S_["f_o"], l * 2 + (h + 1))
                nc.scalar.activation(z(h, 4), ps[h][:, 0, :], ACT.Gelu_apprx_tanh).then_inc(S_["f_og"], 1)

            def affine(l, h, s):
                act.wait_ge(S_["f_tr"], norm_count(l, h, 0))
                linear(cf[:, h], ps[h][:, 1, :], col(V_B1, s), col(V_S1, s)).then_inc(S_["f_x"], 1)

            def gelu_h(l, h, s, chunks):
                for c in chunks:
                    act.wait_ge(S_["f_w1"], l * (2 * FC) + (h * FC + c + 1))
                    nc.scalar.activation(z(h, c), ps[h][:, FFN_BANK[c], :], ACT.Gelu_apprx_tanh,
                                         bias=col(V_FF + c, s)).then_inc(S_["f_h"], 1)

            def gelu_f(l, h):
                act.wait_ge(S_["f_w2"], l * 2 + (h + 1))
                nc.scalar.activation(z(h, 5), ps[h][:, 2, :], ACT.Gelu_apprx_tanh).then_inc(S_["f_w2g"], 1)

            def segment(l, a, sa, m, b, sb_):
                if m is not None:
                    affine(m, b, sb_)
                    gelu_h(m, b, sb_, (0, 1))
                if l is not None:
                    feature_maps(l, a, sa)
                    value_bias(l, a, sa)
                    ratio(l, a)
                if m is not None:
                    gelu_h(m, b, sb_, (2,))
                if l is not None:
                    gelu_o(l, a)
                if m is not None:
                    gelu_h(m, b, sb_, (3,))
                    gelu_f(m, b)

            def layer(l, s):
                segment(l, 1, s, l, 0, s)
                segment(l + 1, 0, 1 - s, l, 1, s)

            segment(0, 0, 0, None, None, None)
            layer(0, 0)
            with act.Fori(0, LAYERS // 2 - 1) as it:
                layer(it * 2 + 1, 1)
                layer(it * 2 + 2, 0)
            last = LAYERS - 1
            segment(last, 1, 1, last, 0, 1)
            affine(last, 1, 1)
            gelu_h(last, 1, 1, range(FC))
            gelu_f(last, 1)

            for h in HALVES:
                act.wait_ge(S_["g_tr"], h + 1)
                copy(x_part(h, 0), ps[h][:, 2, :], "g_xf")
            experts("g", L2S + TYPES, L2S)

            act.wait_ge(S_["p_node"], 1)
            copy(node_t[:, :], ps[1][:, 1, 0:TREES * LEAVES], "p_nodec")
            for h in HALVES:
                act.wait_ge(S_["h_st"], h + 1)
                copy(selt[:, h], ps[h][0:TREES * QUAD, 3, :], "h_stc")
            for t in range(TREES):
                for h in HALVES:
                    act.wait_ge(S_["h_lb"], 2 * t + h + 1)
                    copy(z(h, 12 + t), ps[h][:, t, :], "h_lbc")
            for n in range(TREES * LFC):
                t, c = divmod(n, LFC)
                for h in HALVES:
                    act.wait_ge(S_["h_hid"], 2 * n + h + 1)
                    if n >= 3:
                        act.wait_ge(S_["h_mask"], 2 * (n - 3) + h + 1)
                    nc.scalar.activation(z(h, 4 + n % 3), ps[h][:, n % 2, :], ACT.Relu,
                                         bias=cols[:, R_LEAF + n:R_LEAF + n + 1]).then_inc(S_["h_relu"], 1)
                if n % LFC == 1 and t > 0 or n == TREES * LFC - 1:
                    g = t if n == TREES * LFC - 1 else t - 1
                    for h in HALVES:
                        act.wait_ge(S_["h_acc"], 2 * g + h + 1)
                        copy(z(h, g), ps[h][:, 2 + g % 2, :], "h_accc")
            for h in HALVES:
                act.wait_ge(S_["h_sub"], h + 1)
                nc.scalar.activation(z(h, 3)[:, 0:HT // 4], z(h, 3)[:, 0:HT // 4], ACT.Exp,
                                     scale=float(1.0 / np.sqrt(D))).then_inc(S_["h_exp"], 1)

        @block.vector
        def _(dve):
            own = Chain(dve, S_["dve"])
            V = nc.vector

            dve.wait_ge(S_["ld_ids"], 48)
            dve.wait_ge(S_["ld_const"], 16)
            own.step(V.memset(node_rows[:, :], 0.0))
            own.step(V.memset(node_bias[:, :], 0.0))
            own.link(V.tensor_copy(idf[:, :, :], ids[:, :, :]))
            iota = kc[:, K_IOTA:K_IOTA + 1]
            own.link(V.tensor_scalar(lang_hot[:, :], idf[:, 0, :], iota, None, ALU.is_equal))
            V.tensor_scalar(cat_hot[:, :], idf[:, 1, :], iota, None, ALU.is_equal).then_inc(S_["p_hot"], 1)
            V.tensor_scalar(type_hot[:, :], idf[:, 2, :], iota, None, ALU.is_equal).then_inc(S_["p_hot"], 1)
            V.tensor_copy(lang_tok[:, :, :], spread(lang_hot[0:16, :], S)).then_inc(S_["p_hot"], 1)
            for c in range(LCH):
                own.step(V.tensor_scalar(lang_mask[:, c, :], idf[:, 0, :], kc[:, K_LANG + c:K_LANG + c + 1], None,
                                         ALU.is_equal))
            for t in range(TYPES):
                own.step(V.tensor_scalar(type_mask[:, t, :], idf[:, 2, :], float(t), None, ALU.is_equal))
            own.step(V.tensor_copy(leaf_val[:, :], kc[:, K_SLOT:K_SLOT + 1].to_broadcast([P, P])))
            own.sync()

            def add_residual(h, src, res):
                own.step(V.tensor_tensor(yt[:, h].rearrange("p i d -> p (i d)"), src, res, ALU.add))

            def stats(h, eps):
                own.sync()
                for i in range(TILES):
                    own.step(V.bn_stats(stat[:, h, i, :], yt[:, h, i, :]))
                own.sync()
                own.step(V.memset(after_stats[:, :], 0.0))
                for i in range(TILES):
                    own.step(V.bn_aggr(mv[:, h, i, :], stat[:, h, i, :]))
                own.sync()
                V.tensor_scalar(rv[:, h, :], mv[:, h, :, 1], eps, None, ALU.add).then_inc(S_["var"], 1)
                own.step(V.tensor_tensor(yt[:, h], yt[:, h], spread(mv[:, h, :, 0], D), ALU.subtract))

            def normalise(n, h):
                own.sync()
                dve.wait_ge(S_["rstd"], n)
                V.tensor_tensor(xn[:, h], yt[:, h], spread(rstd[:, h, :], D), ALU.mult).then_inc(S_["xn"], 1)

            for c in range(LCH):
                m = min(P, LANGS * ADIM - c * P)
                for h in HALVES:
                    dve.wait_ge(S_["a_relu"], 2 * c + h + 1)
                    mask = spread(lang_mask[0:m, c, h * HB:(h + 1) * HB], S)
                    V.tensor_tensor(by_batch(z(h, c)[0:m, :]), by_batch(z(h, c)[0:m, :]), mask, ALU.mult
                                    ).then_inc(S_["a_mask"], 1)
            dve.wait_ge(S_["ld_rb"], 32)
            for part in range(3):
                V.tensor_copy(row_part(part), row_bias).then_inc(S_["p_rb"], 1)
                if part < 2:
                    dve.wait_ge(S_["p_rb"], 2 * part + 1)
                    V.tensor_tensor(row_bias, row_bias, row_part(part), ALU.subtract).then_inc(S_["p_rb"], 1)
                    dve.wait_ge(S_["p_rb"], 2 * part + 2)
            for h in HALVES:
                dve.wait_ge(S_["a_out"], h + 1)
                add_residual(h, ps[h][:, 3, :], xt[0][:, h].rearrange("p i d -> p (i d)"))
                stats(h, EPS_COND)
            for h in HALVES:
                normalise(h + 1, h)
            dve.wait_ge(S_["p_batc"], 1)
            for h in HALVES:
                dve.wait_ge(S_["a_tr"], h + 1)
                bs = slice(h * HB, (h + 1) * HB)
                own.link(V.tensor_tensor(by_batch(cf[:, h]), by_batch(ps[h][:, 0, :]), spread(gamma_b[:, bs], S), ALU.mult))
                V.tensor_tensor(by_batch(cf[:, h]), by_batch(cf[:, h]), spread(beta_b[:, bs], S), ALU.add
                                ).then_inc(S_["a_cond"], 1)

            dve.wait_ge(S_["ld_rb"], 16 * 5)
            dve.wait_ge(S_["p_ropec"], 1)
            V.tensor_scalar(key_bias[:, :], vmask[:, 0:QUAD:HD], rope_bias[:, 1:2], None, ALU.mult).then_inc(S_["p_keyb"], 1)
            for h in HALVES:
                dve.wait_ge(S_["b_qk"], h + 1)
                qe = z(h, 8, 4).rearrange("p g (b j s) -> p (g b) j s", b=GB, j=HPQ)
                for j in range(HPQ):
                    ins = V.tensor_scalar(qe[:, :, j, :], by_batch(ps[h][:, 0, :]), rope_bias[:, 0:1],
                                          kc[:, K_HEAD + j:K_HEAD + j + 1], ALU.add, ALU.mult)
                    if j < HPQ - 1:
                        own.step(ins)
                ins.then_inc(S_["b_qe"], 1)

            def grouped(ap, n=S):
                return ap.rearrange("p (a s) -> p a s", s=n)

            def scores(n):
                h, g = n % 2, n // 2
                dve.wait_ge(S_["b_sc"], n + 1)
                sc = ps[h][:, (3, 0)[g % 2], :]
                own.link(V.tensor_reduce(small[:, h, 0:16], grouped(sc), AX_X, ALU.max))
                V.tensor_tensor(grouped(z(h, 4 + g)), grouped(sc), spread(small[:, h, 0:16], S), ALU.subtract
                                ).then_inc(S_["b_sub"], 1)

            def probabilities(n):
                h, g = n % 2, n // 2
                dve.wait_ge(S_["b_exp"], n + 1)
                own.link(V.tensor_reduce(small[:, h, 16:32], grouped(z(h, 4 + g)), AX_X, ALU.add))
                own.link(V.reciprocal(small[:, h, 32:48], small[:, h, 16:32]))
                own.link(V.tensor_tensor(grouped(z(h, 4 + g)), grouped(z(h, 4 + g)), spread(small[:, h, 32:48], S), ALU.mult))
                V.transpose(z(h, 8 + g), z(h, 4 + g)).then_inc(S_["b_pt"], 1)

            for n in range(2 * NG + 1):
                if n < 2 * NG:
                    scores(n)
                if n >= 1:
                    probabilities(n - 1)

            def residual(h, src, old, new, sem):
                V.tensor_tensor(new[:, h].rearrange("p i d -> p (i d)"), src, old[:, h].rearrange("p i d -> p (i d)"),
                                ALU.add).then_inc(S_[sem], 1)

            for h in HALVES:
                dve.wait_ge(S_["b_out"], h + 1)
                residual(h, ps[h][:, 2, :], xt[0], xt[1], "b_res")

            for h in HALVES:
                dve.wait_ge(S_["c_mm"], h + 1)
                V.tensor_tensor(by_batch(cf[:, h]), by_batch(ps[h][:, 0, :]), spread(cbias_b[:, h * HB:(h + 1) * HB], S),
                                ALU.add).then_inc(S_["c_out"], 1)

            def mixture(r):
                zr = [ps[h][:, (1, 0)[r], :].rearrange("p (i k) -> p i k", i=TILES) for h in HALVES]
                for h in HALVES:
                    dve.wait_ge(S_[("d_r1", "d_r2")[r]], h + 1)
                    own.link(V.tensor_reduce(small[:, h, 0:TILES], zr[h][:, :, MER:MER + ME], AX_X, ALU.max))
                    V.tensor_tensor(logit[:, h], zr[h][:, :, MER:MER + ME], spread(small[:, h, 0:TILES], ME), ALU.subtract
                                    ).then_inc(S_["d_z"], 1)
                    dve.wait_ge(S_["d_e"], 2 * r + h + 1)
                    own.link(V.tensor_reduce(small[:, h, 4:4 + TILES], logit[:, h], AX_X, ALU.add))
                    own.link(V.reciprocal(small[:, h, 8:8 + TILES], small[:, h, 4:4 + TILES]))
                    own.link(V.scalar_tensor_tensor(logit[:, h], logit[:, h], 1.0 / MR,
                                                    spread(small[:, h, 8:8 + TILES], ME), ALU.mult, ALU.mult))
                    if r == 1:
                        dve.wait_ge(S_["d_zt"], h + 1)
                    V.tensor_tensor(zg[:, h, :, 0:MER].rearrange("p i (e r) -> p i e r", e=ME),
                                    zr[h][:, :, 0:MER].rearrange("p i (e r) -> p i e r", e=ME),
                                    spread(logit[:, h], MR), ALU.mult).then_inc(S_["d_z"], 1)

            dve.wait_ge(S_["k_mem"], 8)
            mixture(0)
            dve.wait_ge(S_["ld_gv"], 16)
            own.link(V.tensor_reduce(gred[:, 0:1], gvec[:, 0, :], AX_X, ALU.max))
            V.tensor_scalar(gvec[:, 1, :], gvec[:, 0, :], gred[:, 0:1], None, ALU.subtract).then_inc(S_["p_gw"], 1)
            dve.wait_ge(S_["p_gw"], 2)
            own.link(V.reciprocal(gred[:, 2:3], gred[:, 1:2]))
            own.link(V.scalar_tensor_tensor(gvec[:, 2, :], gvec[:, 1, :], gred[:, 2:3], kc[0:TYPES, K_BAND:K_BAND + L1E],
                                            ALU.mult, ALU.mult))
            V.tensor_copy(gwide[:, :, :], spread(gvec[:, 2, :], P)).then_inc(S_["p_gw"], 1)

            mixture(1)
            for h in HALVES:
                dve.wait_ge(S_["d_out"], h + 1)
                residual(h, ps[h][:, 1, :], xt[1], xt[0], "d_res")

            def x_rest(k, copied, bank):
                for h in HALVES:
                    dve.wait_ge(S_[copied], h + 1)
                    V.tensor_tensor(x_part(h, 1), ps[h][:, bank, :], x_part(h, 0), ALU.subtract).then_inc(S_[k + "_xl"], 1)

            x_rest("e", "d_xf", 3)
            def experts(k, n_ffns, shares, coef):
                def weigh(e):
                    for h in HALVES:
                        total, g = z(h, shares), shares + e
                        product = total if e == 0 else yt[:, h].rearrange("p i d -> p (i d)")
                        dve.wait_ge(S_[k + "_acc"], 2 * g + h + 1)
                        V.tensor_tensor(by_batch(product), by_batch(ps[h][:, 2 + g % 2, :]),
                                        spread(coef[:, e, h * HB:(h + 1) * HB], S), ALU.mult).then_inc(S_[k + "_accd"], 1)
                        if e > 0:
                            dve.wait_ge(S_[k + "_accd"], 2 * e + h + 1)
                            ins = V.tensor_tensor(total, total, product, ALU.add)
                            if g == n_ffns - 1:
                                ins.then_inc(S_[k + "_sum"], 1)
                            else:
                                own.step(ins)
                    own.sync()

                for n, (f, c) in enumerate(ffn_items(n_ffns)):
                    for h in HALVES:
                        dve.wait_ge(S_[k + "_hi"], 2 * n + h + 1)
                        V.scalar_tensor_tensor(hidden_part(h, n, 1), ps[h][:, n % 2, :], 0.0, hidden_part(h, n, 0),
                                               ALU.max, ALU.subtract).then_inc(S_[k + "_lo"], 1)
                    if c == 0 and f > shares:
                        weigh(f - 1 - shares)
                weigh(n_ffns - 1 - shares)
                m = shares + 1
                for h in HALVES:
                    dve.wait_ge(S_[k + "_g2"], 2 * h + 1)
                    V.tensor_reduce(gsm[:, h, 8:9], ps[h][0:HB, 1, 0:m], AX_X, ALU.max, negate=True
                                    ).then_inc(S_[k + "_g2"], 1)
                for h in HALVES:
                    dve.wait_ge(S_[k + "_ge"], h + 1)
                    own.link(V.reciprocal(gsm[:, h, 10:11], gsm[:, h, 9:10]))
                    own.link(V.tensor_scalar(gsm[:, h, 0:m], gsm[:, h, 4:4 + m], gsm[:, h, 10:11], None, ALU.mult))
                    V.tensor_copy(gwb[:, h, 0:m, :], spread(gsm[:, h, 0:m], P)).then_inc(S_[k + "_gw"], 1)
                for h in HALVES:
                    dve.wait_ge(S_[k + "_gbc"], h + 1)
                    for j in range(m):
                        g = shares if j == 0 else j - 1
                        own.step(V.tensor_tensor(by_batch(z(h, g)), by_batch(z(h, g)), spread(gcol[:, h, j, :], S), ALU.mult))
                    own.sync()
                    for j in range(1, m - 1):
                        own.link(V.tensor_tensor(z(h, 0), z(h, 0), z(h, j), ALU.add))
                    V.tensor_tensor(cf[:, h], z(h, 0), z(h, m - 1), ALU.add).then_inc(S_[k + "_out"], 1)

            dve.wait_ge(S_["p_coefc"], 1)
            experts("e", NE1, L1S, type_coef)

            def col(r, s):
                return vl[s][:, r:r + 1]

            def keys(l, h, s):
                ksum, kv = small[:, h, 0:HB], small[:, h, HB:2 * HB]
                dve.wait_ge(S_["f_exp"], l * 4 + (2 * h + 1))
                own.link(V.tensor_scalar(z(h, 6), z(h, 6), 1.0, 1.0, ALU.min, ALU.subtract))
                k_done = own.mark(V.scalar_tensor_tensor(z(h, 8), ps[h][:, 2, :], col(V_BK, s), z(h, 6), ALU.add, ALU.max))
                dve.wait_ge(S_["f_exp"], l * 4 + (2 * h + 2))
                q_less = own.mark(V.tensor_scalar(z(h, 4), z(h, 4), 1.0, 1.0, ALU.min, ALU.subtract))
                own.after(k_done)
                sums = own.mark(V.tensor_reduce(small2[:, h, 0:HB], by_batch(z(h, 8)), AX_X, ALU.add))
                own.after(q_less)
                own.step(V.scalar_tensor_tensor(z(h, 11), ps[h][:, 0, :], col(V_BQ, s), z(h, 4), ALU.add, ALU.max))
                own.after(sums)
                own.link(V.tensor_scalar(ksum, small2[:, h, 0:HB], float(S), None, ALU.add))
                V.scalar_tensor_tensor(by_batch(z(h, 10)), by_batch(z(h, 11)), 1.0, spread(ksum, S), ALU.add, ALU.mult
                                       ).then_inc(S_["f_den"], 1)
                dve.wait_ge(S_["f_vb"], l * 2 + (h + 1))
                products = own.mark(V.scalar_tensor_tensor(z(h, 9), z(h, 8), 1.0, z(h, 7), ALU.add, ALU.mult))
                own.step(V.reciprocal(small2[:, h, HB:2 * HB], ksum))
                own.after(products)
                own.link(V.tensor_reduce(kv, by_batch(z(h, 9)), AX_X, ALU.add))
                own.link(V.scalar_tensor_tensor(small2[:, h, 2 * HB:3 * HB], small2[:, h, HB:2 * HB], -1.0, kv,
                                                ALU.mult, ALU.mult))

            def values(l, h):
                dve.wait_ge(S_["f_ratio"], l * 2 + (h + 1))
                V.scalar_tensor_tensor(by_batch(z(h, 12)), by_batch(z(h, 10)), 1.0, spread(small2[:, h, 2 * HB:3 * HB], S),
                                       ALU.subtract, ALU.mult).then_inc(S_["f_u"], 1)

            def affine(l, h, s):
                dve.wait_ge(S_["f_tr"], norm_count(l, h, 1))
                V.tensor_scalar(cf[:, h], ps[h][:, 1, :], col(V_S2, s), col(V_B2, s), ALU.mult, ALU.add
                                ).then_inc(S_["f_y"], 1)

            def norm_sum(l, h, n):
                dve.wait_ge(S_["f_ft"], back_count(l, h, n))
                dve.wait_ge(S_[("f_og", "f_w2g")[n]], l * 2 + (h + 1))
                add_residual(h, ps[h][:, 3, :], z(h, 4 + n))

            def norm_scale(l, h, n):
                normalise(norm_count(l, h, n) + 2, h)

            def segment(l, a, sa, m, b, sb_):
                keys(l, a, sa)
                values(l, a)
                norm_sum(l, a, 0)
                stats(a, EPS_LN)
                if m is not None:
                    norm_sum(m, b, 1)
                norm_scale(l, a, 0)
                if m is not None:
                    stats(b, EPS_LN)
                    norm_scale(m, b, 1)
                    affine(m, b, sb_)

            def layer(l, s):
                segment(l, 1, s, l, 0, s)
                segment(l + 1, 0, 1 - s, l, 1, s)

            segment(0, 0, 0, None, None, None)
            lead = own.n
            layer(0, 0)
            per = own.n - lead
            with dve.Fori(0, LAYERS // 2 - 1) as it:
                own.base, own.n = it * (2 * per) + (lead + per), 0
                layer(it * 2 + 1, 1)
                layer(it * 2 + 2, 0)
                assert own.n == 2 * per, (own.n, per)
            own.base, own.n = None, lead + (LAYERS - 1) * per
            last = LAYERS - 1
            segment(last, 1, 1, last, 0, 1)
            norm_sum(last, 1, 1)
            stats(1, EPS_LN)
            norm_scale(last, 1, 1)
            affine(last, 1, 1)

            for h in HALVES:
                dve.wait_ge(S_["f_ft"], norm_count(last, h, 1) + 2)
                residual(h, ps[h][:, 3, :], xt[0], xt[1], "g_res")

            x_rest("g", "g_xf", 2)
            experts("g", L2S + TYPES, L2S, type_mask)

            own.step(V.memset(sel[:, :, :, :, :], 0.0))
            for h in HALVES:
                dve.wait_ge(S_["h_sc"], h + 1)
                sc = ps[h][:, 0, 0:TILES * 64].rearrange("p (i k) -> p i k", i=TILES)[:, :, 0:TREES * LEAVES]
                d = dec[:, h]
                own.link(V.tensor_scalar(d.rearrange("p (i t) k -> p i (t k)", i=TILES), sc, 0.0, None, ALU.is_ge))
                r = reach[:, h]
                own.step(V.tensor_copy(r[:, :, 1], d[:, :, 0]))
                own.link(V.tensor_scalar(r[:, :, 0], d[:, :, 0], -1.0, 1.0, ALU.mult, ALU.add))
                at, new, first = 0, 2, 1
                while first < NODES:
                    k = first + 1
                    src = r[:, :, at:at + k]
                    if 2 * k == LEAVES:
                        dst = sel[:, h].rearrange("p i t k -> p (i t) k")[:, :, 0:LEAVES]
                    else:
                        dst = r[:, :, new:new + 2 * k]
                    pair = dst.rearrange("p n (k two) -> p n k two", two=2)
                    own.link(V.tensor_tensor(pair[:, :, :, 1], src, d[:, :, first:first + k], ALU.mult))
                    ins = V.tensor_tensor(pair[:, :, :, 0], src, pair[:, :, :, 1], ALU.subtract)
                    if 2 * k == LEAVES:
                        ins.then_inc(S_["h_sel"], 1)
                    else:
                        own.link(ins)
                    at, new, first = new, new + 2 * k, first + k
            for h in HALVES:
                dve.wait_ge(S_["h_stc"], h + 1)
                V.tensor_copy(selb[:, h], selt[:, h]).then_inc(S_["h_stb"], 1)
            for n in range(TREES * LFC):
                t, c = divmod(n, LFC)
                for h in HALVES:
                    dve.wait_ge(S_["h_lbc"], 2 * t + h + 1)
                    dve.wait_ge(S_["h_relu"], 2 * n + h + 1)
                    V.scalar_tensor_tensor(z(h, 8 + n % 3), z(h, 12 + t), kc[:, K_LEAF + c:K_LEAF + c + 1], z(h, 4 + n % 3),
                                           ALU.is_equal, ALU.mult).then_inc(S_["h_mask"], 1)
            for h in HALVES:
                own.step(V.memset(z(h, 12), 0.0))
            for h in HALVES:
                dve.wait_ge(S_["h_s"], h + 1)
                sc = grouped(ps[h][:, 0, 0:TILES * S])
                own.link(V.tensor_reduce(small[:, h, 0:TILES], sc, AX_X, ALU.max))
                V.tensor_tensor(grouped(z(h, 3)[:, 0:TILES * S]), sc, spread(small[:, h, 0:TILES], S), ALU.subtract
                                ).then_inc(S_["h_sub"], 1)
            for h in HALVES:
                dve.wait_ge(S_["h_exp"], h + 1)
                e = grouped(z(h, 3)[:, 0:TILES * S])
                own.link(V.tensor_reduce(small[:, h, 4:4 + TILES], e, AX_X, ALU.add))
                own.link(V.reciprocal(small[:, h, 8:8 + TILES], small[:, h, 4:4 + TILES]))
                own.link(V.tensor_tensor(e, e, spread(small[:, h, 8:8 + TILES], S), ALU.mult))
                for q in range(P // QUAD):
                    rows_q = slice(q * QUAD, (q + 1) * QUAD)
                    pt = z(h, 12).rearrange("p (i n) -> p i n", i=TILES)
                    ins = V.transpose(pt[rows_q, :, rows_q], e[rows_q])
                    if q < P // QUAD - 1:
                        own.step(ins)
                ins.then_inc(S_["h_pt"], 1)
            for h in HALVES:
                dve.wait_ge(S_["h_o"], h + 1)
                residual(h, ps[h][:, 1, :], xt[1], yt, "h_fin")

        @block.tensor
        def _(pe):
            T = nc.tensor

            def turn(dst, srcs, sem, n=P, m=P):
                for i, s in enumerate(srcs):
                    ins = T.transpose(dst[:, i * P:(i + 1) * P], s, ident)
                ins.then_inc(S_[sem], 1)

            def keep_warm(n, bank):
                for _ in range(n):
                    T.matmul(bank, filler[:, :].to_broadcast([P, P]), filler[:, :].to_broadcast([P, HT]), start=True, stop=True)

            pe.wait_ge(S_["k_mem"], 1)
            keep_warm(16, ps[0][:, 1, :])
            pe.wait_ge(S_["ld_const"], 16)
            pe.wait_ge(S_["ld_x"], 16)
            for h in HALVES:
                turn(ps[h][:, 3, :], [xt[0][:, h, i, :] for i in range(TILES)], "x_tr")
            pe.wait_ge(S_["ld_rows0"], 16 * 5)
            T.transpose(ps[0][:, 0, 0:R_END0], rows0[:, :], ident[0:R_END0, 0:R_END0]).then_inc(S_["p_cols0"], 1)
            pe.wait_ge(S_["p_cols0c"], 1)

            pe.wait_ge(S_["ld_a1"], 16)
            for c in range(LCH):
                m = min(P, LANGS * ADIM - c * P)
                for h in HALVES:
                    if c == 0:
                        pe.wait_ge(S_["x_f"], h + 1)
                    T.matmul(ps[h][0:m, c, :], w1a[:, c * P:c * P + m], xf[:, h], start=True, stop=True
                             ).then_inc(S_["a_hid"], 1)

            pe.wait_ge(S_["a_relu"], 2)
            pe.wait_ge(S_["ld_b"], 16 * 5)
            for n, turned in enumerate((rope_q, rope_k, ident, ident)):
                ins = T.matmul(ps[1][:, 0, n * D:(n + 1) * D], w_nat[:, n, :], turned, start=True, stop=True)
            ins.then_inc(S_["p_watt"], 1)
            pe.wait_ge(S_["a_relu"], 3)
            T.matmul(ps[0][:, 1, 0:1], rope_q, cols0[:, R_L0Q:R_L0Q + 1], start=True, stop=True)
            T.matmul(ps[0][:, 1, 1:2], rope_k, cols0[:, R_L0K:R_L0K + 1], start=True, stop=True).then_inc(S_["p_rope"], 1)
            pe.wait_ge(S_["p_hot"], 3)
            pe.wait_ge(S_["ld_a"], 16 * 5)
            pe.wait_ge(S_["ld_c"], 16)
            pe.wait_ge(S_["a_relu"], 5)
            T.matmul(ps[0][:, 2, 0:B], lang_rows[:, 1, :], lang_hot[0:LANGS, :], start=True, stop=True)
            T.matmul(ps[0][:, 2, B:2 * B], lang_rows[:, 2, :], lang_hot[0:LANGS, :], start=True, stop=True)
            T.matmul(ps[0][:, 2, 2 * B:3 * B], cat_bias[:, :], cat_hot[0:CATS, :], start=True, stop=True
                     ).then_inc(S_["p_bat"], 1)
            for h in HALVES:
                pe.wait_ge(S_["a_mask"], 2 * (LCH - 1) + h + 1)
                for i in range(TILES):
                    dst = ps[h][:, 3, tok(h, i)]
                    for c in range(LCH):
                        m = min(P, LANGS * ADIM - c * P)
                        T.matmul(dst, z(h, c)[0:m, tok(h, i)], w2a[0:m, c, :], start=(c == 0), stop=False)
                    b0 = h * HB + i * (P // S)
                    ins = T.matmul(dst, lang_tok[0:LANGS, b0:b0 + P // S, :].rearrange("p b s -> p (b s)"),
                                   lang_rows[:, 0, :], start=False, stop=True)
                ins.then_inc(S_["a_out"], 1)
            pe.wait_ge(S_["ld_rows"], 16 * (LV + TREES))
            turn(ps[1][:, 1, :], [rows[:, :]], "p_cols")
            pe.wait_ge(S_["p_colsc"], 1)
            keep_warm(22, ps[0][:, 1, :])
            for h in HALVES:
                pe.wait_ge(S_["xn"], h + 1)
                turn(ps[h][:, 0, :], [xn[:, h, i, :] for i in range(TILES)], "a_tr")

            for h in HALVES:
                pe.wait_ge(S_["a_cond"], h + 1)
                T.matmul(ps[h][:, 1, :], w_att[:, 1, :], cf[:, h], start=True, stop=True)
                T.matmul(ps[h][:, 0, :], w_att[:, 0, :], cf[:, h], start=True, stop=True).then_inc(S_["b_qk"], 1)

            def batch(ap, b):
                return ap[:, b * S:(b + 1) * S]

            def scores(n):
                h, g = n % 2, n // 2
                pe.wait_ge(S_["b_rep"], n + 1)
                if n >= 2:
                    pe.wait_ge(S_["b_vx"], n - 1)
                for b in range(GB):
                    ins = T.matmul(ps[h][:, 2, b * D:(b + 1) * D], z(h, g % 3)[:, b * P:(b + 1) * P], w_att[:, 2, :],
                                   start=True, stop=True)
                ins.then_inc(S_["b_vr"], 1)
                if g == 0:
                    pe.wait_ge(S_["b_k"], h + 1)
                    pe.wait_ge(S_["b_qe"], h + 1)
                if n >= 4:
                    pe.wait_ge(S_["b_sub"], n - 3)
                for b in range(GB):
                    r = slice(b * P, (b + 1) * P)
                    ins = T.matmul(ps[h][:, (3, 0)[g % 2], r], z(h, 8 + g)[:, r], z(h, 4 + g)[:, r], start=True, stop=True)
                ins.then_inc(S_["b_sc"], 1)

            def context(n):
                h, g = n % 2, n // 2
                pe.wait_ge(S_["b_pt"], n + 1)
                pe.wait_ge(S_["b_vx"], n + 1)
                for b in range(GB):
                    for q in range(HG):
                        r = slice(q * QUAD, (q + 1) * QUAD)
                        at = (b * HG + q) * S
                        col = (g * GB + b) * S
                        ins = T.matmul(ps[h][r, 1, col:col + S], z(h, 12 + g)[:, b * D + q * QUAD:b * D + (q + 1) * QUAD],
                                       z(h, 8 + g)[:, at:at + S], start=True, stop=True, tile_position=(0, q * QUAD))
                if g == NG - 1:
                    ins.then_inc(S_["b_ctx"], 1)

            for n in range(2 * NG + 2):
                if n < 2 * NG:
                    scores(n)
                if n >= 2:
                    if n >= 2 * NG:
                        keep_warm(8, ps[0][:, 0, :])
                    context(n - 2)
            for h in HALVES:
                pe.wait_ge(S_["b_ctxc"], h + 1)
                for i in range(TILES):
                    dst = ps[h][:, 2, tok(h, i)]
                    T.matmul(dst, z(h, 0)[:, tok(h, i)], w_att[:, 3, :], start=True, stop=False)
                    ins = T.matmul(dst, ones[:, :], token_bias[:, :], start=False, stop=True)
                ins.then_inc(S_["b_out"], 1)
            for h in HALVES:
                pe.wait_ge(S_["b_res"], h + 1)
                turn(ps[h][:, 3, :], [xt[1][:, h, i, :] for i in range(TILES)], "b_tr")

            keep_warm(22, ps[0][:, 1, :])
            pe.wait_ge(S_["ld_cat"], 16 * B)
            for h in HALVES:
                pe.wait_ge(S_["b_xf"], h + 1)
                for b in range(HB):
                    ins = T.matmul(batch(ps[h][:, 0, :], b), w_cat[:, h * HB + b, :], batch(xf[:, h], b),
                                   start=True, stop=True)
                ins.then_inc(S_["c_mm"], 1)

            pe.wait_ge(S_["ld_d"], 16 * (2 * ME + 8))
            for h in HALVES:
                pe.wait_ge(S_["c_out"], h + 1)
                for i in range(TILES):
                    ins = T.matmul(ps[h][:, 1, i * P:i * P + MER + ME], cf[:, h][:, tok(h, i)], ar1[:, :], start=True, stop=True)
                ins.then_inc(S_["d_r1"], 1)

            def turn_parts(r):
                keep_warm(4, ps[0][:, 2, :])
                for h in HALVES:
                    pe.wait_ge(S_["d_z"], 2 * (2 * r + h) + 2)
                    turn(ps[h][0:QUAD, 3, :], [zg[:, h, i, :] for i in range(TILES)], "d_zt")

            turn_parts(0)
            for c in range(FC):
                for h in HALVES:
                    if c == 0:
                        pe.wait_ge(S_["d_ztc"], h + 1)
                    if c >= 3:
                        pe.wait_ge(S_["d_relu"], 2 * (c - 3) + h + 1)
                    dst = ps[h][:, c % 3, :]
                    T.matmul(dst, w1f[:, c * P:(c + 1) * P], cf[:, h], start=True, stop=False)
                    T.matmul(dst, b1aug[:, c * P:(c + 1) * P], zgt[0:MER + 1, h], start=False, stop=True
                             ).then_inc(S_["d_hid"], 1)
            for h in HALVES:
                pe.wait_ge(S_["d_relu"], 2 * (FC - 1) + h + 1)
                for i in range(TILES):
                    for c in range(FC):
                        ins = T.matmul(ps[h][:, 0, i * P:i * P + MER + ME], z(h, c)[:, tok(h, i)], ar2[:, c, :],
                                       start=(c == 0), stop=(c == FC - 1))
                ins.then_inc(S_["d_r2"], 1)
            turn_parts(1)
            for h in HALVES:
                pe.wait_ge(S_["d_ztc"], 2 + h + 1)
                for i in range(TILES):
                    dst = ps[h][:, 1, tok(h, i)]
                    for c in range(FC):
                        T.matmul(dst, z(h, c)[:, tok(h, i)], w2f[:, c, :], start=(c == 0), stop=False)
                    ins = T.matmul(dst, zgt[0:MER + 1, h, tok(h, i)], b2aug[:, :], start=False, stop=True)
                ins.then_inc(S_["d_out"], 1)
            pe.wait_ge(S_["p_gw"], 3)
            for e in range(L1E):
                ins = T.matmul(ps[0][:, 2, e * B:(e + 1) * B], gwide[:, e, :], type_hot[0:TYPES, :], start=True, stop=True)
            ins.then_inc(S_["p_coef"], 1)
            for h in HALVES:
                pe.wait_ge(S_["d_res"], h + 1)
                turn(ps[h][:, 3, :], [xt[0][:, h, i, :] for i in range(TILES)], "d_tr")

            def experts(k, n_ffns, shares, g1, g2):
                items = ffn_items(n_ffns)

                def hidden(n):
                    f, c = items[n]
                    if c == 0:
                        pe.wait_ge(S_[k + "_w"], f + 1)
                    for h in HALVES:
                        if n == 0:
                            pe.wait_ge(S_[k + "_xl"], h + 1)
                        if n >= 2:
                            pe.wait_ge(S_[k + "_lo"], 2 * (n - 2) + h + 1)
                        for m, (a, b) in enumerate(CROSS):
                            ins = T.matmul(ps[h][:, n % 2, :], w_part(f, a)[:, c * P:(c + 1) * P], x_part(h, b),
                                           start=(m == 0), stop=(m == 2))
                        ins.then_inc(S_[k + "_hid"], 1)

                def output(n):
                    f, c = items[n]
                    for h in HALVES:
                        pe.wait_ge(S_[k + "_lo"], 2 * n + h + 1)
                        if c == 0 and f >= 2:
                            if f - 2 < shares:
                                pe.wait_ge(S_[k + "_accc"], 2 * (f - 2) + h + 1)
                            else:
                                pe.wait_ge(S_[k + "_accd"], 2 * (f - 2 - shares) + h + 1)
                        for m, (a, b) in enumerate(CROSS):
                            ins = T.matmul(ps[h][:, 2 + f % 2, :], w_part(f, a)[:, FF + c * P:FF + (c + 1) * P],
                                           hidden_part(h, n, b), start=(c == 0 and m == 0), stop=(c == FC - 1 and m == 2))
                        if c == FC - 1:
                            ins.then_inc(S_[k + "_acc"], 1)

                for n in range(len(items) + 1):
                    if n < len(items):
                        hidden(n)
                    if n >= 1:
                        output(n - 1)
                for h in HALVES:
                    pe.wait_ge(S_[k + "_accc"], 2 * (shares - 1) + h + 1)
                    pe.wait_ge(S_[k + "_sum"], h + 1)
                    for j in range(shares + 1):
                        g = shares if j == 0 else j - 1
                        ins = T.matmul(ps[h][:, 0, 0:HB], g1[:, j, :], by_batch(z(h, g))[:, :, 0],
                                       start=(j == 0), stop=(j == shares))
                    ins.then_inc(S_[k + "_g1"], 1)
                for h in HALVES:
                    pe.wait_ge(S_[k + "_g1c"], h + 1)
                    if h == 1:
                        pe.wait_ge(S_[k + "_g2"], 2)
                    T.matmul(ps[h][0:HB, 1, 0:shares + 1], grel[:, h], g2[:, :], start=True, stop=True
                             ).then_inc(S_[k + "_g2"], 1)
                keep_warm(6, ps[0][:, 3, :])
                for h in HALVES:
                    pe.wait_ge(S_[k + "_gw"], h + 1)
                    for j in range(shares + 1):
                        ins = T.matmul(ps[h][:, 2, j * HB:(j + 1) * HB], gwb[:, h, j, :], ident[0:HB, 0:HB],
                                       start=True, stop=True)
                    ins.then_inc(S_[k + "_gb"], 1)

            pe.wait_ge(S_["ld_e"], 16 * (4 + L1S + L1E))
            pe.wait_ge(S_["p_coefc"], 1)
            experts("e", NE1, L1S, gate1, gate2)

            for h in HALVES:
                keep_warm(12, ps[0][:, 1, :])
                pe.wait_ge(S_["e_out"], h + 1)
                turn(ps[h][:, 3, :], [cf[:, h][:, tok(h, i)] for i in range(TILES)], "f_ft")

            def project(l, h, s, n):
                T.matmul(ps[h][:, (0, 2, 1)[n], :], wl[s][:, n * D:(n + 1) * D], cf[:, h], start=True, stop=True
                         ).then_inc(S_[("f_q", "f_k", "f_v")[n]], 1)

            def bias_rows(h, bank, n, s):
                T.matmul(ps[h][:, bank, :], ones3[:, :], rl[s][:, n:n + 1, :].to_broadcast([3, TILES, D]),
                         start=True, stop=False)

            def attn_out(l, h, s):
                pe.wait_ge(S_["f_den"], l * 2 + (h + 1))
                bias_rows(h, 0, 0, s)
                pe.wait_ge(S_["f_u"], l * 2 + (h + 1))
                for i in range(TILES):
                    ins = T.matmul(ps[h][:, 0, tok(h, i)], z(h, 12)[:, tok(h, i)], wl[s][:, 3 * D:4 * D], start=False,
                                   stop=(i == TILES - 1))
                ins.then_inc(S_["f_o"], 1)

            def turns(l, h, n):
                pe.wait_ge(S_["xn"], norm_count(l, h, n) + 2)
                turn(ps[h][:, 1, :], [xn[:, h, i, :] for i in range(TILES)], "f_tr")

            def scaled(l, h, n):
                pe.wait_ge(S_[("f_x", "f_y")[n]], l * 2 + (h + 1))

            def turns_back(l, h, n):
                scaled(l, h, n)
                turn(ps[h][:, 3, :], [cf[:, h][:, tok(h, i)] for i in range(TILES)], "f_ft")

            def ffn_in(l, h, s, chunks):
                for c in chunks:
                    if c == 3:
                        pe.wait_ge(S_["f_h"], l * (2 * FC) + (h * FC + 1))
                    T.matmul(ps[h][:, FFN_BANK[c], :], wl[s][:, 4 * D + c * P:4 * D + (c + 1) * P], cf[:, h],
                             start=True, stop=True).then_inc(S_["f_w1"], 1)

            def ffn_out(l, h, s, chunks):
                if 0 in chunks:
                    pe.wait_ge(S_["f_h"], l * (2 * FC) + (h * FC + 2))
                    bias_rows(h, 2, 1, s)
                for c in chunks:
                    if c >= 2:
                        pe.wait_ge(S_["f_h"], l * (2 * FC) + (h * FC + c + 1))
                    for i in range(TILES):
                        ins = T.matmul(ps[h][:, 2, tok(h, i)], z(h, c)[:, tok(h, i)],
                                       wl[s][:, 4 * D + FF + c * D:4 * D + FF + (c + 1) * D], start=False,
                                       stop=(c == FC - 1 and i == TILES - 1))
                if FC - 1 in chunks:
                    ins.then_inc(S_["f_w2"], 1)

            def arrived(s, k):
                pe.wait_ge(S_[f"ld_f{s}"], k)

            def segment(l, a, sa, m, b, sb_):
                if m is not None:
                    turns(m, b, 0)
                    keep_warm(2, ps[b][:, 0, :])
                    scaled(m, b, 0)
                    ffn_in(m, b, sb_, (0, 1))
                if l is not None:
                    if not (isinstance(l, int) and l == 0):
                        turns(l - 1, a, 1)
                        keep_warm(2, ps[a][:, 0, :])
                        scaled(l - 1, a, 1)
                    project(l, a, sa, 1)
                    project(l, a, sa, 0)
                    project(l, a, sa, 2)
                if m is not None:
                    ffn_in(m, b, sb_, (2, 3))
                    turns_back(m, b, 0)
                if l is not None:
                    if not (isinstance(l, int) and l == 0):
                        turns_back(l - 1, a, 1)
                if m is not None:
                    ffn_out(m, b, sb_, (0, 1))
                if l is not None:
                    attn_out(l, a, sa)
                if m is not None:
                    ffn_out(m, b, sb_, (2, 3))
                    keep_warm(12, ps[b][:, 0, :])

            def layer(l, s, next_loaded):
                segment(l, 1, s, l, 0, s)
                arrived(1 - s, next_loaded)
                segment(l + 1, 0, 1 - s, l, 1, s)

            loaded = 16 * 9
            arrived(0, loaded)
            segment(0, 0, 0, None, None, None)
            layer(0, 0, loaded)
            with pe.Fori(0, LAYERS // 2 - 1) as it:
                layer(it * 2 + 1, 1, it * loaded + 2 * loaded)
                layer(it * 2 + 2, 0, it * loaded + 2 * loaded)
            last = LAYERS - 1
            segment(last, 1, 1, last, 0, 1)
            turns(last, 1, 0)
            scaled(last, 1, 0)
            ffn_in(last, 1, 1, (0, 1))
            turns(last, 0, 1)
            ffn_in(last, 1, 1, (2, 3))
            turns_back(last, 1, 0)
            turns_back(last, 0, 1)
            ffn_out(last, 1, 1, (0, 1, 2, 3))
            turns(last, 1, 1)
            turns_back(last, 1, 1)

            for h in HALVES:
                pe.wait_ge(S_["g_res"], h + 1)
                turn(ps[h][:, 2, :], [xt[1][:, h, i, :] for i in range(TILES)], "g_tr")

            pe.wait_ge(S_["ld_g"], 16 * (4 + L2S + TYPES))
            experts("g", L2S + TYPES, L2S, gate1b, gate2b)

            pe.wait_ge(S_["ld_h"], 16 * 15)
            pe.wait_ge(S_["g_gbc"], 2)
            T.transpose(ps[1][:, 1, 0:TREES * LEAVES], node_rows[:, :], ident[0:TREES * LEAVES, 0:TREES * LEAVES]
                        ).then_inc(S_["p_node"], 1)
            pe.wait_ge(S_["p_nodec"], 1)
            keep_warm(8, ps[0][:, 1, :])
            for h in HALVES:
                pe.wait_ge(S_["g_out"], h + 1)
                for i in range(TILES):
                    dst = ps[h][:, 0, i * 64:i * 64 + TREES * LEAVES]
                    T.matmul(dst, cf[:, h][:, tok(h, i)], node_t[:, :], start=True, stop=False)
                    ins = T.matmul(dst, ones[:, :], node_bias[:, :], start=False, stop=True)
                ins.then_inc(S_["h_sc"], 1)
            keep_warm(16, ps[0][:, 1, :])
            for h in HALVES:
                pe.wait_ge(S_["h_sel"], h + 1)
                turn(ps[h][0:TREES * QUAD, 3, :],
                     [sel[:, h, i].rearrange("p t k -> p (t k)") for i in range(TILES)], "h_st")
            for t in range(TREES):
                r = slice(t * QUAD, t * QUAD + LEAVES)
                for h in HALVES:
                    pe.wait_ge(S_["h_stb"], h + 1)
                    T.matmul(ps[h][:, t, :], leaf_val[r, :], selb[r, h], start=True, stop=True).then_inc(S_["h_lb"], 1)

            def leaf_hidden(n):
                t, c = divmod(n, LFC)
                if c == 0:
                    pe.wait_ge(S_["h_w"], t + 1)
                for h in HALVES:
                    if n < 2:
                        pe.wait_ge(S_["h_lbc"], 2 * TREES - 1 + h)
                    else:
                        pe.wait_ge(S_["h_relu"], 2 * (n - 2) + h + 1)
                    if n == 0:
                        pe.wait_ge(S_["h_xl"], h + 1)
                    for m, (a, b) in enumerate(CROSS):
                        ins = T.matmul(ps[h][:, n % 2, :], tree_part(t, a)[:, c * P:(c + 1) * P], (xn_r, xf_r)[b][:, h],
                                       start=(m == 0), stop=(m == 2))
                    ins.then_inc(S_["h_hid"], 1)

            def leaf_output(n):
                t, c = divmod(n, LFC)
                r = slice(t * QUAD, t * QUAD + LEAVES)
                for h in HALVES:
                    bank = ps[h][:, 2 + t % 2, :]
                    if c == 0:
                        pe.wait_ge(S_["h_stc"], h + 1)
                        if t == 2:
                            pe.wait_ge(S_["h_accc"], h + 1)
                    pe.wait_ge(S_["h_mask"], 2 * n + h + 1)
                    hm = z(h, 8 + n % 3)
                    if t < 2:
                        ins = T.matmul(bank, w_tree(t)[:, 1, c, :], hm, start=(c == 0), stop=False)
                        if c == LFC - 1:
                            ins = T.matmul(bank, leaf_b2[r, :], selt[r, h], start=False, stop=True)
                    else:
                        for i in range(TILES):
                            ins = T.matmul(bank[:, tok(h, i)], hm[:, tok(h, i)], w_tree(t)[:, 1, c, :],
                                           start=(c == 0 and i == 0), stop=False, skip_group_check=True)
                        if c == LFC - 1:
                            for i in range(TILES):
                                ins = T.matmul(bank[:, tok(h, i)], selt[r, h, tok(h, i)], leaf_b2[r, :],
                                               start=False, stop=(i == TILES - 1), skip_group_check=True)
                    if c == LFC - 1:
                        ins.then_inc(S_["h_acc"], 1)

            for n in range(TREES * LFC + 1):
                if n < TREES * LFC:
                    leaf_hidden(n)
                if n >= 1:
                    leaf_output(n - 1)
            for h in HALVES:
                pe.wait_ge(S_["h_accc"], 2 + h + 1)
                for b in range(HB):
                    i, q = divmod(b, P // S)
                    r = slice(q * QUAD, (q + 1) * QUAD)
                    ins = T.matmul(ps[h][r, 0, i * S:(i + 1) * S], batch(z(h, 0), b), batch(z(h, 1), b),
                                   start=True, stop=True, tile_position=(0, q * QUAD))
                ins.then_inc(S_["h_s"], 1)
            for h in HALVES:
                pe.wait_ge(S_["h_pt"], h + 1)
                pe.wait_ge(S_["h_accc"], 4 + h + 1)
                for i in range(TILES):
                    ins = T.matmul(ps[h][:, 1, tok(h, i)], z(h, 12)[:, tok(h, i)], z(h, 2)[:, tok(h, i)],
                                   start=True, stop=True)
                ins.then_inc(S_["h_o"], 1)


def kernel(**inputs):
    import concourse.bacc as _bacc
    from concourse.bass_utils import run_bass_kernel_spmd as _run

    nc = _bacc.Bacc("TRN2", target_bir_lowering=False, num_devices=1)
    arrays, aps = {}, {}
    for name, value in inputs.items():
        a = np.ascontiguousarray(value)
        arrays[f"in_{name}"] = a
        aps[name] = nc.dram_tensor(f"in_{name}", a.shape, mybir.dt.from_np(a.dtype), kind="ExternalInput").ap()
    k = shape_constants()
    arrays["shape_constants"] = k
    konst = nc.dram_tensor("shape_constants", k.shape, F32, kind="ExternalInput").ap()
    out = nc.dram_tensor("out", (B, S, D), F32, kind="ExternalOutput").ap()
    network(nc, aps, konst, out)
    r = _run(nc, [arrays], core_ids=[0])
    return r.results[0]["out"]
```
